# Optimizing a Trainium2 kernel written in Bass

```python
import numpy as np
import jax
import jax.numpy as jnp

def _softmax(x, axis=-1):
    return jax.nn.softmax(x, axis=axis)

def _gelu(x):
    return jax.nn.gelu(x, approximate=True)

def _silu(x):
    return jax.nn.silu(x)

def _sigmoid(x):
    return jax.nn.sigmoid(x)

def _layernorm(x, axis=-1, eps=1e-05):
    m = jnp.mean(x, axis=axis, keepdims=True)
    v = jnp.var(x, axis=axis, keepdims=True)
    return (x - m) / jnp.sqrt(v + eps)

def _scatter_add(tgt, idx, src, axis=0):
    return tgt.at[idx].add(src)

def _segment_sum(src, seg, n):
    return jax.ops.segment_sum(src, seg, n)
kernel_name = 'mk_hybrid_d2_jaxref_r8_632e92'

def setup_inputs(seed: int=0):
    np.random.seed(seed)
    _w = jnp.asarray

    def _L0_attn_a_setup():
        import jax, jax.numpy as jnp
        import numpy as np
        B, T, C = (2, 256, 256)
        NH, NKV, HD = (16, 8, 32)
        SOFTCAP = 50.0
        ROPE_BASE = 10000.0

        def _rotate_half(x):
            x1, x2 = (x[..., :x.shape[-1] // 2], x[..., x.shape[-1] // 2:])
            return jnp.concatenate((-x2, x1), axis=-1)

        def _rope_cos_sin(t, head_dim, dtype):
            inv_freq = 1.0 / ROPE_BASE ** (jnp.arange(0, head_dim, 2, dtype=jnp.int32).astype(jnp.float32) / head_dim)
            pos = jnp.arange(t, dtype=jnp.float32)
            freqs = pos[:, None] * inv_freq[None, :]
            emb = jnp.concatenate((freqs, freqs), axis=-1)
            return (jnp.cos(emb).astype(dtype)[None, None], jnp.sin(emb).astype(dtype)[None, None])
        key = jax.random.key(seed)
        ks = jax.random.split(key, 5)
        s = 0.02
        return {'X': jax.random.normal(ks[0], (B, T, C), dtype=jnp.float32), 'Wq': jax.random.normal(ks[1], (C, NH * HD), dtype=jnp.float32) * s, 'Wk': jax.random.normal(ks[2], (C, NKV * HD), dtype=jnp.float32) * s, 'Wv': jax.random.normal(ks[3], (C, NKV * HD), dtype=jnp.float32) * s, 'Wo': jax.random.normal(ks[4], (NH * HD, C), dtype=jnp.float32) * s}
    _L0_attn_a_in = _L0_attn_a_setup()

    def _L0_attn_b_setup():
        import jax, jax.numpy as jnp
        import numpy as np
        B, T, C = (2, 256, 256)
        NH, NKV = (16, 4)
        HD = C // NH

        def _rope(x):
            D = x.shape[-1]
            t = x.shape[-2]
            inv_freq = 1.0 / 10000.0 ** (jnp.arange(0, D, 2, dtype=jnp.float32) / D)
            freqs = jnp.arange(t, dtype=jnp.float32)[:, None] * inv_freq[None, :]
            emb = jnp.concatenate([freqs, freqs], axis=-1)
            cos, sin = (jnp.cos(emb), jnp.sin(emb))
            x1, x2 = (x[..., :D // 2], x[..., D // 2:])
            rotated = jnp.concatenate([-x2, x1], axis=-1)
            return x * cos + rotated * sin
        key = jax.random.key(seed)
        ks = jax.random.split(key, 5)
        w = lambda k, shape: jax.random.normal(k, shape, jnp.float32) * 0.02
        return {'x': jax.random.normal(ks[0], (B, T, C), jnp.float32), 'Wq': w(ks[1], (C, C)), 'Wk': w(ks[2], (C, NKV * HD)), 'Wv': w(ks[3], (C, NKV * HD)), 'Wproj': w(ks[4], (C, C))}
    _L0_attn_b_in = _L0_attn_b_setup()

    def _L0_ffn_setup():
        import jax, jax.numpy as jnp
        import numpy as np
        B, P = (32, 32)
        DIMS = [256, 512, 512, 256]
        key = jax.random.key(seed)
        ks = jax.random.split(key, 7)

        def lin(k, fan_out, fan_in):
            s = 1.0 / np.sqrt(fan_in)
            return jax.random.uniform(k, (fan_out, fan_in), jnp.float32, -s, s)
        return {'classifier_input': jax.random.normal(ks[0], (B, P, DIMS[0]), jnp.float32), 'W1': lin(ks[1], DIMS[1], DIMS[0]), 'b1': jax.random.uniform(ks[2], (DIMS[1],), jnp.float32, -0.02, 0.02), 'W2': lin(ks[3], DIMS[2], DIMS[1]), 'b2': jax.random.uniform(ks[4], (DIMS[2],), jnp.float32, -0.02, 0.02), 'W3': lin(ks[5], DIMS[3], DIMS[2]), 'b3': jax.random.uniform(ks[6], (DIMS[3],), jnp.float32, -0.02, 0.02)}
    _L0_ffn_in = _L0_ffn_setup()

    def _L1_attn_a_setup():
        import jax, jax.numpy as jnp
        import numpy as np
        B, S, E, H, KVH = (2, 128, 256, 16, 4)
        D = E // H
        RATIO = H // KVH
        NEG = -1e+30
        EPS = 1e-08
        LAM_INIT = 0.8 - 0.6 * float(np.exp(-0.3 * 0))

        def _rope(t):
            d2 = t.shape[-1]
            theta = 1.0 / 10000.0 ** (jnp.arange(0, d2, 2, dtype=jnp.float32) / d2)
            ang = jnp.arange(t.shape[1], dtype=jnp.float32)[:, None] * theta[None, :]
            cos = jnp.cos(ang)[None, :, None, :]
            sin = jnp.sin(ang)[None, :, None, :]
            tr = t.reshape(*t.shape[:-1], d2 // 2, 2)
            re, im = (tr[..., 0], tr[..., 1])
            out = jnp.stack([re * cos - im * sin, re * sin + im * cos], axis=-1)
            return out.reshape(t.shape)
        key = jax.random.key(seed)
        ks = jax.random.split(key, 10)
        sc = 0.02
        return {'x': jax.random.normal(ks[0], (B, S, E), jnp.float32), 'Wq': jax.random.normal(ks[1], (E, 2 * H * D), jnp.float32) * sc, 'Wk': jax.random.normal(ks[2], (E, 2 * KVH * D), jnp.float32) * sc, 'Wv': jax.random.normal(ks[3], (E, KVH * D), jnp.float32) * sc, 'Wo': jax.random.normal(ks[4], (E, E), jnp.float32) * sc, 'lq1': jax.random.normal(ks[5], (H, D), jnp.float32) * 0.1, 'lq2': jax.random.normal(ks[6], (H, D), jnp.float32) * 0.1, 'lk1': jax.random.normal(ks[7], (H, D), jnp.float32) * 0.1, 'lk2': jax.random.normal(ks[8], (H, D), jnp.float32) * 0.1, 'rms_w': jnp.ones((D,), jnp.float32)}
    _L1_attn_a_in = _L1_attn_a_setup()

    def _L1_attn_b_setup():
        import jax, jax.numpy as jnp
        import numpy as np
        EPS = 1e-06
        CHUNK = 16

        def _ln(x, g, b):
            mu = jnp.mean(x, -1, keepdims=True)
            var = jnp.var(x, -1, keepdims=True)
            xhat = (x - mu) * jax.lax.rsqrt(var + EPS)
            return g * xhat + b

        def chunk_ttt_linear(q, k, v, w, b, eta, scale=1.0):
            B, T, H, D = q.shape
            NC = T // CHUNK
            q = q * scale
            qc = q.reshape(B, NC, CHUNK, H, D).swapaxes(0, 1)
            kc = k.reshape(B, NC, CHUNK, H, D).swapaxes(0, 1)
            vc = v.reshape(B, NC, CHUNK, H, D).swapaxes(0, 1)
            ec = eta.reshape(B, NC, CHUNK, H).swapaxes(0, 1)
            tri = jnp.tril(jnp.ones((CHUNK, CHUNK), bool))
            S0 = jnp.zeros((B, H, D, D), q.dtype)

            def step(S, inp):
                qi, ki, vi, ei = inp
                kh = jnp.einsum('bchd,bhde->bche', ki, S)
                target = vi - ki
                mu = jnp.mean(kh, -1, keepdims=True)
                rstd = jax.lax.rsqrt(jnp.var(kh, -1, keepdims=True) + EPS)
                kh_hat = (kh - mu) * rstd
                g = w * kh_hat + b - target
                gw = g * w
                v_new = (gw - jnp.mean(gw, -1, keepdims=True) - kh_hat * jnp.mean(gw * kh_hat, -1, keepdims=True)) * rstd
                A = jnp.einsum('bchd,bshd->bhcs', qi, ki)
                A = jnp.where(tri, A, 0.0) * jnp.transpose(ei, (0, 2, 1))[:, :, None, :]
                qh = jnp.einsum('bchd,bhde->bche', qi, S) - jnp.einsum('bhcs,bshe->bche', A, v_new)
                o = qi + _ln(qh, w, b)
                S = S - jnp.einsum('bchd,bche->bhde', ki * ei[..., None], v_new)
                return (S, o)
            S_fin, o = jax.lax.scan(step, S0, (qc, kc, vc, ec))
            o = o.swapaxes(0, 1).reshape(B, T, H, D)
            return (o, S_fin)
        key = jax.random.key(seed)
        ks = jax.random.split(key, 11)
        B, T, D, H = (2, 512, 256, 16)
        Dh = D // H
        std = 0.02
        x = jax.random.normal(ks[0], (B, T, D), jnp.float32)
        Wq = jax.random.normal(ks[1], (D, D), jnp.float32) * std
        Wk = jax.random.normal(ks[2], (D, D), jnp.float32) * std
        Wv = jax.random.normal(ks[3], (D, D), jnp.float32) * std
        Wo = jax.random.normal(ks[4], (D, D), jnp.float32) * std
        Wbeta = jax.random.normal(ks[5], (D, H), jnp.float32) * std
        ln_w = 1.0 + jax.random.normal(ks[6], (H, Dh), jnp.float32) * std
        ln_b = jax.random.normal(ks[7], (H, Dh), jnp.float32) * std
        Wg1 = jax.random.normal(ks[8], (D, Dh), jnp.float32) * std
        Wg2 = jax.random.normal(ks[9], (Dh, D), jnp.float32) * std
        norm_w = 1.0 + jax.random.normal(ks[10], (D,), jnp.float32) * std
        return dict(x=x, Wq=Wq, Wk=Wk, Wv=Wv, Wo=Wo, Wbeta=Wbeta, ln_w=ln_w, ln_b=ln_b, Wg1=Wg1, Wg2=Wg2, norm_w=norm_w)
    _L1_attn_b_in = _L1_attn_b_setup()

    def _L1_ffn_setup():
        import jax, jax.numpy as jnp
        import numpy as np
        BLOCK_SIZE = 32
        HIDDEN_SIZE = 256
        MLP_DIM = 2048
        NVFP4_LUT = jnp.array([0.0, 0.5, 1.0, 1.5, 2.0, 3.0, 4.0, 6.0, 0.0, -0.5, -1.0, -1.5, -2.0, -3.0, -4.0, -6.0], dtype=jnp.float32)

        def dequant_nvfp4(W_packed, scales, block=BLOCK_SIZE):
            N = W_packed.shape[0]
            low = W_packed & 15
            high = W_packed >> 4 & 15
            idx = jnp.stack([low, high], axis=-1).reshape(N, -1)
            vals = NVFP4_LUT[idx]
            K = vals.shape[1]
            vals = vals.reshape(N, K // block, block) * scales[:, :, None]
            return vals.reshape(N, K)
        key = jax.random.key(seed)
        ks = jax.random.split(key, 7)
        x = jax.random.normal(ks[0], (4, 32, HIDDEN_SIZE), dtype=jnp.float32)
        gate_W_packed = jax.random.randint(ks[1], (MLP_DIM, HIDDEN_SIZE // 2), 0, 32, dtype=jnp.int32)
        gate_scales = jax.random.uniform(ks[2], (MLP_DIM, HIDDEN_SIZE // BLOCK_SIZE), dtype=jnp.float32) * 0.1 + 0.001
        up_W_packed = jax.random.randint(ks[3], (MLP_DIM, HIDDEN_SIZE // 2), 0, 32, dtype=jnp.int32)
        up_scales = jax.random.uniform(ks[4], (MLP_DIM, HIDDEN_SIZE // BLOCK_SIZE), dtype=jnp.float32) * 0.1 + 0.001
        down_W_packed = jax.random.randint(ks[5], (HIDDEN_SIZE, MLP_DIM // 2), 0, 32, dtype=jnp.int32)
        down_scales = jax.random.uniform(ks[6], (HIDDEN_SIZE, MLP_DIM // BLOCK_SIZE), dtype=jnp.float32) * 0.1 + 0.001
        return {'x': x, 'gate_W_packed': gate_W_packed, 'gate_scales': gate_scales, 'up_W_packed': up_W_packed, 'up_scales': up_scales, 'down_W_packed': down_W_packed, 'down_scales': down_scales}
    _L1_ffn_in = _L1_ffn_setup()
    _d = {'L0_attn_a_X': _L0_attn_a_in['X'], 'L0_attn_a_Wq': _L0_attn_a_in['Wq'], 'L0_attn_a_Wk': _L0_attn_a_in['Wk'], 'L0_attn_a_Wv': _L0_attn_a_in['Wv'], 'L0_attn_a_Wo': _L0_attn_a_in['Wo'], 'L0_attn_b_Wq': _L0_attn_b_in['Wq'], 'L0_attn_b_Wk': _L0_attn_b_in['Wk'], 'L0_attn_b_Wv': _L0_attn_b_in['Wv'], 'L0_attn_b_Wproj': _L0_attn_b_in['Wproj'], 'L0_ffn_W1': _L0_ffn_in['W1'], 'L0_ffn_b1': _L0_ffn_in['b1'], 'L0_ffn_W2': _L0_ffn_in['W2'], 'L0_ffn_b2': _L0_ffn_in['b2'], 'L0_ffn_W3': _L0_ffn_in['W3'], 'L0_ffn_b3': _L0_ffn_in['b3'], 'L1_attn_a_Wq': _L1_attn_a_in['Wq'], 'L1_attn_a_Wk': _L1_attn_a_in['Wk'], 'L1_attn_a_Wv': _L1_attn_a_in['Wv'], 'L1_attn_a_Wo': _L1_attn_a_in['Wo'], 'L1_attn_a_lq1': _L1_attn_a_in['lq1'], 'L1_attn_a_lq2': _L1_attn_a_in['lq2'], 'L1_attn_a_lk1': _L1_attn_a_in['lk1'], 'L1_attn_a_lk2': _L1_attn_a_in['lk2'], 'L1_attn_a_rms_w': _L1_attn_a_in['rms_w'], 'L1_attn_b_Wq': _L1_attn_b_in['Wq'], 'L1_attn_b_Wk': _L1_attn_b_in['Wk'], 'L1_attn_b_Wv': _L1_attn_b_in['Wv'], 'L1_attn_b_Wo': _L1_attn_b_in['Wo'], 'L1_attn_b_Wbeta': _L1_attn_b_in['Wbeta'], 'L1_attn_b_ln_w': _L1_attn_b_in['ln_w'], 'L1_attn_b_ln_b': _L1_attn_b_in['ln_b'], 'L1_attn_b_Wg1': _L1_attn_b_in['Wg1'], 'L1_attn_b_Wg2': _L1_attn_b_in['Wg2'], 'L1_attn_b_norm_w': _L1_attn_b_in['norm_w'], 'L1_ffn_gate_W_packed': _L1_ffn_in['gate_W_packed'], 'L1_ffn_gate_scales': _L1_ffn_in['gate_scales'], 'L1_ffn_up_W_packed': _L1_ffn_in['up_W_packed'], 'L1_ffn_up_scales': _L1_ffn_in['up_scales'], 'L1_ffn_down_W_packed': _L1_ffn_in['down_W_packed'], 'L1_ffn_down_scales': _L1_ffn_in['down_scales']}
    _x0 = _d['L0_attn_a_X']
    _d['L0_attn_a_X'] = jax.random.normal(jax.random.fold_in(jax.random.key(seed), 1), (2, 1024, 256), dtype=_x0.dtype)
    del _x0
    return _d

def reference(L0_attn_a_X, L0_attn_a_Wq, L0_attn_a_Wk, L0_attn_a_Wv, L0_attn_a_Wo, L0_attn_b_Wq, L0_attn_b_Wk, L0_attn_b_Wv, L0_attn_b_Wproj, L0_ffn_W1, L0_ffn_b1, L0_ffn_W2, L0_ffn_b2, L0_ffn_W3, L0_ffn_b3, L1_attn_a_Wq, L1_attn_a_Wk, L1_attn_a_Wv, L1_attn_a_Wo, L1_attn_a_lq1, L1_attn_a_lq2, L1_attn_a_lk1, L1_attn_a_lk2, L1_attn_a_rms_w, L1_attn_b_Wq, L1_attn_b_Wk, L1_attn_b_Wv, L1_attn_b_Wo, L1_attn_b_Wbeta, L1_attn_b_ln_w, L1_attn_b_ln_b, L1_attn_b_Wg1, L1_attn_b_Wg2, L1_attn_b_norm_w, L1_ffn_gate_W_packed, L1_ffn_gate_scales, L1_ffn_up_W_packed, L1_ffn_up_scales, L1_ffn_down_W_packed, L1_ffn_down_scales):

    def _L0_attn_a_ref(X, Wq, Wk, Wv, Wo):
        import jax, jax.numpy as jnp
        import numpy as np
        B, T, C = (2, 256, 256)
        NH, NKV, HD = (16, 8, 32)
        SOFTCAP = 50.0
        ROPE_BASE = 10000.0

        def _rotate_half(x):
            x1, x2 = (x[..., :x.shape[-1] // 2], x[..., x.shape[-1] // 2:])
            return jnp.concatenate((-x2, x1), axis=-1)

        def _rope_cos_sin(t, head_dim, dtype):
            inv_freq = 1.0 / ROPE_BASE ** (jnp.arange(0, head_dim, 2, dtype=jnp.int32).astype(jnp.float32) / head_dim)
            pos = jnp.arange(t, dtype=jnp.float32)
            freqs = pos[:, None] * inv_freq[None, :]
            emb = jnp.concatenate((freqs, freqs), axis=-1)
            return (jnp.cos(emb).astype(dtype)[None, None], jnp.sin(emb).astype(dtype)[None, None])
        b, t, c = X.shape
        n_rep = NH // NKV
        q = (X @ Wq).reshape(b, t, NH, HD).transpose(0, 2, 1, 3)
        k = (X @ Wk).reshape(b, t, NKV, HD).transpose(0, 2, 1, 3)
        v = (X @ Wv).reshape(b, t, NKV, HD).transpose(0, 2, 1, 3)
        cos, sin = _rope_cos_sin(t, HD, X.dtype)
        q = q * cos + _rotate_half(q) * sin
        k = k * cos + _rotate_half(k) * sin
        k = jnp.repeat(k, n_rep, axis=1)
        v = jnp.repeat(v, n_rep, axis=1)
        scale = 256.0 ** (-0.5)
        att = jnp.einsum('bhqd,bhkd->bhqk', q, k) * scale
        att = SOFTCAP * jnp.tanh(att / SOFTCAP)
        causal = jnp.tril(jnp.ones((t, t), dtype=bool))
        att = jnp.where(causal[None, None], att, -jnp.inf)
        att = jax.nn.softmax(att, axis=-1)
        y = jnp.einsum('bhqk,bhkd->bhqd', att, v)
        y = y.transpose(0, 2, 1, 3).reshape(b, t, NH * HD)
        return y @ Wo

    def _L0_attn_b_ref(x, Wq, Wk, Wv, Wproj):
        import jax, jax.numpy as jnp
        import numpy as np
        B, T, C = (2, 256, 256)
        NH, NKV = (16, 4)
        HD = C // NH

        def _rope(x):
            D = x.shape[-1]
            t = x.shape[-2]
            inv_freq = 1.0 / 10000.0 ** (jnp.arange(0, D, 2, dtype=jnp.float32) / D)
            freqs = jnp.arange(t, dtype=jnp.float32)[:, None] * inv_freq[None, :]
            emb = jnp.concatenate([freqs, freqs], axis=-1)
            cos, sin = (jnp.cos(emb), jnp.sin(emb))
            x1, x2 = (x[..., :D // 2], x[..., D // 2:])
            rotated = jnp.concatenate([-x2, x1], axis=-1)
            return x * cos + rotated * sin
        b, t, c = x.shape
        q = (x @ Wq).reshape(b, t, NH, HD).transpose(0, 2, 1, 3)
        k = (x @ Wk).reshape(b, t, NKV, HD).transpose(0, 2, 1, 3)
        v = (x @ Wv).reshape(b, t, NKV, HD).transpose(0, 2, 1, 3)
        q = _rope(q)
        k = _rope(k)
        rep = NH // NKV
        k = jnp.repeat(k, rep, axis=1)
        v = jnp.repeat(v, rep, axis=1)
        scale = 1.0 / jnp.sqrt(jnp.float32(HD))
        scores = jnp.einsum('bhqd,bhkd->bhqk', q, k) * scale
        causal = jnp.tril(jnp.ones((t, t), dtype=bool))
        scores = jnp.where(causal, scores, jnp.finfo(scores.dtype).min)
        attn = jax.nn.softmax(scores, axis=-1)
        y = jnp.einsum('bhqk,bhkd->bhqd', attn, v)
        y = y.transpose(0, 2, 1, 3).reshape(b, t, c)
        return y @ Wproj

    def _L0_ffn_ref(classifier_input, W1, b1, W2, b2, W3, b3):
        import jax, jax.numpy as jnp
        import numpy as np
        B, P = (32, 32)
        DIMS = [256, 512, 512, 256]
        x = classifier_input
        x = jax.nn.relu(jnp.einsum('bpd,hd->bph', x, W1) + b1)
        x = jax.nn.relu(jnp.einsum('bpd,hd->bph', x, W2) + b2)
        out = jnp.einsum('bpd,od->bpo', x, W3) + b3
        return out

    def _L1_attn_a_ref(x, Wq, Wk, Wv, Wo, lq1, lq2, lk1, lk2, rms_w):
        import jax, jax.numpy as jnp
        import numpy as np
        B, S, E, H, KVH = (2, 128, 256, 16, 4)
        D = E // H
        RATIO = H // KVH
        NEG = -1e+30
        EPS = 1e-08
        LAM_INIT = 0.8 - 0.6 * float(np.exp(-0.3 * 0))

        def _rope(t):
            d2 = t.shape[-1]
            theta = 1.0 / 10000.0 ** (jnp.arange(0, d2, 2, dtype=jnp.float32) / d2)
            ang = jnp.arange(t.shape[1], dtype=jnp.float32)[:, None] * theta[None, :]
            cos = jnp.cos(ang)[None, :, None, :]
            sin = jnp.sin(ang)[None, :, None, :]
            tr = t.reshape(*t.shape[:-1], d2 // 2, 2)
            re, im = (tr[..., 0], tr[..., 1])
            out = jnp.stack([re * cos - im * sin, re * sin + im * cos], axis=-1)
            return out.reshape(t.shape)
        b, s, _ = x.shape
        q = (x @ Wq).reshape(b, s, H, 2 * D)
        k = (x @ Wk).reshape(b, s, KVH, 2 * D)
        v = (x @ Wv).reshape(b, s, KVH, D)
        q = _rope(q)
        k = _rope(k)
        k = jnp.repeat(k, RATIO, axis=2)
        v = jnp.repeat(v, RATIO, axis=2)
        qd = q.reshape(b, s, H, 2, D)
        kd = k.reshape(b, s, H, 2, D)
        energy = jnp.einsum('bqhad,bkhad->bahqk', qd, kd)
        causal = jnp.triu(jnp.ones((s, s), dtype=bool), 1)
        energy = jnp.where(causal, NEG, energy)
        scores = jax.nn.softmax(energy / np.sqrt(D), axis=-1)
        lam = (jnp.exp(jnp.sum(lq1 * lk1, -1)) - jnp.exp(jnp.sum(lq2 * lk2, -1)) + LAM_INIT)[None, :, None, None]
        diff = scores[:, 0] - lam * scores[:, 1]
        diff = jnp.where(causal, NEG, diff)
        diff = jax.nn.softmax(diff, axis=-1)
        att = jnp.einsum('bhqv,bvhd->bqhd', diff, v)
        att = att * jax.lax.rsqrt(jnp.mean(att * att, axis=-1, keepdims=True) + EPS) * rms_w
        att = att * (1.0 - LAM_INIT)
        return att.reshape(b, s, E) @ Wo

    def _L1_attn_b_ref(x, Wq, Wk, Wv, Wo, Wbeta, ln_w, ln_b, Wg1, Wg2, norm_w):
        import jax, jax.numpy as jnp
        import numpy as np
        EPS = 1e-06
        CHUNK = 16

        def _ln(x, g, b):
            mu = jnp.mean(x, -1, keepdims=True)
            var = jnp.var(x, -1, keepdims=True)
            xhat = (x - mu) * jax.lax.rsqrt(var + EPS)
            return g * xhat + b

        def chunk_ttt_linear(q, k, v, w, b, eta, scale=1.0):
            B, T, H, D = q.shape
            NC = T // CHUNK
            q = q * scale
            qc = q.reshape(B, NC, CHUNK, H, D).swapaxes(0, 1)
            kc = k.reshape(B, NC, CHUNK, H, D).swapaxes(0, 1)
            vc = v.reshape(B, NC, CHUNK, H, D).swapaxes(0, 1)
            ec = eta.reshape(B, NC, CHUNK, H).swapaxes(0, 1)
            tri = jnp.tril(jnp.ones((CHUNK, CHUNK), bool))
            S0 = jnp.zeros((B, H, D, D), q.dtype)

            def step(S, inp):
                qi, ki, vi, ei = inp
                kh = jnp.einsum('bchd,bhde->bche', ki, S)
                target = vi - ki
                mu = jnp.mean(kh, -1, keepdims=True)
                rstd = jax.lax.rsqrt(jnp.var(kh, -1, keepdims=True) + EPS)
                kh_hat = (kh - mu) * rstd
                g = w * kh_hat + b - target
                gw = g * w
                v_new = (gw - jnp.mean(gw, -1, keepdims=True) - kh_hat * jnp.mean(gw * kh_hat, -1, keepdims=True)) * rstd
                A = jnp.einsum('bchd,bshd->bhcs', qi, ki)
                A = jnp.where(tri, A, 0.0) * jnp.transpose(ei, (0, 2, 1))[:, :, None, :]
                qh = jnp.einsum('bchd,bhde->bche', qi, S) - jnp.einsum('bhcs,bshe->bche', A, v_new)
                o = qi + _ln(qh, w, b)
                S = S - jnp.einsum('bchd,bche->bhde', ki * ei[..., None], v_new)
                return (S, o)
            S_fin, o = jax.lax.scan(step, S0, (qc, kc, vc, ec))
            o = o.swapaxes(0, 1).reshape(B, T, H, D)
            return (o, S_fin)
        B, T, D = x.shape
        H, Dh = ln_w.shape
        q = jax.nn.silu(x @ Wq).reshape(B, T, H, Dh)
        k = (x @ Wk).reshape(B, T, H, Dh)
        k = k * jax.lax.rsqrt(jnp.sum(k * k, -1, keepdims=True) + EPS)
        v = (x @ Wv).reshape(B, T, H, Dh)
        beta = jax.nn.sigmoid(x @ Wbeta) * 2.0
        o, _ = chunk_ttt_linear(q, k, v, ln_w, ln_b, beta, 1.0)
        gate = x @ Wg1 @ Wg2
        og = o * jax.nn.sigmoid(gate.reshape(B, T, H, Dh))
        og = og * jax.lax.rsqrt(jnp.mean(og * og, -1, keepdims=True) + EPS)
        o = og.reshape(B, T, D) * norm_w
        return o @ Wo

    def _L1_ffn_ref(x, gate_W_packed, gate_scales, up_W_packed, up_scales, down_W_packed, down_scales):
        import jax, jax.numpy as jnp
        import numpy as np
        BLOCK_SIZE = 32
        HIDDEN_SIZE = 256
        MLP_DIM = 2048
        NVFP4_LUT = jnp.array([0.0, 0.5, 1.0, 1.5, 2.0, 3.0, 4.0, 6.0, 0.0, -0.5, -1.0, -1.5, -2.0, -3.0, -4.0, -6.0], dtype=jnp.float32)

        def dequant_nvfp4(W_packed, scales, block=BLOCK_SIZE):
            N = W_packed.shape[0]
            low = W_packed & 15
            high = W_packed >> 4 & 15
            idx = jnp.stack([low, high], axis=-1).reshape(N, -1)
            vals = NVFP4_LUT[idx]
            K = vals.shape[1]
            vals = vals.reshape(N, K // block, block) * scales[:, :, None]
            return vals.reshape(N, K)
        B, S, H = x.shape
        xt = x.reshape(B * S, H)
        Wg = dequant_nvfp4(gate_W_packed, gate_scales)
        Wu = dequant_nvfp4(up_W_packed, up_scales)
        Wd = dequant_nvfp4(down_W_packed, down_scales)
        gate = jnp.einsum('th,nh->tn', xt, Wg)
        up = jnp.einsum('th,nh->tn', xt, Wu)
        gelu = jnp.tanh(0.7978845608028654 * (gate + 0.044715 * gate ** 3)) * gate * 0.5 + gate * 0.5
        inter = gelu * up
        out = jnp.einsum('tn,hn->th', inter, Wd)
        return out.reshape(B, S, H)
    x = L0_attn_a_X
    x = x + _L0_attn_a_ref(_layernorm(x, axis=-1), L0_attn_a_Wq, L0_attn_a_Wk, L0_attn_a_Wv, L0_attn_a_Wo)
    x = x + _L0_ffn_ref(_layernorm(x, axis=-1), L0_ffn_W1, L0_ffn_b1, L0_ffn_W2, L0_ffn_b2, L0_ffn_W3, L0_ffn_b3)
    x = x + _L0_attn_b_ref(_layernorm(x, axis=-1), L0_attn_b_Wq, L0_attn_b_Wk, L0_attn_b_Wv, L0_attn_b_Wproj)
    x = x + _L0_ffn_ref(_layernorm(x, axis=-1), L0_ffn_W1, L0_ffn_b1, L0_ffn_W2, L0_ffn_b2, L0_ffn_W3, L0_ffn_b3)
    x = x + _L1_attn_a_ref(_layernorm(x, axis=-1), L1_attn_a_Wq, L1_attn_a_Wk, L1_attn_a_Wv, L1_attn_a_Wo, L1_attn_a_lq1, L1_attn_a_lq2, L1_attn_a_lk1, L1_attn_a_lk2, L1_attn_a_rms_w)
    x = x + _L1_ffn_ref(_layernorm(x, axis=-1), L1_ffn_gate_W_packed, L1_ffn_gate_scales, L1_ffn_up_W_packed, L1_ffn_up_scales, L1_ffn_down_W_packed, L1_ffn_down_scales)
    x = x + _L1_attn_b_ref(_layernorm(x, axis=-1), L1_attn_b_Wq, L1_attn_b_Wk, L1_attn_b_Wv, L1_attn_b_Wo, L1_attn_b_Wbeta, L1_attn_b_ln_w, L1_attn_b_ln_b, L1_attn_b_Wg1, L1_attn_b_Wg2, L1_attn_b_norm_w)
    x = x + _L1_ffn_ref(_layernorm(x, axis=-1), L1_ffn_gate_W_packed, L1_ffn_gate_scales, L1_ffn_up_W_packed, L1_ffn_up_scales, L1_ffn_down_W_packed, L1_ffn_down_scales)
    return x

_drawn_inputs = setup_inputs


def setup_inputs(seed=0):
    import zlib

    import numpy as np

    out = dict(_drawn_inputs(seed))
    spreads = {'L1_attn_a_rms_w': (1.0, 0.2)}
    factors = {'L0_attn_a_Wq': 8.0,
     'L0_attn_a_Wk': 8.0,
     'L0_attn_b_Wq': 8.0,
     'L0_attn_b_Wk': 8.0,
     'L0_ffn_b1': 6.955,
     'L1_attn_a_Wq': 8.0,
     'L1_attn_a_Wk': 8.0,
     'L1_attn_a_lq1': 8.0,
     'L1_attn_a_lq2': 8.0,
     'L1_attn_a_lk1': 8.0,
     'L1_attn_a_lk2': 8.0,
     'L1_attn_b_Wv': 2.782,
     'L1_attn_b_Wbeta': 8.0,
     'L1_attn_b_ln_w': 59.995,
     'L1_attn_b_ln_b': 8.0,
     'L1_attn_b_Wg1': 8.0,
     'L1_attn_b_Wg2': 8.0,
     'L1_attn_b_norm_w': 64.0}
    for name, (base, spread) in spreads.items():
        noise = np.random.default_rng([zlib.crc32(name.encode()), seed]).standard_normal(out[name].shape)
        drawn = base * np.exp(spread * noise) if base else spread * noise
        out[name] = jnp.asarray(drawn.astype(out[name].dtype))
    for name, factor in factors.items():
        out[name] = (out[name] * factor).astype(out[name].dtype)
    return out
```

```python
from contextlib import ExitStack

import concourse.bass as bass
import numpy as np
from concourse import mybir

F32 = mybir.dt.float32
BF16 = mybir.dt.bfloat16
I32 = mybir.dt.int32
ALU = mybir.AluOpType
ACT = mybir.ActivationFunctionType
AX = mybir.AxisListType
ds = bass.ds

P = 128
B, T, C = 2, 1024, 256
TOK = B * T
TILES = TOK // P
BT = T // P
KC = C // P
QB = 512
NEG = -1.0e30


class Phase:

    def __init__(self, nc, tag):
        self.nc, self.tag, self.sems, self.stack = nc, tag, [], ExitStack()

    def sem(self, name):
        s = self.nc.alloc_semaphore(name=f"{self.tag}_{name}")
        self.sems.append(s)
        return s

    def sb(self, name, shape, dt=F32):
        return self.stack.enter_context(self.nc.sbuf_tensor(f"{self.tag}_{name}", shape, dt))

    def close(self):
        self.nc.clear_and_free_semaphores(self.sems)
        self.nc.all_engine_barrier()
        self.stack.close()


def load_and_constants(nc, m, x_d):
    ph = Phase(nc, "init")
    x_loaded, filled, made = ph.sem("x_loaded"), ph.sem("filled"), ph.sem("made")
    with nc.Block() as block:
        @block.sync
        def _(sp):
            sp.dma_start(m.x[:], x_d.rearrange("b (t p) c -> p (b t) c", p=P)).then_inc(x_loaded, 16)
            sp.wait_ge(x_loaded, 16)

        @block.gpsimd
        def _(pool):
            pool.memset(m.ident[:], 0.0).then_inc(filled, 1)
            pool.memset(m.later_k[:], 0.0).then_inc(filled, 1)
            pool.memset(m.later_q[:], 0.0).then_inc(filled, 1)
            pool.memset(m.keep[:], 1.0).then_inc(filled, 1)
            pool.wait_ge(filled, 4)
            pool.affine_select(out=m.ident[:], in_=m.ident[:], compare_op=ALU.not_equal, fill=1.0, base=0,
                               pattern=[[-1, P]], channel_multiplier=1).then_inc(made, 1)
            pool.affine_select(out=m.later_k[:], in_=m.later_k[:], compare_op=ALU.is_ge, fill=NEG, base=0,
                               pattern=[[-1, P]], channel_multiplier=1).then_inc(made, 1)
            pool.affine_select(out=m.later_q[:], in_=m.later_q[:], compare_op=ALU.is_ge, fill=NEG, base=0,
                               pattern=[[1, P]], channel_multiplier=-1).then_inc(made, 1)
            pool.affine_select(out=m.keep[:], in_=m.keep[:], compare_op=ALU.is_ge, fill=0.0, base=0,
                               pattern=[[1, P]], channel_multiplier=-1).then_inc(made, 1)

        @block.vector
        def _(dve):
            dve.wait_ge(made, 1)
            dve.tensor_copy(m.ident_b[:], m.ident[:]).then_inc(made, 1)
    ph.close()


def norm_transpose(nc, m, tag, interleave=False):
    ph = Phase(nc, tag)
    st = ph.sb("st", [P, TILES, 6])
    mv = ph.sb("mv", [P, TILES, 2])
    rstd = ph.sb("rstd", [P, TILES])
    xn = ph.sb("xn", [P, TILES, C])
    stats, var_eps, root = ph.sem("stats"), ph.sem("var_eps"), ph.sem("root")
    inverse, normed, turned, copied = ph.sem("inverse"), ph.sem("normed"), ph.sem("turned"), ph.sem("copied")
    with nc.Block() as block:
        @block.vector
        def _(dve):
            for t in range(TILES):
                dve.bn_stats(st[:, t, :], m.x[:, t, :]).then_inc(stats, 1)
            for t in range(TILES):
                dve.wait_ge(stats, t + 1)
                dve.bn_aggr(mv[:, t, :], st[:, t, :]).then_inc(var_eps, 1)
            dve.wait_ge(var_eps, TILES)
            dve.tensor_scalar(rstd[:], mv[:, :, 1], 1e-5, None, ALU.add).then_inc(var_eps, 1)
            dve.wait_ge(root, 1)
            dve.reciprocal(rstd[:], rstd[:]).then_inc(inverse, 1)
            dve.wait_ge(inverse, 1)
            for t in range(TILES):
                dve.tensor_scalar(xn[:, t, :], m.x[:, t, :], mv[:, t, 0:1], rstd[:, t:t + 1],
                                  ALU.subtract, ALU.mult).then_inc(normed, 1)
            for q in range(TILES // 4):
                dve.wait_ge(turned, 2 * q + 2)
                dve.tensor_copy(m.xnT[:, 1, q * 512:(q + 1) * 512], m.ps[:, 2 * q + 1, :])

        @block.scalar
        def _(act):
            act.wait_ge(var_eps, TILES + 1)
            act.activation(rstd[:], rstd[:], ACT.Sqrt).then_inc(root, 1)
            for q in range(TILES // 4):
                act.wait_ge(turned, 2 * q + 1)
                act.copy(m.xnT[:, 0, q * 512:(q + 1) * 512], m.ps[:, 2 * q, :])

        @block.tensor
        def _(pe):
            for q in range(TILES // 4):
                pe.wait_ge(normed, 4 * q + 4)
                for c in range(KC):
                    for t in range(4):
                        src = xn[:, 4 * q + t, c::2] if interleave else xn[:, 4 * q + t, c * P:(c + 1) * P]
                        last = pe.transpose(m.ps[:, 2 * q + c, t * P:(t + 1) * P], src, m.ident[:])
                    last.then_inc(turned, 1)
    ph.close()


def project_rope(nc, m, tag, w_d, tiles, wv_d, kv, hd, vpad, cos_d, sin_d, scr, v_sb):
    ph = Phase(nc, tag)
    w = ph.sb("w", [P, KC, 2 * tiles * P])
    wv = ph.sb("wv", [P, KC, kv * hd])
    cos = ph.sb("cos", [P, T])
    sin = ph.sb("sin", [P, T])
    tc = ph.sb("tc", [P, 2, QB])
    ts = ph.sb("ts", [P, 2, QB])
    r = ph.sb("r", [P, 2, QB])
    rest = ph.sb("rest", [P, 2, QB])
    parts = ph.sb("parts", [P, 2, 3, QB], BF16)
    loaded = ph.sem("loaded")
    product, turned, summed = ph.sem("product"), ph.sem("turned"), ph.sem("summed")
    high, low1, mid, low2 = ph.sem("high"), ph.sem("low1"), ph.sem("mid"), ph.sem("low2")
    stored = [ph.sem("stored0"), ph.sem("stored1")]
    v_product, v_copied, padded = ph.sem("v_product"), ph.sem("v_copied"), ph.sem("padded")
    items = [(mt, tb) for tb in range(TOK // QB) for mt in range(tiles)]
    with nc.Block() as block:
        @block.sync
        def _(sp):
            sp.dma_start(w[:], w_d.rearrange("(k p) n -> p k n", p=P)).then_inc(loaded, 16)
            sp.dma_start(wv[:], wv_d.rearrange("(k p) n -> p k n", p=P)).then_inc(loaded, 16)
            sp.dma_start(cos[:], cos_d).then_inc(loaded, 16)
            sp.dma_start(sin[:], sin_d).then_inc(loaded, 16)
            for n, (mt, tb) in enumerate(items):
                sp.wait_ge(low2, n + 1)
                sp.dma_start(scr[:, mt * P:(mt + 1) * P, tb * QB:(tb + 1) * QB].rearrange("s p n -> p s n"),
                             parts[:, n % 2, :, :]).then_inc(stored[n % 2], 16)
            for par in range(2):
                sp.wait_ge(stored[par], 16 * (len(items) // 2))

        @block.tensor
        def _(pe):
            pe.wait_ge(loaded, 64)
            for n, (mt, tb) in enumerate(items):
                if n >= 2:
                    pe.wait_ge(turned, n - 1)
                for s in range(2):
                    for k in range(KC):
                        col = (s * tiles + mt) * P
                        last = pe.matmul(m.ps[:, 2 * (n % 2) + s, :], w[:, k, col:col + P],
                                         m.xnT[:, k, tb * QB:(tb + 1) * QB], start=(k == 0), stop=(k == KC - 1))
                last.then_inc(product, 1)
            for t in range(TILES):
                if t >= 4:
                    pe.wait_ge(v_copied, t - 3)
                for k in range(KC):
                    last = pe.matmul(m.ps[:, 4 + t % 4, 0:kv * hd], m.xnT[:, k, t * P:(t + 1) * P], wv[:, k, :],
                                     start=(k == 0), stop=(k == KC - 1))
                last.then_inc(v_product, 1)

        @block.vector
        def _(dve):
            if vpad > hd:
                dve.memset(v_sb[:], 1.0).then_inc(padded, 1)
            dve.wait_ge(loaded, 64)
            for n, (mt, tb) in enumerate(items):
                at = (tb * QB) % T
                dve.wait_ge(product, n + 1)
                if n >= 2:
                    dve.wait_ge(summed, n - 1)
                dve.tensor_tensor(tc[:, n % 2, :], m.ps[:, 2 * (n % 2), :], cos[:, at:at + QB], ALU.mult)
                dve.tensor_tensor(ts[:, n % 2, :], m.ps[:, 2 * (n % 2) + 1, :], sin[:, at:at + QB],
                                  ALU.mult).then_inc(turned, 1)

        @block.gpsimd
        def _(pool):
            for n in range(len(items)):
                a = n % 2
                pool.wait_ge(turned, n + 1)
                if n >= 2:
                    pool.wait_ge(stored[a], 16 * (n // 2))
                pool.tensor_tensor(r[:, a, :], tc[:, a, :], ts[:, a, :], ALU.add).then_inc(summed, 1)
                pool.wait_ge(high, n + 1)
                pool.tensor_tensor(rest[:, a, :], r[:, a, :], parts[:, a, 0, :], ALU.subtract).then_inc(low1, 1)
                pool.wait_ge(mid, n + 1)
                pool.tensor_tensor(parts[:, a, 2, :], rest[:, a, :], parts[:, a, 1, :],
                                   ALU.subtract).then_inc(low2, 1)

        @block.scalar
        def _(act):
            for n in range(len(items)):
                a = n % 2
                act.wait_ge(summed, n + 1)
                act.copy(parts[:, a, 0, :], r[:, a, :]).then_inc(high, 1)
                act.wait_ge(low1, n + 1)
                act.copy(parts[:, a, 1, :], rest[:, a, :]).then_inc(mid, 1)
            if vpad > hd:
                act.wait_ge(padded, 1)
            for t in range(TILES):
                act.wait_ge(v_product, t + 1)
                act.copy(v_sb[:, t, :, 0:hd],
                         m.ps[:, 4 + t % 4, 0:kv * hd].rearrange("p (h d) -> p h d", h=kv)).then_inc(v_copied, 1)
    ph.close()


Q_PARTS = (0, 0, 0, 1, 1, 2)
K_PARTS = (0, 1, 2, 0, 1, 0)
HG = 4
GB = 16 // HG


def pipelined(e, ops, per, iters, lead=8):
    def slot(i, s, end):
        for lag, fn in ops:
            if 0 <= s - lag < end:
                fn(i, s - lag)

    assert max(lag for lag, _ in ops) < lead <= per
    for s in range(lead):
        slot(0, s, per)
    with e.Fori(0, iters - 1) as i:
        for s in range(lead, per + lead):
            slot(i, s, per + lead)
    for s in range(lead, per + max(lag for lag, _ in ops)):
        slot(iters - 1, s, per)


def wait(e, sem, i, each, k):
    if isinstance(i, int):
        if i * each + k > 0:
            e.wait_ge(sem, i * each + k)
    else:
        assert k > 0
        e.wait_ge(sem, i * each + k)


def attention(nc, m, tag, scr, v_sb, wo_d, hd, kv_in_group, q_rows, scale, softcap):
    ph = Phase(nc, tag)
    plain = not softcap
    stacks = 1 if 6 * hd <= 96 else 2
    per = 6 // stacks
    rows = per * hd
    aug = 3 if plain else 0
    ER = 3
    wo = ph.sb("wo", [P, GB, C])
    q_st = ph.sb("q_st", [rows + aug, 2, HG, stacks, T], BF16)
    k_st = ph.sb("k_st", [rows + aug, 2, kv_in_group, stacks, T], BF16)
    v_st = ph.sb("v_st", [P, 2, BT, kv_in_group, 32])
    e = ph.sb("e", [P, ER, HG, QB])
    rz = ph.sb("rz", [P, QB])
    y = ph.sb("y", [P, QB])
    if plain:
        q_row = ph.sb("q_row", [rows, 2, HG, T], BF16)
        k_row = ph.sb("k_row", [rows, 2, T], BF16)
        y_raw = ph.sb("y_raw", [P, QB])
        nm = ph.sb("nm", [P, HG, BT])
        nm_two = ph.sb("nm_two", [P, HG, 2, 4])
        nmT = ph.sb("nmT", [HG * BT, P])
        nmp = ph.sb("nmp", [HG * BT, 3, P], BF16)
        spread = ph.sb("spread", [P, P])
    else:
        ones = ph.sb("ones", [P, 32])
    wo_loaded, ones_set = ph.sem("wo_loaded"), ph.sem("ones_set")
    staged, row_staged = [ph.sem("staged0"), ph.sem("staged1")], [ph.sem("row_staged0"), ph.sem("row_staged1")]
    s_ready = [ph.sem("s_ready0"), ph.sem("s_ready1")]
    s_read = [ph.sem("s_read0"), ph.sem("s_read1")]
    exped, masked, weighed = ph.sem("exped"), ph.sem("masked"), ph.sem("weighed")
    raw_copied, z_spread = ph.sem("raw_copied"), ph.sem("z_spread")
    inverse, y_scaled, o_ready, o_added = ph.sem("inverse"), ph.sem("y_scaled"), ph.sem("o_ready"), ph.sem("o_added")
    row_scores, row_max, max_turned = ph.sem("row_scores"), ph.sem("row_max"), ph.sem("max_turned")
    max_step, max_staged = ph.sem("max_step"), ph.sem("max_staged")
    steps = [(qb, kt) for qb in range(T // QB) for kt in range((qb + 1) * QB // P)]
    NS, NQ = len(steps), T // QB
    PER, ITERS = 2 * NS, B * GB // 2
    ends = {s: qb for s, (qb, kt) in enumerate(steps) if kt == (qb + 1) * QB // P - 1}
    share = HG // kv_in_group
    N_DMA, SPLIT = 13, 6
    PIECES = 12
    lo_of = lambda qb, kt: max(kt * P - qb * QB, 0)

    def place(u):
        g, s = u // NS, u % NS
        return g, g % 2, s, *steps[s], lo_of(*steps[s])

    def piece(n):
        h, r = n // PIECES, n % PIECES
        if r < 4:
            return h, r, 0, (r + 1) * P, None
        t, c = 4 + (r - 4) // 2, (r - 4) % 2
        return h, t, c * QB, QB if c == 0 else (t - 3) * P, c

    with nc.Block() as block:
        @block.sync
        def _(sp):
            sp.dma_start(wo[:], wo_d.rearrange("(j p) n -> p j n", p=P)).then_inc(wo_loaded, 16)

            def stage(g):
                b, j, par = g // GB, g % GB, g % 2
                tok = slice(b * T, (b + 1) * T)
                for n in range(6):
                    row, st = (n % per) * hd, n // per
                    sp.dma_start(q_st[row:row + hd, par, :, st, :],
                                 scr[Q_PARTS[n], j * HG * hd:(j + 1) * HG * hd, tok]
                                 .rearrange("(h d) t -> d h t", d=hd)).then_inc(staged[par], 16)
                    k0 = q_rows + j * kv_in_group * hd
                    sp.dma_start(k_st[row:row + hd, par, :, st, :],
                                 scr[K_PARTS[n], k0:k0 + kv_in_group * hd, tok]
                                 .rearrange("(h d) t -> d h t", d=hd)).then_inc(staged[par], 16)
                sp.dma_start(v_st[:, par, :, :, :], v_sb[:, b * BT:(b + 1) * BT,
                                                         j * kv_in_group:(j + 1) * kv_in_group, :]).then_inc(staged[par], 16)

            def stage_rows(g):
                b, j, par = g // GB, g % GB, g % 2
                tok = slice(b * T, (b + 1) * T)
                for n in range(6):
                    sp.dma_start(q_row[n * hd:(n + 1) * hd, par, :, :],
                                 scr[Q_PARTS[n], j * HG * hd:(j + 1) * HG * hd, tok]
                                 .rearrange("(h d) t -> d h t", d=hd)).then_inc(row_staged[par], 16)
                    k0 = q_rows + j * hd
                    sp.dma_start(k_row[n * hd:(n + 1) * hd, par, :],
                                 scr[K_PARTS[n], k0:k0 + hd, tok]).then_inc(row_staged[par], 16)

            if plain:
                stage_rows(0)
                stage_rows(1)
            for g in range(B * GB):
                if g >= 2:
                    sp.wait_ge(weighed, (g - 1) * NS)
                stage(g)
                if plain:
                    sp.wait_ge(max_step, SPLIT * (g + 1))
                    for s in range(3):
                        sp.dma_start(q_st[rows + s:rows + s + 1, g % 2, :, 0, :], nmp[:, s, :]).then_inc(max_staged, 16)
                    if g + 2 < B * GB:
                        stage_rows(g + 2)

        @block.tensor
        def _(pe):
            pe.wait_ge(ones_set, 3 if plain else 1)
            pe.wait_ge(wo_loaded, 16)

            def row_piece(k):
                def run(i, u):
                    g, par, s, *_ = place(u)
                    n = 4 * s + k
                    h, t, key, keys, c = piece(n)
                    if n == 0:
                        pe.wait_ge(row_staged[par], i * (12 * 16) + (g // 2 + 1) * 12 * 16)
                    wait(pe, row_max, i, 4 * PER, 4 * u + k - 1)
                    last = pe.matmul(m.ps[:, 5 + k % 2, 0:keys], q_row[:, par, h, t * P:(t + 1) * P],
                                     k_row[:, par, key:key + keys], start=True, stop=True)
                    if c != 0:
                        last = pe.matmul(m.ps[:, 5 + k % 2, keys - P:keys], m.ident_b[:], m.later_k[:],
                                         start=False, stop=True, skip_group_check=True)
                    last.then_inc(row_scores, 1)
                return run

            def turn_maxima(i, u):
                g, par, s, *_ = place(u)
                if s == NS - 1:
                    wait(pe, max_step, i, 2 * SPLIT, g * SPLIT + 1)
                    wait(pe, o_added, i, 4 * NQ, 2 * (g - 1) * NQ + 2)
                    pe.transpose(m.ps[0:HG * BT, 7, 0:P], nm[:].rearrange("p h t -> p (h t)"), m.ident[:]).then_inc(max_turned, 1)

            def scores(p):
                def run(i, u):
                    g, par, s, qb, kt, lo = place(u)
                    if s == 0 and p == 0:
                        pe.wait_ge(staged[par], i * (16 * N_DMA) + (g // 2 + 1) * 16 * N_DMA)
                        if plain:
                            pe.wait_ge(max_staged, i * 96 + (g + 1) * 48)
                    wait(pe, s_read[p], i, PER, u)
                    for h in (2 * p, 2 * p + 1):
                        for st in range(stacks):
                            last = pe.matmul(m.ps[:, h, lo:QB], k_st[:, par, h // share, st, kt * P:(kt + 1) * P],
                                             q_st[:, par, h, st, qb * QB + lo:(qb + 1) * QB],
                                             start=(st == 0), stop=(st == stacks - 1))
                        if plain and kt * P >= qb * QB:
                            last = pe.matmul(m.ps[:, h, lo:lo + P], m.ident_b[:], m.later_q[:],
                                             start=False, stop=True, skip_group_check=True)
                    last.then_inc(s_ready[p], 1)
                return run

            def weigh(i, u):
                g, par, s, qb, kt, lo = place(u)
                wait(pe, exped, i, PER, u + 1)
                if kt * P >= qb * QB and not plain:
                    wait(pe, masked, i, 2 * BT, g * BT + kt + 1)
                if kt == 0:
                    wait(pe, raw_copied if plain else y_scaled, i, 2 * NQ, g * NQ + qb)
                for h in range(HG):
                    last = pe.matmul(m.ps[32 * h:32 * h + 32, 4, lo:QB], v_st[:, par, kt, h // share, :],
                                     e[:, u % ER, h, lo:QB], start=(kt == 0), stop=(s in ends))
                if not plain:
                    for h in range(HG):
                        last = pe.matmul(m.ps[32 * h:32 * h + 32, 5, lo:QB], ones[:], e[:, u % ER, h, lo:QB],
                                         start=(kt == 0), stop=(s in ends))
                last.then_inc(weighed, 1)

            def spread_z(i, u):
                g, par, s, qb, *_ = place(u)
                if s in ends:
                    wait(pe, raw_copied, i, 2 * NQ, g * NQ + qb + 1)
                    wait(pe, o_added, i, 4 * NQ, 2 * (g * NQ + qb))
                    if qb == 0 or g == 0 or not isinstance(i, int):
                        wait(pe, max_step, i, 2 * SPLIT, (g + qb) * SPLIT + 2)
                    pe.matmul(m.ps[:, 7, :], spread[:], y_raw[:], start=True, stop=True).then_inc(z_spread, 1)

            def project(half):
                def run(i, u):
                    g, par, s, qb, *_ = place(u)
                    if s not in ends:
                        return
                    bank = 7 if plain else 6 + half
                    wait(pe, y_scaled, i, 2 * NQ, g * NQ + qb + 1)
                    wait(pe, o_added, i, 4 * NQ, 2 * (g * NQ + qb) + half - (0 if plain else 1))
                    j = (i % 2) * 2 + g if isinstance(i, int) else (i + g // 2) % 2 * 2 + par
                    w = wo[:, j % GB, :] if isinstance(i, int) else wo[:, ds(j, 1), :].rearrange("p o c -> p (o c)")
                    for t in range(2):
                        q = (2 * half + t) * P
                        last = pe.matmul(m.ps[:, bank, t * C:(t + 1) * C], y[:, q:q + P], w, start=True, stop=True)
                    last.then_inc(o_ready, 1)
                return run

            if plain:
                pipelined(pe, [(1, turn_maxima), (0, row_piece(0)), (15, scores(0)), (0, row_piece(1)), (15, scores(1)), (0, row_piece(2)),
                               (17, weigh), (0, row_piece(3)), (18, spread_z),
                               (19, project(0)), (20, project(1))], PER, ITERS, lead=23)
            else:
                pipelined(pe, [(0, scores(0)), (0, scores(1)), (2, weigh), (3, project(0)), (4, project(1))], PER, ITERS)

        @block.scalar
        def _(act):
            def from_scores(i, u):
                g, par, s, qb, kt, lo = place(u)
                wait(act, weighed, i, PER, u - ER + 1)
                for p in range(2):
                    wait(act, s_ready[p], i, PER, u + 1)
                    src, dst = m.ps[:, 2 * p:2 * p + 2, lo:QB], e[:, u % ER, 2 * p:2 * p + 2, lo:QB]
                    if softcap:
                        act.activation(dst, src, ACT.Tanh, scale=scale / softcap).then_inc(s_read[p], 1)
                    else:
                        act.activation(dst, src, ACT.Exp, scale=scale).then_inc(s_read[p], 1)

            def exponential(i, u):
                g, par, s, qb, kt, lo = place(u)
                wait(act, s_read[1], i, PER, u + 1)
                tile = e[:, u % ER, :, lo:QB]
                act.activation(tile, tile, ACT.Exp, scale=softcap).then_inc(exped, 1)

            def signal(i, u):
                wait(act, s_read[1], i, PER, u + 1)
                act.sem_inc(exped, 1)

            def copy_raw(i, u):
                g, par, s, qb, *_ = place(u)
                if s in ends:
                    wait(act, weighed, i, PER, u + 1)
                    wait(act, y_scaled, i, 2 * NQ, g * NQ + qb)
                    act.copy(y_raw[:], m.ps[:, 4, :]).then_inc(raw_copied, 1)

            if plain:
                pipelined(act, [(15, from_scores), (15, signal), (17, copy_raw)], PER, ITERS, lead=23)
            else:
                pipelined(act, [(0, from_scores), (1, exponential)], PER, ITERS)

        @block.gpsimd
        def _(pool):
            if plain:
                pool.memset(k_st[rows:rows + aug, :, :, :, :], 1.0).then_inc(ones_set, 1)
                pool.wait_ge(ones_set, 1)
                pool.memset(spread[:], 0.0).then_inc(ones_set, 1)
                pool.wait_ge(ones_set, 2)
                sel = spread[:].rearrange("p (h r) -> p h r", r=32)
                pool.affine_select(out=sel, in_=sel, compare_op=ALU.not_equal, fill=1.0, base=-16,
                                   pattern=[[-32, HG], [0, 32]], channel_multiplier=1).then_inc(ones_set, 1)
            else:
                pool.memset(ones[:], 1.0).then_inc(ones_set, 1)

                def mask(i, u):
                    g, par, s, qb, kt, lo = place(u)
                    if kt * P >= qb * QB:
                        wait(pool, exped, i, PER, u + 1)
                        tile = e[:, u % ER, :, lo:lo + P]
                        pool.tensor_tensor(tile, tile, m.keep[:, None, :].to_broadcast([P, HG, P]),
                                           ALU.mult).then_inc(masked, 1)

                pipelined(pool, [(1, mask)], PER, ITERS)

        @block.vector
        def _(dve):
            def maxima(i, u):
                g, par, s, *_ = place(u)
                for k in range(4):
                    h, t, key, keys, c = piece(4 * s + k)
                    if 4 * s + k == 0:
                        wait(dve, max_turned, i, 2, g)
                    wait(dve, row_scores, i, 4 * PER, 4 * u + k + 1)
                    dst = nm[:, h, t:t + 1] if c is None else nm_two[:, h, c, t - 4:t - 3]
                    dve.tensor_reduce(dst, m.ps[:, 5 + k % 2, 0:keys], AX.X, ALU.max, negate=True).then_inc(row_max, 1)

            def split_maxima(i, u):
                g, par, s, *_ = place(u)
                if s != NS - 1:
                    return
                step = lambda k: wait(dve, max_step, i, 2 * SPLIT, g * SPLIT + k)
                wait(dve, row_max, i, 4 * PER, 4 * u + 4)
                dve.tensor_tensor(nm[:, :, 4:8], nm_two[:, :, 0, :], nm_two[:, :, 1, :], ALU.min).then_inc(max_step, 1)
                wait(dve, max_staged, i, 96, g * 48)
                wait(dve, max_turned, i, 2, g + 1)
                dve.tensor_copy(nmT[:], m.ps[0:HG * BT, 7, 0:P]).then_inc(max_step, 1)
                step(2)
                dve.tensor_copy(nmp[:, 0, :], nmT[:]).then_inc(max_step, 1)
                step(3)
                dve.tensor_tensor(nmT[:], nmT[:], nmp[:, 0, :], ALU.subtract).then_inc(max_step, 1)
                step(4)
                dve.tensor_copy(nmp[:, 1, :], nmT[:]).then_inc(max_step, 1)
                step(5)
                dve.tensor_tensor(nmp[:, 2, :], nmT[:], nmp[:, 1, :], ALU.subtract).then_inc(max_step, 1)

            def normalise(i, u):
                g, par, s, qb, *_ = place(u)
                if s not in ends:
                    return
                n = g * NQ + qb
                if plain:
                    wait(dve, z_spread, i, 2 * NQ, n + 1)
                else:
                    wait(dve, weighed, i, PER, u + 1)
                dve.reciprocal(rz[:], m.ps[:, 7 if plain else 5, :]).then_inc(inverse, 1)
                wait(dve, inverse, i, 2 * NQ, n + 1)
                wait(dve, o_ready, i, 4 * NQ, 2 * n)
                dve.tensor_tensor(y[:], y_raw[:] if plain else m.ps[:, 4, :], rz[:], ALU.mult).then_inc(y_scaled, 1)

            def add(half):
                def run(i, u):
                    g, par, s, qb, *_ = place(u)
                    if s not in ends:
                        return
                    wait(dve, o_ready, i, 4 * NQ, 2 * (g * NQ + qb) + half + 1)
                    b = (i * 2 + g) // GB if isinstance(i, int) else (i + g // 2) // 2
                    rows_x = m.x[:, ds(b * BT + (qb * 4 + 2 * half), 2), :]
                    dve.tensor_tensor(rows_x, rows_x, m.ps[:, 7 if plain else 6 + half, :]
                                      .rearrange("p (t c) -> p t c", c=C), ALU.add).then_inc(o_added, 1)
                return run

            if plain:
                pipelined(dve, [(0, maxima), (18, normalise), (19, add(0)), (20, add(1)), (0, split_maxima)],
                          PER, ITERS, lead=23)
            else:
                pipelined(dve, [(2, normalise), (3, add(0)), (4, add(1))], PER, ITERS)
    ph.close()


def in_blocks(e, n, body):
    body(0)
    with e.Fori(1, n) as i:
        body(i)


def wait_from(e, sem, i, each, k=0):
    assert k >= 0
    if not isinstance(i, int) or i * each + k > 0:
        e.wait_ge(sem, i * each + k)


def relu_ffn(nc, m, tag, w1_d, b1_d, w2_d, b2_d, w3_d, b3_d):
    ph = Phase(nc, tag)
    H = 512
    HT = H // P
    w1 = ph.sb("w1", [P, KC, H])
    w2 = ph.sb("w2", [P, HT, H])
    w3 = ph.sb("w3", [P, HT, C])
    b1 = ph.sb("b1", [P, HT])
    b2 = ph.sb("b2", [P, HT])
    b3 = ph.sb("b3", [P, C])
    h1 = ph.sb("h1", [P, HT, QB])
    h2 = ph.sb("h2", [P, HT, QB])
    loaded, b3_added = ph.sem("loaded"), ph.sem("b3_added")
    p1, p2, p3 = ph.sem("p1"), ph.sem("p2"), ph.sem("p3")
    r1, r2, added = ph.sem("r1"), ph.sem("r2"), ph.sem("added")
    NB = TOK // QB
    with nc.Block() as block:
        @block.sync
        def _(sp):
            sp.dma_start(w1[:], w1_d.rearrange("(k p) n -> p k n", p=P)).then_inc(loaded, 16)
            sp.dma_start(w2[:], w2_d.rearrange("(k p) n -> p k n", p=P)).then_inc(loaded, 16)
            sp.dma_start(w3[:], w3_d.rearrange("(k p) n -> p k n", p=P)).then_inc(loaded, 16)
            sp.dma_start(b1[:], b1_d).then_inc(loaded, 16)
            sp.dma_start(b2[:], b2_d).then_inc(loaded, 16)
            sp.dma_start(b3[:], b3_d.partition_broadcast(P)).then_inc(loaded, 16)

        @block.gpsimd
        def _(pool):
            pool.wait_ge(loaded, 96)
            for t in range(TILES):
                pool.tensor_tensor(m.x[:, t, :], m.x[:, t, :], b3[:], ALU.add).then_inc(b3_added, 1)

        @block.tensor
        def _(pe):
            pe.wait_ge(loaded, 96)
            def block_of(i):
                for o in range(HT):
                    wait_from(pe, r1, i, HT)
                    for k in range(KC):
                        last = pe.matmul(m.ps[:, o, :], w1[:, k, o * P:(o + 1) * P], m.xnT[:, k, ds(i * QB, QB)],
                                         start=(k == 0), stop=(k == KC - 1))
                    last.then_inc(p1, 1)
                for o in range(HT):
                    wait_from(pe, added, i, HT)
                    for k in range(HT):
                        if o == 0:
                            wait_from(pe, r1, i, HT, k + 1)
                        last = pe.matmul(m.ps[:, 4 + o, :], w2[:, k, o * P:(o + 1) * P], h1[:, k, :],
                                         start=(k == 0), stop=(k == HT - 1))
                    last.then_inc(p2, 1)
                wait_from(pe, r2, i, HT, HT)
                for t in range(HT):
                    for k in range(HT):
                        last = pe.matmul(m.ps[:, 4 + t, 0:C], h2[:, k, t * P:(t + 1) * P], w3[:, k, :],
                                         start=(k == 0), stop=(k == HT - 1))
                    last.then_inc(p3, 1)

            in_blocks(pe, NB, block_of)

        @block.scalar
        def _(act):
            act.wait_ge(loaded, 96)
            def block_of(i):
                for o in range(HT):
                    wait_from(act, p1, i, HT, o + 1)
                    if o == 0:
                        wait_from(act, p2, i, HT)
                    act.activation(h1[:, o, :], m.ps[:, o, :], ACT.Relu, bias=b1[:, o:o + 1]).then_inc(r1, 1)
                for o in range(HT):
                    wait_from(act, p2, i, HT, o + 1)
                    if o == 0:
                        wait_from(act, p3, i, HT)
                    act.activation(h2[:, o, :], m.ps[:, 4 + o, :], ACT.Relu, bias=b2[:, o:o + 1]).then_inc(r2, 1)

            in_blocks(act, NB, block_of)

        @block.vector
        def _(dve):
            dve.wait_ge(b3_added, TILES)
            def block_of(i):
                for t in range(HT):
                    wait_from(dve, p3, i, HT, t + 1)
                    row = m.x[:, ds(i * HT + t, 1), :]
                    dve.tensor_tensor(row, row, m.ps[:, 4 + t:5 + t, 0:C], ALU.add).then_inc(added, 1)

            in_blocks(dve, NB, block_of)
    ph.close()


MLP = 2048


def dequantise(nc, m, a):
    ph = Phase(nc, "dq")
    packed = ph.sb("packed", [P, 3, MLP], I32)
    scale = ph.sb("scale", [P, 3, MLP])
    code = ph.sb("code", [P, MLP], I32)
    sign = ph.sb("sign", [P, MLP], I32)
    val = ph.sb("val", [P, MLP])
    half = ph.sb("half", [P, MLP])
    loaded, step = ph.sem("loaded"), ph.sem("step")
    with nc.Block() as block:
        @block.sync
        def _(sp):
            sp.dma_start(packed[:, 0, :], a["gate_p"]).then_inc(loaded, 16)
            sp.dma_start(packed[:, 1, :], a["up_p"]).then_inc(loaded, 16)
            sp.dma_start(packed[:, 2, :].rearrange("p (m h) -> p m h", m=8),
                         a["down_p"].rearrange("(m p) h -> p m h", p=P)).then_inc(loaded, 16)
            for k in range(8):
                rows = slice(16 * k, 16 * k + 16)
                sp.dma_start(scale[rows, 0, :], a["gate_s"][k].partition_broadcast(16)).then_inc(loaded, 16)
                sp.dma_start(scale[rows, 1, :], a["up_s"][k].partition_broadcast(16)).then_inc(loaded, 16)
                sp.dma_start(scale[rows, 2, :], a["down_s"][k].partition_broadcast(16)).then_inc(loaded, 16)

        @block.vector
        def _(dve):
            dve.wait_ge(loaded, 16 * 27)
            n = 0
            for w in range(3):
                for odd in range(2):
                    dst = (m.wg, m.wu, m.wd)[w][:, odd, :]
                    sh = 4 * odd
                    dve.wait_ge(step, n) if n else None
                    dve.tensor_scalar(code[:], packed[:, w, :], sh, 7, ALU.logical_shift_right,
                                      ALU.bitwise_and).then_inc(step, 1)
                    dve.tensor_scalar(sign[:], packed[:, w, :], sh, 8, ALU.logical_shift_right,
                                      ALU.bitwise_and).then_inc(step, 1)
                    dve.wait_ge(step, n + 2)
                    dve.scalar_tensor_tensor(val[:], code[:], 4.0, code[:], ALU.max, ALU.add).then_inc(step, 1)
                    dve.tensor_scalar(half[:], sign[:], -0.125, 0.5, ALU.mult, ALU.add).then_inc(step, 1)
                    dve.wait_ge(step, n + 4)
                    dve.scalar_tensor_tensor(val[:], code[:], 6.0, val[:], ALU.max, ALU.add).then_inc(step, 1)
                    dve.wait_ge(step, n + 5)
                    dve.scalar_tensor_tensor(val[:], code[:], 6.0, val[:], ALU.max, ALU.add).then_inc(step, 1)
                    dve.wait_ge(step, n + 6)
                    dve.scalar_tensor_tensor(val[:], val[:], -16.0, half[:], ALU.add, ALU.mult).then_inc(step, 1)
                    dve.wait_ge(step, n + 7)
                    dve.tensor_tensor(dst, val[:], scale[:, w, :], ALU.mult).then_inc(step, 1)
                    n += 8
    ph.close()


def gated_ffn(nc, m, tag):
    ph = Phase(nc, tag)
    NT, NB = MLP // P, TOK // QB
    ge = ph.sb("ge", [P, 2, QB])
    it = ph.sb("it", [P, 2, QB])
    gate, up, gelued, gated, down, added = (ph.sem("gate"), ph.sem("up"), ph.sem("gelued"), ph.sem("gated"),
                                            ph.sem("down"), ph.sem("added"))
    with nc.Block() as block:
        @block.tensor
        def _(pe):
            def first(i, n):
                cols = slice(n * P, (n + 1) * P)
                wait_from(pe, gated, i, NT, max(n - 1, 0))
                for w, bank, done in ((m.wg, 0, gate), (m.wu, 2, up)):
                    for k in range(2):
                        last = pe.matmul(m.ps[:, bank + n % 2, :], w[:, k, cols], m.xnT[:, k, ds(i * QB, QB)],
                                         start=(k == 0), stop=(k == 1))
                    last.then_inc(done, 1)

            def second(i, n):
                wait_from(pe, gated, i, NT, n + 1)
                if n == 0:
                    wait_from(pe, added, i, 4)
                for t in range(4):
                    last = pe.matmul(m.ps[:, 4 + t, 0:C], it[:, n % 2, t * P:(t + 1) * P],
                                     m.wd[:, n % 2, (n // 2) * C:(n // 2 + 1) * C],
                                     start=(n == 0), stop=(n == NT - 1))
                last.then_inc(down, 1)

            def block_of(i):
                first(i, 0)
                for n in range(NT):
                    if n + 1 < NT:
                        first(i, n + 1)
                    second(i, n)

            in_blocks(pe, NB, block_of)

        @block.scalar
        def _(act):
            def block_of(i):
                for n in range(NT):
                    wait_from(act, gate, i, NT, n + 1)
                    if n >= 2:
                        wait_from(act, gated, i, NT, n - 1)
                    act.activation(ge[:, n % 2, :], m.ps[:, n % 2, :], ACT.Gelu_apprx_tanh).then_inc(gelued, 1)

            in_blocks(act, NB, block_of)

        @block.vector
        def _(dve):
            def block_of(i):
                for n in range(NT):
                    wait_from(dve, gelued, i, NT, n + 1)
                    wait_from(dve, up, i, NT, n + 1)
                    if n >= 2:
                        wait_from(dve, down, i, NT, n - 1)
                    dve.tensor_tensor(it[:, n % 2, :], ge[:, n % 2, :], m.ps[:, 2 + n % 2, :],
                                      ALU.mult).then_inc(gated, 1)
                wait_from(dve, down, i, NT, NT)
                x_block = m.x[:, ds(i * 4, 4), :]
                dve.tensor_tensor(x_block, x_block, m.ps[:, 4:8, 0:C], ALU.add).then_inc(added, 4)

            in_blocks(dve, NB, block_of)
    ph.close()


def diff_attention(nc, m, a, tag, scr, v_sb):
    ph = Phase(nc, tag)
    HD, U = 16, HG * BT
    PER, ITERS = 2 * U, GB
    q_st = ph.sb("q_st", [96, 2, 2 * HG, T], BF16)
    k_st = ph.sb("k_st", [96, 2, 2, T], BF16)
    v_st = ph.sb("v_st", [P, 2, BT, HD])
    lv = ph.sb("lv", [P, 4, 256])
    dots = ph.sb("dots", [P, 2, 16])
    nlam = ph.sb("nlam", [P, 16])
    nm = ph.sb("nm", [P, 4, 2])
    e = ph.sb("e", [P, 4, 2, T])
    z = ph.sb("z", [P, 4, 2])
    rz = ph.sb("rz", [P, 4, 2])
    c = ph.sb("c", [P, 4])
    t2 = ph.sb("t2", [P, 2, T])
    low = ph.sb("low", [P, 4])
    z2 = ph.sb("z2", [P, 4])
    rz2 = ph.sb("rz2", [P, 4])
    pr = ph.sb("pr", [P, 2, T])
    prT = ph.sb("prT", [P, 2, T])
    lam_loaded, lam_step = ph.sem("lam_loaded"), ph.sem("lam_step")
    staged = [ph.sem("staged0"), ph.sem("staged1")]
    scored, maxed, exped, masked = ph.sem("scored"), ph.sem("maxed"), ph.sem("exped"), ph.sem("masked")
    inv, coef, mixed, lowered = ph.sem("inv"), ph.sem("coef"), ph.sem("mixed"), ph.sem("lowered")
    p_done, turned, copied, valued = ph.sem("p_done"), ph.sem("turned"), ph.sem("copied"), ph.sem("valued")
    inv2, scaled, mixable = ph.sem("inv2"), ph.sem("scaled"), ph.sem("mixable")

    def place(u):
        b, h, t = (u // U) % 2, (u // BT) % HG, u % BT
        return b, h, t, (t + 1) * P

    with nc.Block() as block:
        @block.sync
        def _(sp):
            for n, name in enumerate(("lq1", "lk1", "lq2", "lk2")):
                sp.dma_start(lv[:, n, :], a[name].partition_broadcast(P)).then_inc(lam_loaded, 16)
            for g in range(2 * GB):
                if g >= 2:
                    sp.wait_ge(valued, U * (g - 1))
                j, b = g // 2, g % 2
                tok = slice(b * T, (b + 1) * T)
                for n in range(6):
                    sp.dma_start(q_st[n * HD:(n + 1) * HD, b, :, :],
                                 scr[Q_PARTS[n], j * 128:(j + 1) * 128, tok]
                                 .rearrange("(h d) t -> d h t", d=HD)).then_inc(staged[b], 16)
                    sp.dma_start(k_st[n * HD:(n + 1) * HD, b, :, :],
                                 scr[K_PARTS[n], 512 + j * 32:512 + (j + 1) * 32, tok]
                                 .rearrange("(h d) t -> d h t", d=HD)).then_inc(staged[b], 16)
                sp.dma_start(v_st[:, b, :, :], v_sb[:, b * BT:(b + 1) * BT, j, :]).then_inc(staged[b], 16)

        @block.tensor
        def _(pe):
            def score(i, u):
                b, h, t, L = place(u)
                if u % U == 0:
                    pe.wait_ge(staged[b], (i + u // PER) * (16 * 13) + 16 * 13)
                short = t < 4
                wait(pe, exped, i, 2 * PER, 2 * u - (2 if short and t else 0))
                for s in range(2):
                    for cc in range(t // 4 + 1):
                        bank = 2 * (t % 2) + s if short else 2 * s + cc
                        n = min(QB, L - cc * QB)
                        diag = cc == t // 4
                        pe.matmul(m.ps[:, bank, 0:n], q_st[:, b, 2 * h + s, t * P:(t + 1) * P],
                                  k_st[:, b, s, cc * QB:cc * QB + n], start=True, stop=True)
                        if diag:
                            last = pe.matmul(m.ps[:, bank, n - P:n], m.ident_b[:], m.later_k[:],
                                             start=False, stop=True, skip_group_check=True)
                last.then_inc(scored, 1)

            def turn(i, u):
                b, h, t, L = place(u)
                wait(pe, p_done, i, PER, u + 1)
                wait(pe, copied, i, PER, u - (1 if 1 <= t < 4 else 0))
                for kb in range(t + 1):
                    bank = 4 + (t % 2 if t < 4 else kb // 4)
                    last = pe.transpose(m.ps[:, bank, (kb % 4) * P:(kb % 4 + 1) * P],
                                        pr[:, u % 2, kb * P:(kb + 1) * P], m.ident[:])
                last.then_inc(turned, 1)

            def value(i, u):
                b, h, t, L = place(u)
                wait(pe, copied, i, PER, u + 1)
                wait(pe, scaled, i, PER, u - 1)
                for kb in range(t + 1):
                    last = pe.matmul(m.ps[:, 6 + u % 2, 0:HD], prT[:, u % 2, kb * P:(kb + 1) * P],
                                     v_st[:, b, kb, :], start=(kb == 0), stop=(kb == t))
                last.then_inc(valued, 1)

            pipelined(pe, [(0, score), (2, turn), (3, value)], PER, ITERS)

        @block.scalar
        def _(act):
            act.wait_ge(lam_step, 2)
            act.activation(dots[:], dots[:], ACT.Exp).then_inc(lam_step, 1)

            def exps(i, u):
                b, h, t, L = place(u)
                wait(act, maxed, i, PER, u + 1)
                wait(act, lowered, i, PER, u - 3)
                for s in range(2):
                    bank = 2 * (t % 2) + s if t < 4 else 2 * s
                    src = m.ps[:, bank, 0:L] if t < 4 else m.ps[:, bank:bank + 2, :].rearrange("p a n -> p (a n)")[:, 0:L]
                    act.activation(e[:, u % 4, s, 0:L], src, ACT.Exp, bias=nm[:, u % 4, s:s + 1],
                                   accum_out=z[:, u % 4, s:s + 1]).then_inc(exped, 1)

            def softmax(i, u):
                b, h, t, L = place(u)
                wait(act, lowered, i, PER, u + 1)
                wait(act, turned, i, PER, u - 1)
                act.activation(pr[:, u % 2, 0:L], t2[:, u % 2, 0:L], ACT.Exp, bias=low[:, u % 4:u % 4 + 1], scale=-1.0,
                               accum_out=z2[:, u % 4:u % 4 + 1]).then_inc(p_done, 1)

            def copy(i, u):
                b, h, t, L = place(u)
                wait(act, turned, i, PER, u + 1)
                wait(act, valued, i, PER, u - 1)
                bank = 4 + (t % 2 if t < 4 else 0)
                src = m.ps[:, bank, 0:L] if t < 4 else m.ps[:, bank:bank + 2, :].rearrange("p a n -> p (a n)")[:, 0:L]
                act.copy(prT[:, u % 2, 0:L], src).then_inc(copied, 1)

            pipelined(act, [(0, exps), (1, softmax), (2, copy)], PER, ITERS)

        @block.gpsimd
        def _(pool):
            def mask(i, u):
                b, h, t, L = place(u)
                wait(pool, exped, i, 2 * PER, 2 * u + 2)
                tile = e[:, u % 4, 0, t * P:L]
                pool.tensor_tensor(tile, tile, m.later_k[:], ALU.add).then_inc(masked, 1)

            pipelined(pool, [(0, mask)], PER, ITERS)

        @block.vector
        def _(dve):
            dve.wait_ge(lam_loaded, 64)
            dve.tensor_tensor(lv[:, 0, :], lv[:, 0, :], lv[:, 1, :], ALU.mult).then_inc(lam_step, 0 + 1)
            dve.tensor_tensor(lv[:, 2, :], lv[:, 2, :], lv[:, 3, :], ALU.mult).then_inc(inv, 1)
            dve.wait_ge(lam_step, 1)
            dve.wait_ge(inv, 1)
            dve.tensor_reduce(dots[:], lv[:, 0:4:2, :].rearrange("p n (h d) -> p n h d", d=HD), AX.X,
                              ALU.add).then_inc(lam_step, 1)
            dve.wait_ge(lam_step, 3)
            dve.tensor_tensor(nlam[:], dots[:, 1, :], dots[:, 0, :], ALU.subtract).then_inc(lam_step, 1)
            dve.wait_ge(lam_step, 4)
            dve.tensor_scalar(nlam[:], nlam[:], float(0.8 - 0.6 * float(np.exp(-0.3 * 0))), None,
                              ALU.subtract).then_inc(lam_step, 1)
            dve.wait_ge(lam_step, 5)

            def maxima(i, u):
                b, h, t, L = place(u)
                wait(dve, scored, i, PER, u + 1)
                if t < 4:
                    src = m.ps[:, 2 * (t % 2):2 * (t % 2) + 2, 0:L]
                else:
                    src = m.ps[:, 0:4, :].rearrange("p (s a) n -> p s (a n)", s=2)[:, :, 0:L]
                dve.tensor_reduce(nm[:, u % 4, :], src, AX.X, ALU.max, negate=True).then_inc(maxed, 1)

            def mix(i, u):
                b, h, t, L = place(u)
                hh = i * HG + (h + HG * (u // PER))
                k = u % 4
                er = u % 4
                wait(dve, exped, i, 2 * PER, 2 * u + 2)
                dve.reciprocal(rz[:, k, :], z[:, k, :]).then_inc(inv, 1)
                wait(dve, inv, i, PER, u + 2)
                dve.scalar_tensor_tensor(c[:, k:k + 1], rz[:, k, 1:2], nlam[:, ds(hh, 1)], z[:, k, 0:1],
                                         ALU.mult, ALU.mult).then_inc(coef, 1)
                dve.tensor_scalar(rz[:, k, 0:1], rz[:, k, 0:1], -1.0, None, ALU.mult).then_inc(coef, 1)
                wait(dve, coef, i, 2 * PER, 2 * u + 1)
                dve.tensor_scalar(e[:, er, 1, 0:L], e[:, er, 1, 0:L], c[:, k:k + 1], None, ALU.mult).then_inc(mixed, 1)
                wait(dve, mixed, i, PER, u + 1)
                wait(dve, coef, i, 2 * PER, 2 * u + 2)
                wait(dve, masked, i, PER, u + 1)
                wait(dve, p_done, i, PER, u - 1)
                dve.sem_inc(mixable, 1)
                dve.tensor_tensor_reduce(t2[:, u % 2, 0:L], e[:, er, 0, 0:L], e[:, er, 1, 0:L], rz[:, k, 0:1], 3.0e38,
                                         ALU.add, ALU.min, low[:, k:k + 1]).then_inc(lowered, 1)

            def result(i, u):
                b, h, t, L = place(u)
                k = u % 4
                wait(dve, p_done, i, PER, u + 1)
                dve.reciprocal(rz2[:, k:k + 1], z2[:, k:k + 1]).then_inc(inv2, 1)
                wait(dve, inv2, i, PER, u + 1)
                wait(dve, valued, i, PER, u + 1)
                hh = i * HG + (h + HG * (u // PER))
                dve.tensor_scalar(m.y_tok[:, b * BT + t, ds(hh * HD, HD)], m.ps[:, 6 + u % 2, 0:HD],
                                  rz2[:, k:k + 1], None, ALU.mult).then_inc(scaled, 1)

            pipelined(dve, [(0, maxima), (1, mix), (3, result)], PER, ITERS)
    ph.close()


def norm_project(nc, m, tag, w_d, g_d, eps, factor):
    ph = Phase(nc, tag)
    w = ph.sb("w", [P, KC, C])
    g = ph.sb("g", [P, C])
    sq = ph.sb("sq", [P, TILES, C])
    ms = ph.sb("ms", [P, TILES, 16])
    yT = ph.sb("yT", [P, 2, C])
    loaded, step, root = ph.sem("loaded"), ph.sem("step"), ph.sem("root")
    turned, copied, product, added = ph.sem("turned"), ph.sem("copied"), ph.sem("product"), ph.sem("added")
    with nc.Block() as block:
        @block.sync
        def _(sp):
            sp.dma_start(w[:], w_d.rearrange("(k p) n -> p k n", p=P)).then_inc(loaded, 16)
            sp.dma_start(g[:], g_d.partition_broadcast(P)).then_inc(loaded, 16)

        @block.vector
        def _(dve):
            y = m.y_tok
            dve.tensor_tensor(sq[:], y[:], y[:], ALU.mult).then_inc(step, 1)
            dve.wait_ge(step, 1)
            dve.tensor_reduce(ms[:], sq[:].rearrange("p t (h d) -> p t h d", d=16), AX.X, ALU.add).then_inc(step, 1)
            dve.wait_ge(step, 2)
            dve.tensor_scalar(ms[:], ms[:], 1.0 / 16, eps, ALU.mult, ALU.add).then_inc(step, 1)
            dve.wait_ge(root, 1)
            dve.reciprocal(ms[:], ms[:]).then_inc(step, 1)
            dve.wait_ge(step, 4)
            dve.wait_ge(loaded, 32)
            for t in range(TILES):
                dve.scalar_tensor_tensor(sq[:, t, :], y[:, t, :], factor, g[:], ALU.mult, ALU.mult).then_inc(step, 1)
                dve.wait_ge(step, 5 + 2 * t)
                yt = sq[:, t, :].rearrange("p (h d) -> p h d", d=16)
                dve.tensor_tensor(yt, yt, ms[:, t, :, None].to_broadcast([P, 16, 16]), ALU.mult).then_inc(step, 1)
                if t >= 1:
                    dve.wait_ge(product, t)
                    dve.tensor_tensor(m.x[:, t - 1, :], m.x[:, t - 1, :], m.ps[:, 2 + (t - 1) % 2, 0:C],
                                      ALU.add).then_inc(added, 1)
            dve.wait_ge(product, TILES)
            dve.tensor_tensor(m.x[:, TILES - 1, :], m.x[:, TILES - 1, :], m.ps[:, 2 + (TILES - 1) % 2, 0:C], ALU.add)

        @block.scalar
        def _(act):
            act.wait_ge(step, 3)
            act.activation(ms[:], ms[:], ACT.Sqrt).then_inc(root, 1)
            for t in range(TILES):
                act.wait_ge(turned, t + 1)
                if t >= 2:
                    act.wait_ge(product, t - 1)
                act.copy(yT[:, t % 2, :], m.ps[:, t % 2, 0:C]).then_inc(copied, 1)

        @block.tensor
        def _(pe):
            pe.wait_ge(loaded, 32)

            def turn(t):
                pe.wait_ge(step, 6 + 2 * t)
                if t >= 2:
                    pe.wait_ge(copied, t - 1)
                for k in range(KC):
                    last = pe.transpose(m.ps[:, t % 2, k * P:(k + 1) * P], sq[:, t, k * P:(k + 1) * P], m.ident[:])
                last.then_inc(turned, 1)

            turn(0)
            for t in range(TILES):
                if t + 1 < TILES:
                    turn(t + 1)
                pe.wait_ge(copied, t + 1)
                if t >= 2:
                    pe.wait_ge(added, t - 1)
                for k in range(KC):
                    last = pe.matmul(m.ps[:, 2 + t % 2, 0:C], yT[:, t % 2, k * P:(k + 1) * P], w[:, k, :],
                                     start=(k == 0), stop=(k == KC - 1))
                last.then_inc(product, 1)
    ph.close()


CH = 16
NCH = T // CH
NG = 4
HL = 8


def ttt_project(nc, m, a, tag):
    ph = Phase(nc, tag)
    w = ph.sb("w", [P, KC, 3 * C + 16])
    wg1 = ph.sb("wg1", [P, KC, 16])
    wg2 = ph.sb("wg2", [16, C])
    g1T = ph.sb("g1T", [16, TOK])
    k = ph.sb("k", [P, TILES, 16, CH + 1])
    k_flat = ph.sb("k_flat", [P, TILES, C])
    v = ph.sb("v", [P, TILES, C])
    sq = ph.sb("sq", [P, C])
    kn = ph.sb("kn", [P, TILES, 16])
    lw = ph.sb("lw", [P, 2, C])
    loaded, g1, g1_copied = ph.sem("loaded"), ph.sem("g1"), ph.sem("g1_copied")
    product, read_a, read_d = ph.sem("product"), ph.sem("read_a"), ph.sem("read_d")
    norm, root, keyed, acts = ph.sem("norm"), ph.sem("root"), ph.sem("keyed"), ph.sem("acts")
    target, turned, copied, stored = ph.sem("target"), ph.sem("turned"), ph.sem("copied"), ph.sem("stored")
    qT, kT = m.xnT, m.kT
    with nc.Block() as block:
        @block.sync
        def _(sp):
            sp.dma_start(w[:], a["w_t"].rearrange("(k p) n -> p k n", p=P)).then_inc(loaded, 16)
            sp.dma_start(wg1[:], a["wg1"].rearrange("(k p) n -> p k n", p=P)).then_inc(loaded, 16)
            sp.dma_start(wg2[:], a["wg2"]).then_inc(loaded, 16)
            sp.dma_start(lw[:, 0, :], a["ln_w"].partition_broadcast(P)).then_inc(loaded, 16)
            sp.dma_start(lw[:, 1, :], a["ln_b"].partition_broadcast(P)).then_inc(loaded, 16)
            sp.wait_ge(acts, 3)
            sp.wait_ge(keyed, 1)
            sp.dma_start(a["scr_k"].rearrange("(t p) n -> p t n", p=P), k[:].rearrange("p t h d -> p t (h d)")).then_inc(stored, 16)
            sp.wait_ge(target, 2 * TILES)
            sp.dma_start(a["scr_t"].rearrange("(t p) n -> p t n", p=P), v[:]).then_inc(stored, 16)
            sp.wait_ge(stored, 32)

        @block.tensor
        def _(pe):
            pe.wait_ge(loaded, 80)
            for n in range(4):
                for c in range(KC):
                    last = pe.matmul(m.ps[0:16, n, :], wg1[:, c, :], m.xnT[:, c, n * QB:(n + 1) * QB],
                                     start=(c == 0), stop=(c == KC - 1))
            last.then_inc(g1, 1)
            pe.wait_ge(g1_copied, 1)
            for t in range(TILES):
                s = 4 * (t % 2)
                if t >= 2:
                    pe.wait_ge(read_a, 2 * (t - 1))
                    pe.wait_ge(read_d, t - 1)
                for bank, col, n in ((0, 0, C), (1, C, 2 * C), (2, 3 * C, 16)):
                    for c in range(KC):
                        pe.matmul(m.ps[:, s + bank, 0:n], m.xnT[:, c, t * P:(t + 1) * P], w[:, c, col:col + n],
                                  start=(c == 0), stop=(c == KC - 1))
                pe.matmul(m.ps[:, s, C:2 * C], g1T[:, t * P:(t + 1) * P], wg2[:], start=True, stop=True).then_inc(product, 1)
            pe.wait_ge(acts, 1)
            pe.wait_ge(keyed, 1)
            n = 0
            for src in (m.q_tok, k_flat):
                for c in range(KC):
                    for q in range(4):
                        if n >= 8:
                            pe.wait_ge(copied, n - 7)
                        else:
                            pe.wait_ge(read_a, 2 * TILES)
                            pe.wait_ge(read_d, TILES)
                        for t in range(4):
                            last = pe.transpose(m.ps[:, n % 8, t * P:(t + 1) * P],
                                                src[:, 4 * q + t, c * P:(c + 1) * P], m.ident[:])
                        last.then_inc(turned, 1)
                        n += 1

        @block.scalar
        def _(act):
            act.wait_ge(g1, 1)
            act.copy(g1T[:].rearrange("p (n t) -> p n t", n=4), m.ps[0:16, 0:4, :]).then_inc(g1_copied, 1)
            for t in range(TILES):
                s = 4 * (t % 2)
                act.wait_ge(product, t + 1)
                act.copy(m.q_tok[:, t, :], m.ps[:, s, 0:C]).then_inc(read_a, 1)
                act.copy(m.gate[:, t, :], m.ps[:, s, C:2 * C]).then_inc(read_a, 1)
            act.wait_ge(read_a, 2 * TILES)
            act.activation(m.q_tok[:], m.q_tok[:], ACT.Silu).then_inc(acts, 1)
            act.activation(m.gate[:], m.gate[:], ACT.Sigmoid).then_inc(acts, 1)
            act.wait_ge(read_d, TILES)
            act.activation(k[:, :, :, CH], k[:, :, :, CH], ACT.Sigmoid).then_inc(acts, 1)
            act.wait_ge(norm, TILES + 1)
            act.activation(kn[:], kn[:], ACT.Sqrt).then_inc(root, 1)
            for n in range(16):
                act.wait_ge(turned, n + 1)
                c, q = (n // 4) % 2, n % 4
                dst = (qT if n < 8 else kT)[:, c, q * QB:(q + 1) * QB]
                act.copy(dst, m.ps[:, n % 8, :]).then_inc(copied, 1)

        @block.vector
        def _(dve):
            for t in range(TILES):
                s = 4 * (t % 2)
                dve.wait_ge(product, t + 1)
                dve.tensor_copy(k_flat[:, t, :], m.ps[:, s + 1, 0:C])
                dve.tensor_copy(v[:, t, :], m.ps[:, s + 1, C:2 * C])
                dve.tensor_copy(k[:, t, :, CH], m.ps[:, s + 2, 0:16]).then_inc(read_d, 1)
                dve.wait_ge(read_d, t + 1)
                dve.tensor_tensor(sq[:], k_flat[:, t, :], k_flat[:, t, :], ALU.mult).then_inc(target, 1)
                dve.wait_ge(target, t + 1)
                dve.tensor_reduce(kn[:, t, :], sq[:].rearrange("p (h d) -> p h d", d=CH), AX.X, ALU.add).then_inc(norm, 1)
            dve.wait_ge(norm, TILES)
            dve.tensor_scalar(kn[:], kn[:], 1e-6, None, ALU.add).then_inc(norm, 1)
            dve.wait_ge(root, 1)
            dve.reciprocal(kn[:], kn[:]).then_inc(norm, 1)
            dve.wait_ge(norm, TILES + 2)
            kf = k_flat[:].rearrange("p t (h d) -> p t h d", d=CH)
            bc = kn[:, :, :, None].to_broadcast([P, TILES, 16, CH])
            dve.tensor_tensor(kf, kf, bc, ALU.mult).then_inc(norm, 1)
            dve.wait_ge(norm, TILES + 3)
            dve.tensor_copy(k[:, :, :, 0:CH], kf).then_inc(keyed, 1)
            dve.wait_ge(acts, 3)
            dve.wait_ge(loaded, 80)
            for t in range(TILES):
                dve.tensor_tensor(v[:, t, :], k_flat[:, t, :], v[:, t, :], ALU.subtract).then_inc(read_d, 1)
                dve.wait_ge(read_d, TILES + 2 * t + 1)
                dve.tensor_tensor(v[:, t, :], v[:, t, :], lw[:, 1, :], ALU.add).then_inc(read_d, 1)
                dve.wait_ge(read_d, TILES + 2 * t + 2)
                dve.tensor_tensor(v[:, t, :], v[:, t, :], lw[:, 0, :], ALU.mult).then_inc(target, 1)
    ph.close()


def ttt_scan(nc, m, a, tag):
    ph = Phase(nc, tag)
    tb = ph.sb("tb", [P, NCH, NG, CH])
    kc = ph.sb("kc", [P, NCH, NG, CH + 1])
    qh = ph.sb("qh", [P, NCH, NG, CH])
    block_mask = ph.sb("block_mask", [P, P])
    tri = ph.sb("tri", [P, P])
    w2 = ph.sb("w2", [P, 2, CH])
    S = ph.sb("S", [P, NG, CH])
    kT_bd = ph.sb("kT_bd", [P, 2, NG, P])
    qT_bd = ph.sb("qT_bd", [P, 2, NG, P])
    k_bd = ph.sb("k_bd", [P, 2, NG, P])
    at = ph.sb("at", [P, 2, NG, P])
    s4 = lambda name: ph.sb(name, [P, NG])
    s64 = lambda name: ph.sb(name, [P, NG, CH])
    mu, var, root, rstd, rate, m1, m2 = (s4(x) for x in ("mu", "var", "root", "rstd", "rate", "m1", "m2"))
    cen, sq, hat, gw, pg, hm, vv, u = (s64(x) for x in ("cen", "sq", "hat", "gw", "pg", "hm", "vv", "u"))
    loaded, made = ph.sem("loaded"), ph.sem("made")
    bd_p, k_spread = ph.sem("bd_p"), ph.sem("k_spread")
    kh_ready, at_ready, at_done, qh_ready, qh_copied = (ph.sem("kh_ready"), ph.sem("at_ready"), ph.sem("at_done"),
                                                        ph.sem("qh_ready"), ph.sem("qh_copied"))
    var_ready, rooted, chain, u_ready, ds_ready, s_ready = (ph.sem("var_ready"), ph.sem("rooted"), ph.sem("chain"),
                                                            ph.sem("u_ready"), ph.sem("ds_ready"), ph.sem("s_ready"))
    stored = ph.sem("stored")
    qT, kT = m.xnT, m.kT
    LINKS, PER = 15, 8
    bc = lambda x: x[:, :, None].to_broadcast([P, NG, CH])

    with nc.Block() as block:
        @block.sync
        def _(sp):
            n = 0
            for b in range(B):
                for half in range(2):
                    g = 2 * b + half
                    for h in range(HL):
                        rows, hd = slice(h * CH, (h + 1) * CH), half * HL + h
                        tok = slice(b * T, (b + 1) * T)
                        sp.dma_start(tb[rows, :, g, :], a["scr_t"][tok, hd * CH:(hd + 1) * CH]
                                     .rearrange("(n c) e -> c n e", c=CH)).then_inc(loaded, 16)
                        sp.dma_start(kc[rows, :, g, :], a["scr_k"][tok, hd * (CH + 1):(hd + 1) * (CH + 1)]
                                     .rearrange("(n c) e -> c n e", c=CH)).then_inc(loaded, 16)
            sp.dma_start(w2[:], a["ln_w_rows"]).then_inc(loaded, 16)
            sp.wait_ge(qh_copied, NCH)
            for b in range(B):
                for half in range(2):
                    for h in range(HL):
                        rows, hd = slice(h * CH, (h + 1) * CH), half * HL + h
                        sp.dma_start(a["scr_q"][b * T:(b + 1) * T, hd * CH:(hd + 1) * CH]
                                     .rearrange("(n c) e -> c n e", c=CH), qh[rows, :, 2 * b + half, :]).then_inc(stored, 16)
            sp.wait_ge(stored, 16 * 32)

        @block.gpsimd
        def _(pool):
            pool.memset(block_mask[:], 1.0).then_inc(made, 1)
            pool.memset(tri[:], 1.0).then_inc(made, 1)
            pool.wait_ge(made, 2)
            bm = block_mask[:].rearrange("p (h c) -> p h c", c=CH)
            pool.affine_select(out=bm, in_=bm, compare_op=ALU.is_ge, fill=0.0, base=0,
                               pattern=[[-CH, HL], [0, CH]], channel_multiplier=1).then_inc(made, 1)
            pool.affine_select(out=tri[:], in_=tri[:], compare_op=ALU.is_ge, fill=0.0, base=0,
                               pattern=[[1, P]], channel_multiplier=-1).then_inc(made, 1)
            pool.wait_ge(made, 4)
            pool.affine_select(out=bm, in_=bm, compare_op=ALU.is_ge, fill=0.0, base=CH - 1,
                               pattern=[[CH, HL], [0, CH]], channel_multiplier=-1).then_inc(made, 1)
            pool.wait_ge(made, 5)

            def spread(i, n):
                wait(pool, qh_ready, i, PER, n - 1)
                for src, dst in ((kT, kT_bd), (qT, qT_bd)):
                    for b in range(B):
                        cols = src[:, :, ds(i * (PER * CH) + (b * T + n * CH), CH)][:, :, None, :].to_broadcast([P, 2, HL, CH])
                        pool.tensor_tensor(dst[:, n % 2, 2 * b:2 * b + 2, :].rearrange("p g (h c) -> p g h c", c=CH), cols,
                                           block_mask[:].rearrange("p (h c) -> p h c", c=CH)[:, None, :, :]
                                           .to_broadcast([P, 2, HL, CH]), ALU.mult).then_inc(bd_p, 1)

            pipelined(pool, [(0, spread)], PER, NCH // PER, lead=4)

        @block.tensor
        def _(pe):
            def early(i, n):
                wait(pe, bd_p, i, 4 * PER, 4 * n + 4)
                wait(pe, at_done, i, PER, n - 1)
                for g in range(NG):
                    last = pe.matmul(m.ps[:, 4 + n % 2, g * P:(g + 1) * P], kT_bd[:, n % 2, g, :],
                                     qT_bd[:, n % 2, g, :], start=True, stop=True)
                last.then_inc(at_ready, 1)

            def state(i, n):
                wait(pe, s_ready, i, PER, n + 1)
                for g in range(NG):
                    last = pe.matmul(m.ps[:, 0, g * CH:(g + 1) * CH], kT_bd[:, n % 2, g, :], S[:, g, :],
                                     start=True, stop=True)
                last.then_inc(kh_ready, 1)
                wait(pe, qh_copied, i, PER, n - 1)
                for g in range(NG):
                    pe.matmul(m.ps[:, 2 + n % 2, g * CH:(g + 1) * CH], qT_bd[:, n % 2, g, :], S[:, g, :],
                              start=(g == 0), stop=True, skip_group_check=True)

            def update(i, n):
                wait(pe, k_spread, i, PER, n + 1)
                wait(pe, u_ready, i, PER, n + 1)
                for g in range(NG):
                    last = pe.matmul(m.ps[:, 1, g * CH:(g + 1) * CH], k_bd[:, n % 2, g, :], u[:, g, :],
                                     start=True, stop=True)
                last.then_inc(ds_ready, 1)
                wait(pe, at_done, i, PER, n + 1)
                for g in range(NG):
                    last = pe.matmul(m.ps[:, 2 + n % 2, g * CH:(g + 1) * CH], at[:, n % 2, g, :], u[:, g, :],
                                     start=False, stop=True, skip_group_check=True)
                last.then_inc(qh_ready, 1)

            pipelined(pe, [(1, state), (0, early), (1, update)], PER, NCH // PER, lead=4)

        @block.scalar
        def _(act):
            def square_root(i, n):
                wait(act, var_ready, i, PER, n + 1)
                act.activation(root[:], var[:], ACT.Sqrt).then_inc(rooted, 1)

            def copy(i, n):
                wait(act, qh_ready, i, PER, n + 1)
                act.copy(qh[:, ds(i * PER + n, 1), :, :], m.ps[:, 2 + n % 2, 0:NG * CH]
                         .rearrange("p (o g e) -> p o g e", o=1, e=CH)).then_inc(qh_copied, 1)

            pipelined(act, [(0, square_root), (1, copy)], PER, NCH // PER, lead=4)

        @block.vector
        def _(dve):
            dve.memset(S[:], 0.0).then_inc(s_ready, 1)
            dve.wait_ge(made, 5)
            dve.wait_ge(loaded, 16 * 65)
            dve.tensor_scalar(kc[:, :, :, CH], kc[:, :, :, CH], -2.0, None, ALU.mult).then_inc(chain, 1)
            dve.tensor_tensor(w2[:], w2[:], w2[:], ALU.mult).then_inc(chain, 1)
            dve.wait_ge(chain, 2)
            FIRST = 2

            def done(i, n, k):
                wait(dve, chain, i, PER * LINKS, n * LINKS + k + FIRST)

            def variance(i, n):
                kh = m.ps[:, 0, 0:NG * CH].rearrange("p (g e) -> p g e", e=CH)
                wait(dve, kh_ready, i, PER, n + 1)
                dve.tensor_reduce(mu[:], kh, AX.X, ALU.add).then_inc(chain, 1)
                done(i, n, 1)
                dve.scalar_tensor_tensor(cen[:], bc(mu), -1.0 / CH, kh, ALU.mult, ALU.add).then_inc(chain, 1)
                done(i, n, 2)
                dve.tensor_tensor(sq[:], cen[:], cen[:], ALU.mult).then_inc(chain, 1)
                done(i, n, 3)
                dve.tensor_reduce(var[:], sq[:], AX.X, ALU.add).then_inc(chain, 1)
                done(i, n, 4)
                dve.tensor_scalar(var[:], var[:], 1.0 / CH, 1e-6, ALU.mult, ALU.add).then_inc(var_ready, 1)

            def spread_k(i, n):
                wait(dve, ds_ready, i, PER, n - 1)
                keys = kc[:, ds(i * PER + n, 1), :, 0:CH].rearrange("p o g d -> p (o g) d")[:, :, None, :]
                dve.tensor_tensor(k_bd[:, n % 2, :, :].rearrange("p g (h d) -> p g h d", d=CH),
                                  keys.to_broadcast([P, NG, HL, CH]),
                                  block_mask[:].rearrange("p (h d) -> p h d", d=CH)[:, None, :, :]
                                  .to_broadcast([P, NG, HL, CH]), ALU.mult).then_inc(k_spread, 1)

            def gradient(i, n):
                wait(dve, rooted, i, PER, n + 1)
                dve.reciprocal(rstd[:], root[:]).then_inc(chain, 1)
                done(i, n, 5)
                dve.tensor_tensor(hat[:], cen[:], bc(rstd), ALU.mult).then_inc(chain, 1)
                now = kc[:, ds(i * PER + n, 1), :, CH].rearrange("p o g -> p (o g)")
                dve.tensor_tensor(rate[:], rstd[:], now, ALU.mult).then_inc(chain, 1)
                done(i, n, 6)
                dve.tensor_tensor(gw[:].rearrange("p (b h) e -> p b h e", h=2),
                                  hat[:].rearrange("p (b h) e -> p b h e", h=2),
                                  w2[:, None, :, :].to_broadcast([P, B, 2, CH]), ALU.mult).then_inc(chain, 1)
                done(i, n, 8)
                dve.tensor_tensor(gw[:], gw[:], tb[:, ds(i * PER + n, 1), :, :].rearrange("p o g e -> p (o g) e"),
                                  ALU.add).then_inc(chain, 1)
                done(i, n, 9)
                dve.tensor_tensor(pg[:], gw[:], hat[:], ALU.mult).then_inc(chain, 1)
                dve.tensor_reduce(m1[:], gw[:], AX.X, ALU.add).then_inc(chain, 1)
                done(i, n, 10)
                dve.tensor_reduce(m2[:], pg[:], AX.X, ALU.add).then_inc(chain, 1)
                done(i, n, 12)
                dve.tensor_tensor(hm[:], hat[:], bc(m2), ALU.mult).then_inc(chain, 1)
                done(i, n, 13)
                dve.tensor_tensor(hm[:], hm[:], bc(m1), ALU.add).then_inc(chain, 1)
                done(i, n, 14)
                dve.scalar_tensor_tensor(vv[:], hm[:], -1.0 / CH, gw[:], ALU.mult, ALU.add).then_inc(chain, 1)
                done(i, n, 15)
                wait(dve, qh_ready, i, PER, n)
                dve.tensor_tensor(u[:], vv[:], bc(rate), ALU.mult).then_inc(u_ready, 1)

            def mask(i, n):
                wait(dve, at_ready, i, PER, n + 1)
                wait(dve, qh_ready, i, PER, n - 1)
                dve.tensor_tensor(at[:, n % 2, :, :], m.ps[:, 4 + n % 2, :].rearrange("p (g c) -> p g c", c=P),
                                  tri[:, None, :].to_broadcast([P, NG, P]), ALU.mult).then_inc(at_done, 1)

            def advance(i, n):
                wait(dve, ds_ready, i, PER, n + 1)
                dve.tensor_tensor(S[:], S[:], m.ps[:, 1, 0:NG * CH].rearrange("p (g e) -> p g e", e=CH),
                                  ALU.add).then_inc(s_ready, 1)

            pipelined(dve, [(1, variance), (0, spread_k), (1, gradient), (0, mask), (1, advance)],
                      PER, NCH // PER, lead=4)
    ph.close()


def ttt_output(nc, m, a, tag):
    ph = Phase(nc, tag)
    z = m.y_tok
    sq = ph.sb("sq", [P, TILES, C])
    lw = ph.sb("lw", [P, 2, C])
    mu = ph.sb("mu", [P, TILES, 16])
    var = ph.sb("var", [P, TILES, 16])
    loaded, step, root = ph.sem("loaded"), ph.sem("step"), ph.sem("root")
    heads = lambda t: t[:].rearrange("p t (h e) -> p t h e", e=CH)
    wide = lambda t: t[:, :, :, None].to_broadcast([P, TILES, 16, CH])
    with nc.Block() as block:
        @block.sync
        def _(sp):
            sp.dma_start(z[:], a["scr_q"].rearrange("(t p) n -> p t n", p=P)).then_inc(loaded, 16)
            sp.dma_start(lw[:, 0, :], a["ln_w"].partition_broadcast(P)).then_inc(loaded, 16)
            sp.dma_start(lw[:, 1, :], a["ln_b"].partition_broadcast(P)).then_inc(loaded, 16)

        @block.scalar
        def _(act):
            act.wait_ge(step, 6)
            act.activation(var[:], var[:], ACT.Sqrt).then_inc(root, 1)

        @block.vector
        def _(dve):
            n = [0]

            def then(ins):
                n[0] += 1
                ins.then_inc(step, 1)
                dve.wait_ge(step, n[0])

            dve.wait_ge(loaded, 48)
            then(dve.tensor_reduce(mu[:], heads(z), AX.X, ALU.add))
            then(dve.tensor_scalar(mu[:], mu[:], 1.0 / CH, None, ALU.mult))
            then(dve.tensor_tensor(heads(z), heads(z), wide(mu), ALU.subtract))
            then(dve.tensor_tensor(sq[:], z[:], z[:], ALU.mult))
            then(dve.tensor_reduce(var[:], heads(sq), AX.X, ALU.add))
            then(dve.tensor_scalar(var[:], var[:], 1.0 / CH, 1e-6, ALU.mult, ALU.add))
            dve.wait_ge(root, 1)
            then(dve.reciprocal(var[:], var[:]))
            then(dve.tensor_tensor(heads(z), heads(z), wide(var), ALU.mult))
            then(dve.tensor_tensor(z[:], z[:], lw[:, 0:1, :].to_broadcast([P, TILES, C]), ALU.mult))
            then(dve.tensor_tensor(z[:], z[:], lw[:, 1:2, :].to_broadcast([P, TILES, C]), ALU.add))
            then(dve.tensor_tensor(z[:], z[:], m.q_tok[:], ALU.add))
            then(dve.tensor_tensor(z[:], z[:], m.gate[:], ALU.mult))
    ph.close()


def store_x(nc, m, out_d):
    ph = Phase(nc, "store")
    stored = ph.sem("stored")
    with nc.Block() as block:
        @block.sync
        def _(sp):
            sp.dma_start(out_d.rearrange("b (t p) c -> p (b t) c", p=P), m.x[:]).then_inc(stored, 16)
            sp.wait_ge(stored, 16)
    ph.close()


class Memory:
    pass


def build_program(nc, a, out_d, limit=99):
    m = Memory()
    with ExitStack() as ctx:
        def sb(name, shape, dt=F32):
            return ctx.enter_context(nc.sbuf_tensor(name, shape, dt))

        m.x = sb("x", [P, TILES, C])
        m.xnT = sb("xnT", [P, KC, TOK])
        m.ident = sb("ident", [P, P])
        m.ident_b = sb("ident_b", [P, P], BF16)
        m.later_k = sb("later_k", [P, P], BF16)
        m.keep = sb("keep", [P, P])
        m.later_q = sb("later_q", [P, P], BF16)
        m.wg = sb("wg", [P, 2, MLP])
        m.wu = sb("wu", [P, 2, MLP])
        m.wd = sb("wd", [P, 2, MLP])
        m.ps = ctx.enter_context(nc.psum_tensor("ps", [P, 8, 512], F32))

        load_and_constants(nc, m, a["x"])
        stages = STAGES(nc, m, a)
        for n, s in enumerate(stages[:limit]):
            s()
        store_x(nc, m, out_d)


def STAGES(nc, m, a):
    def attn_softcap():
        norm_transpose(nc, m, "n1")
        with nc.sbuf_tensor("v_a", [P, TILES, 8, 32], F32) as v_sb:
            project_rope(nc, m, "pa", a["wqk_a"], 6, a["wv_a"], 8, 32, 32, a["cos_a"], a["sin_a"], a["scr_a"], v_sb)
            attention(nc, m, "aa", a["scr_a"], v_sb, a["wo_a"], 32, 2, 512, 256.0 ** -0.5, 50.0)

    def ffn(tag):
        norm_transpose(nc, m, tag + "n")
        relu_ffn(nc, m, tag, a["w1"], a["b1"], a["w2"], a["b2"], a["w3"], a["b3"])

    def attn_plain():
        norm_transpose(nc, m, "n3")
        with nc.sbuf_tensor("v_b", [P, TILES, 4, 32], F32) as v_sb:
            project_rope(nc, m, "pb", a["wqk_b"], 3, a["wv_b"], 4, 16, 32, a["cos_b"], a["sin_b"], a["scr_b"], v_sb)
            attention(nc, m, "ab", a["scr_b"], v_sb, a["wo_b"], 16, 1, 256, 0.25, None)

    def gated(tag):
        norm_transpose(nc, m, tag + "n", interleave=True)
        gated_ffn(nc, m, tag)

    def attn_diff():
        norm_transpose(nc, m, "n5")
        with nc.sbuf_tensor("y_tok", [P, TILES, C], F32) as m.y_tok:
            with nc.sbuf_tensor("v_d", [P, TILES, 4, 16], F32) as v_sb:
                project_rope(nc, m, "pd", a["wqk_d"], 5, a["wv_d"], 4, 16, 16, a["cos_d"], a["sin_d"], a["scr_d"], v_sb)
                diff_attention(nc, m, a, "ad", a["scr_d"], v_sb)
            norm_project(nc, m, "od", a["wo_d"], a["rms_d"], 1e-8, 1.0 - (0.8 - 0.6 * float(np.exp(-0.3 * 0))))

    def attn_ttt():
        norm_transpose(nc, m, "n7")
        with ExitStack() as st:
            sb = lambda name, shape: st.enter_context(nc.sbuf_tensor(name, shape, F32))
            m.q_tok, m.gate = sb("q_tok", [P, TILES, C]), sb("gate_t", [P, TILES, C])
            with nc.sbuf_tensor("kT_t", [P, KC, TOK], F32) as m.kT:
                ttt_project(nc, m, a, "pt")
                ttt_scan(nc, m, a, "st")
            m.y_tok = sb("y_tok2", [P, TILES, C])
            ttt_output(nc, m, a, "ot")
            norm_project(nc, m, "ow", a["wo_t"], a["norm_w"], 1e-6, 1.0)

    return [attn_softcap, lambda: ffn("f2"), attn_plain, lambda: ffn("f4"),
            attn_diff, lambda: (dequantise(nc, m, a), gated("g6")), attn_ttt, lambda: gated("g8")]


def rope_tables(hd, interleaved, factor=1.0):
    inv = (1.0 / np.float32(10000.0) ** (np.arange(0, hd, 2, dtype=np.float32) / np.float32(hd))).astype(np.float32)
    ang = np.arange(T, dtype=np.float32)[:, None] * inv[None, :]
    cos, sin = np.cos(ang).T, np.sin(ang).T
    if interleaved:
        cos, sin = np.repeat(cos, 2, 0), np.stack([-sin, sin], 1).reshape(hd, T)
    else:
        cos, sin = np.concatenate([cos, cos]), np.concatenate([-sin, sin])
    cos, sin = cos * np.float32(factor), sin * np.float32(factor)
    return (np.ascontiguousarray(np.tile(cos, (P // hd, 1)), np.float32),
            np.ascontiguousarray(np.tile(sin, (P // hd, 1)), np.float32))


def swap_halves(w, hd):
    n = w.shape[1]
    return w.reshape(-1, n // hd, 2, hd // 2)[:, :, ::-1].reshape(-1, n)


def lay_out(i):
    f = {k: np.asarray(v) for k, v in i.items()}
    cat = lambda *p: np.ascontiguousarray(np.concatenate(p, 1))
    d = {"x": f["L0_attn_a_X"]}
    q, k = f["L0_attn_a_Wq"], f["L0_attn_a_Wk"]
    d["wqk_a"] = cat(q, k, swap_halves(q, 32), swap_halves(k, 32))
    d["wv_a"], d["wo_a"] = f["L0_attn_a_Wv"], f["L0_attn_a_Wo"]
    d["cos_a"], d["sin_a"] = rope_tables(32, False)
    q, k = f["L0_attn_b_Wq"], f["L0_attn_b_Wk"]
    ks = swap_halves(k, 16)
    d["wqk_b"] = cat(q, k, k, swap_halves(q, 16), ks, ks)
    d["wv_b"] = f["L0_attn_b_Wv"]
    wo = np.zeros((16, 32, C), np.float32)
    wo[:, :16] = f["L0_attn_b_Wproj"].reshape(16, 16, C)
    d["wo_b"] = wo.reshape(512, C)
    d["cos_b"], d["sin_b"] = rope_tables(16, False)
    d["w1"], d["w2"], d["w3"] = (np.ascontiguousarray(f[f"L0_ffn_W{n}"].T) for n in (1, 2, 3))
    d["b1"], d["b2"] = (np.ascontiguousarray(f[f"L0_ffn_b{n}"].reshape(4, P).T) for n in (1, 2))
    d["b3"] = f["L0_ffn_b3"]
    q, k = f["L1_attn_a_Wq"], f["L1_attn_a_Wk"]
    d["wqk_d"] = cat(q, k, swap_halves(q, 2), swap_halves(k, 2))
    d["wv_d"], d["wo_d"] = f["L1_attn_a_Wv"], f["L1_attn_a_Wo"]
    d["cos_d"], d["sin_d"] = rope_tables(32, True, 0.5)
    d["lq1"], d["lk1"], d["lq2"], d["lk2"] = (f[f"L1_attn_a_{n}"].reshape(-1) for n in ("lq1", "lk1", "lq2", "lk2"))
    d["rms_d"] = np.tile(f["L1_attn_a_rms_w"], 16)

    w = [f[f"L1_attn_b_W{n}"] for n in ("q", "k", "v", "beta")]
    d["w_t"], d["wg1"], d["wg2"], d["wo_t"] = cat(*w), f["L1_attn_b_Wg1"], f["L1_attn_b_Wg2"], f["L1_attn_b_Wo"]
    ln_w = f["L1_attn_b_ln_w"]
    d["ln_w"], d["ln_b"], d["norm_w"] = ln_w.reshape(-1), f["L1_attn_b_ln_b"].reshape(-1), f["L1_attn_b_norm_w"]
    d["ln_w_rows"] = np.ascontiguousarray(np.repeat(ln_w.reshape(2, 8, 1, 16), 16, 2).reshape(2, P, 16).transpose(1, 0, 2))

    def hidden(p):
        return np.ascontiguousarray(p.T.reshape(-1, MLP // 256, P, 2).transpose(0, 1, 3, 2).reshape(-1, MLP))
    d["gate_p"], d["up_p"] = hidden(f["L1_ffn_gate_W_packed"]), hidden(f["L1_ffn_up_W_packed"])
    d["gate_s"], d["up_s"] = hidden(f["L1_ffn_gate_scales"]), hidden(f["L1_ffn_up_scales"])
    d["down_p"] = np.ascontiguousarray(f["L1_ffn_down_W_packed"].T)
    d["down_s"] = np.ascontiguousarray(f["L1_ffn_down_scales"].T.reshape(8, 8, C).transpose(1, 0, 2).reshape(8, MLP))
    return d


SCRATCH = {"scr_a": (3, 768, TOK), "scr_b": (3, 384, TOK), "scr_d": (3, 640, TOK)}
SCRATCH_F32 = {"scr_k": (TOK, 16 * 17), "scr_t": (TOK, C), "scr_q": (TOK, C)}


def kernel(**inputs):
    import concourse.bacc as bacc
    from concourse.bass_utils import run_bass_kernel_spmd

    nc = bacc.Bacc("TRN2", target_bir_lowering=False, num_devices=1)
    arrays = {f"in_{k}": v for k, v in lay_out(inputs).items()}
    a = {k[3:]: nc.dram_tensor(k, v.shape, mybir.dt.from_np(v.dtype), kind="ExternalInput").ap()
         for k, v in arrays.items()}
    for k, shape in SCRATCH.items():
        a[k] = nc.dram_tensor(k, shape, BF16, kind="Internal").ap()
    for k, shape in SCRATCH_F32.items():
        a[k] = nc.dram_tensor(k, shape, F32, kind="Internal").ap()
    out = nc.dram_tensor("out", (B, T, C), F32, kind="ExternalOutput").ap()
    build_program(nc, a, out)
    return run_bass_kernel_spmd(nc, [arrays], core_ids=[0]).results[0]["out"]
```

```python
from contextlib import ExitStack

import concourse.bass as bass
import numpy as np
from concourse import mybir

F32 = mybir.dt.float32
BF16 = mybir.dt.bfloat16
I32 = mybir.dt.int32
ALU = mybir.AluOpType
ACT = mybir.ActivationFunctionType
AX = mybir.AxisListType
ds = bass.ds

P = 128
B, T, C = 2, 1024, 256
TOK = B * T
TILES = TOK // P
BT = T // P
KC = C // P
QB = 512
NEG = -1.0e30


class Phase:

    def __init__(self, nc, tag):
        self.nc, self.tag, self.sems, self.stack = nc, tag, [], ExitStack()

    def sem(self, name):
        s = self.nc.alloc_semaphore(name=f"{self.tag}_{name}")
        self.sems.append(s)
        return s

    def sb(self, name, shape, dt=F32):
        return self.stack.enter_context(self.nc.sbuf_tensor(f"{self.tag}_{name}", shape, dt))

    def close(self):
        self.nc.clear_and_free_semaphores(self.sems)
        self.nc.all_engine_barrier()
        self.stack.close()


def load_and_constants(nc, m, x_d):
    ph = Phase(nc, "init")
    x_loaded, filled, made = ph.sem("x_loaded"), ph.sem("filled"), ph.sem("made")
    with nc.Block() as block:
        @block.sync
        def _(sp):
            sp.dma_start(m.x[:], x_d.rearrange("b (t p) c -> p (b t) c", p=P)).then_inc(x_loaded, 16)
            sp.wait_ge(x_loaded, 16)

        @block.gpsimd
        def _(pool):
            pool.memset(m.ident[:], 0.0).then_inc(filled, 1)
            pool.memset(m.later_k[:], 0.0).then_inc(filled, 1)
            pool.memset(m.later_q[:], 0.0).then_inc(filled, 1)
            pool.memset(m.keep[:], 1.0).then_inc(filled, 1)
            pool.wait_ge(filled, 4)
            pool.affine_select(out=m.ident[:], in_=m.ident[:], compare_op=ALU.not_equal, fill=1.0, base=0,
                               pattern=[[-1, P]], channel_multiplier=1).then_inc(made, 1)
            pool.affine_select(out=m.later_k[:], in_=m.later_k[:], compare_op=ALU.is_ge, fill=NEG, base=0,
                               pattern=[[-1, P]], channel_multiplier=1).then_inc(made, 1)
            pool.affine_select(out=m.later_q[:], in_=m.later_q[:], compare_op=ALU.is_ge, fill=NEG, base=0,
                               pattern=[[1, P]], channel_multiplier=-1).then_inc(made, 1)
            pool.affine_select(out=m.keep[:], in_=m.keep[:], compare_op=ALU.is_ge, fill=0.0, base=0,
                               pattern=[[1, P]], channel_multiplier=-1).then_inc(made, 1)

        @block.vector
        def _(dve):
            dve.wait_ge(made, 1)
            dve.tensor_copy(m.ident_b[:], m.ident[:]).then_inc(made, 1)
    ph.close()


def norm_transpose(nc, m, tag, interleave=False):
    ph = Phase(nc, tag)
    st = ph.sb("st", [P, TILES, 6])
    mv = ph.sb("mv", [P, TILES, 2])
    rstd = ph.sb("rstd", [P, TILES])
    xn = ph.sb("xn", [P, TILES, C])
    stats, var_eps, root = ph.sem("stats"), ph.sem("var_eps"), ph.sem("root")
    inverse, normed, turned, copied = ph.sem("inverse"), ph.sem("normed"), ph.sem("turned"), ph.sem("copied")
    with nc.Block() as block:
        @block.vector
        def _(dve):
            for t in range(TILES):
                dve.bn_stats(st[:, t, :], m.x[:, t, :]).then_inc(stats, 1)
            for t in range(TILES):
                dve.wait_ge(stats, t + 1)
                dve.bn_aggr(mv[:, t, :], st[:, t, :]).then_inc(var_eps, 1)
            dve.wait_ge(var_eps, TILES)
            dve.tensor_scalar(rstd[:], mv[:, :, 1], 1e-5, None, ALU.add).then_inc(var_eps, 1)
            dve.wait_ge(root, 1)
            dve.reciprocal(rstd[:], rstd[:]).then_inc(inverse, 1)
            dve.wait_ge(inverse, 1)
            for t in range(TILES):
                dve.tensor_scalar(xn[:, t, :], m.x[:, t, :], mv[:, t, 0:1], rstd[:, t:t + 1],
                                  ALU.subtract, ALU.mult).then_inc(normed, 1)
            for q in range(TILES // 4):
                dve.wait_ge(turned, 2 * q + 2)
                dve.tensor_copy(m.xnT[:, 1, q * 512:(q + 1) * 512], m.ps[:, 2 * q + 1, :])

        @block.scalar
        def _(act):
            act.wait_ge(var_eps, TILES + 1)
            act.activation(rstd[:], rstd[:], ACT.Sqrt).then_inc(root, 1)
            for q in range(TILES // 4):
                act.wait_ge(turned, 2 * q + 1)
                act.copy(m.xnT[:, 0, q * 512:(q + 1) * 512], m.ps[:, 2 * q, :])

        @block.tensor
        def _(pe):
            for q in range(TILES // 4):
                pe.wait_ge(normed, 4 * q + 4)
                for c in range(KC):
                    for t in range(4):
                        src = xn[:, 4 * q + t, c::2] if interleave else xn[:, 4 * q + t, c * P:(c + 1) * P]
                        last = pe.transpose(m.ps[:, 2 * q + c, t * P:(t + 1) * P], src, m.ident[:])
                    last.then_inc(turned, 1)
    ph.close()


def project_rope(nc, m, tag, w_d, tiles, wv_d, kv, hd, vpad, cos_d, sin_d, scr, v_sb):
    ph = Phase(nc, tag)
    PB = 4
    w = ph.sb("w", [P, KC, 2 * tiles * P])
    wv = ph.sb("wv", [P, KC, kv * hd])
    cos = ph.sb("cos", [P, T])
    sin = ph.sb("sin", [P, T])
    tc = ph.sb("tc", [P, 2, QB])
    ts = ph.sb("ts", [P, 2, QB])
    r = ph.sb("r", [P, 2, QB])
    rest = ph.sb("rest", [P, 2, QB])
    parts = ph.sb("parts", [P, PB, 3, QB], BF16)
    loaded = ph.sem("loaded")
    product, turned, summed = ph.sem("product"), ph.sem("turned"), ph.sem("summed")
    high, low1, mid, low2 = ph.sem("high"), ph.sem("low1"), ph.sem("mid"), ph.sem("low2")
    stored = [ph.sem(f"stored{p}") for p in range(PB)]
    v_product, v_copied, padded = ph.sem("v_product"), ph.sem("v_copied"), ph.sem("padded")
    items = [(mt, tb) for tb in range(TOK // QB) for mt in range(tiles)]
    with nc.Block() as block:
        @block.sync
        def _(sp):
            sp.dma_start(w[:], w_d.rearrange("(k p) n -> p k n", p=P)).then_inc(loaded, 16)
            sp.dma_start(wv[:], wv_d.rearrange("(k p) n -> p k n", p=P)).then_inc(loaded, 16)
            sp.dma_start(cos[:], cos_d).then_inc(loaded, 16)
            sp.dma_start(sin[:], sin_d).then_inc(loaded, 16)
            for n, (mt, tb) in enumerate(items):
                sp.wait_ge(low2, n + 1)
                sp.dma_start(scr[:, mt * P:(mt + 1) * P, tb * QB:(tb + 1) * QB].rearrange("s p n -> p s n"),
                             parts[:, n % PB, :, :]).then_inc(stored[n % PB], 16)
            for par in range(PB):
                sp.wait_ge(stored[par], 16 * (len(items) // PB))

        @block.tensor
        def _(pe):
            pe.wait_ge(loaded, 64)
            for n, (mt, tb) in enumerate(items):
                if n >= 2:
                    pe.wait_ge(turned, 2 * (n - 1))
                for s in range(2):
                    for k in range(KC):
                        col = (s * tiles + mt) * P
                        last = pe.matmul(m.ps[:, 2 * (n % 2) + s, :], w[:, k, col:col + P],
                                         m.xnT[:, k, tb * QB:(tb + 1) * QB], start=(k == 0), stop=(k == KC - 1))
                last.then_inc(product, 1)
            for t in range(TILES):
                if t >= 4:
                    pe.wait_ge(v_copied, t - 3)
                for k in range(KC):
                    last = pe.matmul(m.ps[:, 4 + t % 4, 0:kv * hd], m.xnT[:, k, t * P:(t + 1) * P], wv[:, k, :],
                                     start=(k == 0), stop=(k == KC - 1))
                last.then_inc(v_product, 1)

        @block.vector
        def _(dve):
            def rotate(n):
                mt, tb = items[n]
                at, a = (tb * QB) % T, n % 2
                dve.wait_ge(product, n + 1)
                dve.tensor_tensor(tc[:, a, :], m.ps[:, 2 * a, :], cos[:, at:at + QB], ALU.mult).then_inc(turned, 1)
                dve.tensor_tensor(ts[:, a, :], m.ps[:, 2 * a + 1, :], sin[:, at:at + QB], ALU.mult).then_inc(turned, 1)

            def add(n):
                a = n % 2
                dve.wait_ge(turned, 2 * n + 2)
                if n >= 2:
                    dve.wait_ge(high, n - 1)
                dve.tensor_tensor(r[:, a, :], tc[:, a, :], ts[:, a, :], ALU.add).then_inc(summed, 1)

            def remainder(n):
                a = n % 2
                dve.wait_ge(high, n + 1)
                dve.wait_ge(summed, n + 1)
                if n >= 2:
                    dve.wait_ge(low2, n - 1)
                dve.tensor_tensor(rest[:, a, :], r[:, a, :], parts[:, n % PB, 0, :], ALU.subtract).then_inc(low1, 1)

            if vpad > hd:
                dve.memset(v_sb[:], 1.0).then_inc(padded, 1)
            dve.wait_ge(loaded, 64)
            for n in range(len(items)):
                rotate(n)
                if n >= 1:
                    remainder(n - 1)
                add(n)
            remainder(len(items) - 1)

        @block.gpsimd
        def _(pool):
            for n in range(len(items)):
                a = n % 2
                pool.wait_ge(mid, n + 1)
                pool.tensor_tensor(parts[:, n % PB, 2, :], rest[:, a, :], parts[:, n % PB, 1, :],
                                   ALU.subtract).then_inc(low2, 1)

        @block.scalar
        def _(act):
            def first_part(n):
                a = n % 2
                act.wait_ge(summed, n + 1)
                if n >= PB:
                    act.wait_ge(stored[n % PB], 16 * (n // PB))
                act.copy(parts[:, n % PB, 0, :], r[:, a, :]).then_inc(high, 1)

            def second_part(n):
                act.wait_ge(low1, n + 1)
                act.copy(parts[:, n % PB, 1, :], rest[:, n % 2, :]).then_inc(mid, 1)

            for n in range(len(items)):
                first_part(n)
                if n >= 1:
                    second_part(n - 1)
            second_part(len(items) - 1)
            if vpad > hd:
                act.wait_ge(padded, 1)
            for t in range(TILES):
                act.wait_ge(v_product, t + 1)
                act.copy(v_sb[:, t, :, 0:hd],
                         m.ps[:, 4 + t % 4, 0:kv * hd].rearrange("p (h d) -> p h d", h=kv)).then_inc(v_copied, 1)
    ph.close()


Q_PARTS = (0, 0, 0, 1, 1, 2)
K_PARTS = (0, 1, 2, 0, 1, 0)
HG = 4
GB = 16 // HG


def pipelined(e, ops, per, iters, lead=8):
    def slot(i, s, end):
        for lag, fn in ops:
            if 0 <= s - lag < end:
                fn(i, s - lag)

    assert max(lag for lag, _ in ops) < lead <= per
    for s in range(lead):
        slot(0, s, per)
    with e.Fori(0, iters - 1) as i:
        for s in range(lead, per + lead):
            slot(i, s, per + lead)
    for s in range(lead, per + max(lag for lag, _ in ops)):
        slot(iters - 1, s, per)


def wait(e, sem, i, each, k):
    if isinstance(i, int):
        if i * each + k > 0:
            e.wait_ge(sem, i * each + k)
    else:
        assert k > 0
        e.wait_ge(sem, i * each + k)


def attention(nc, m, tag, scr, v_sb, wo_d, hd, kv_in_group, q_rows, scale, softcap):
    ph = Phase(nc, tag)
    plain = not softcap
    stacks = 1 if 6 * hd <= 96 else 2
    per = 6 // stacks
    rows = per * hd
    aug = 3 if plain else 0
    ER = 3
    wo = ph.sb("wo", [P, GB, C])
    q_st = ph.sb("q_st", [rows + aug, 2, HG, stacks, T], BF16)
    k_st = ph.sb("k_st", [rows + aug, 2, kv_in_group, stacks, T], BF16)
    v_st = ph.sb("v_st", [P, 2, BT, kv_in_group, 32])
    e = ph.sb("e", [P, ER, HG, QB])
    rz = ph.sb("rz", [P, QB])
    y = ph.sb("y", [P, QB])
    if plain:
        q_row = ph.sb("q_row", [rows, 2, HG, T], BF16)
        k_row = ph.sb("k_row", [rows, 2, T], BF16)
        y_raw = ph.sb("y_raw", [P, QB])
        nm = ph.sb("nm", [P, HG, BT])
        nm_two = ph.sb("nm_two", [P, HG, 2, 4])
        nmT = ph.sb("nmT", [HG * BT, P])
        nmp = ph.sb("nmp", [HG * BT, 3, P], BF16)
        spread = ph.sb("spread", [P, P])
    else:
        ones = ph.sb("ones", [P, 32])
    wo_loaded, ones_set = ph.sem("wo_loaded"), ph.sem("ones_set")
    staged, row_staged = [ph.sem("staged0"), ph.sem("staged1")], [ph.sem("row_staged0"), ph.sem("row_staged1")]
    s_ready = [ph.sem("s_ready0"), ph.sem("s_ready1")]
    s_read = [ph.sem("s_read0"), ph.sem("s_read1")]
    exped, masked, weighed = ph.sem("exped"), ph.sem("masked"), ph.sem("weighed")
    raw_copied, z_spread = ph.sem("raw_copied"), ph.sem("z_spread")
    inverse, y_scaled, o_ready, o_added = ph.sem("inverse"), ph.sem("y_scaled"), ph.sem("o_ready"), ph.sem("o_added")
    row_scores, row_max, max_turned = ph.sem("row_scores"), ph.sem("row_max"), ph.sem("max_turned")
    max_step, max_staged = ph.sem("max_step"), ph.sem("max_staged")
    steps = [(qb, kt) for qb in range(T // QB) for kt in range((qb + 1) * QB // P)]
    NS, NQ = len(steps), T // QB
    PER, ITERS = 2 * NS, B * GB // 2
    ends = {s: qb for s, (qb, kt) in enumerate(steps) if kt == (qb + 1) * QB // P - 1}
    share = HG // kv_in_group
    N_DMA, SPLIT = 13, 6
    PIECES = 12
    lo_of = lambda qb, kt: max(kt * P - qb * QB, 0)

    def place(u):
        g, s = u // NS, u % NS
        return g, g % 2, s, *steps[s], lo_of(*steps[s])

    def piece(n):
        h, r = n // PIECES, n % PIECES
        if r < 4:
            return h, r, 0, (r + 1) * P, None
        t, c = 4 + (r - 4) // 2, (r - 4) % 2
        return h, t, c * QB, QB if c == 0 else (t - 3) * P, c

    with nc.Block() as block:
        @block.sync
        def _(sp):
            sp.dma_start(wo[:], wo_d.rearrange("(j p) n -> p j n", p=P)).then_inc(wo_loaded, 16)

            def stage(g):
                b, j, par = g // GB, g % GB, g % 2
                tok = slice(b * T, (b + 1) * T)
                for n in range(6):
                    row, st = (n % per) * hd, n // per
                    sp.dma_start(q_st[row:row + hd, par, :, st, :],
                                 scr[Q_PARTS[n], j * HG * hd:(j + 1) * HG * hd, tok]
                                 .rearrange("(h d) t -> d h t", d=hd)).then_inc(staged[par], 16)
                    k0 = q_rows + j * kv_in_group * hd
                    sp.dma_start(k_st[row:row + hd, par, :, st, :],
                                 scr[K_PARTS[n], k0:k0 + kv_in_group * hd, tok]
                                 .rearrange("(h d) t -> d h t", d=hd)).then_inc(staged[par], 16)
                sp.dma_start(v_st[:, par, :, :, :], v_sb[:, b * BT:(b + 1) * BT,
                                                         j * kv_in_group:(j + 1) * kv_in_group, :]).then_inc(staged[par], 16)

            def stage_rows(g):
                b, j, par = g // GB, g % GB, g % 2
                tok = slice(b * T, (b + 1) * T)
                for n in range(6):
                    sp.dma_start(q_row[n * hd:(n + 1) * hd, par, :, :],
                                 scr[Q_PARTS[n], j * HG * hd:(j + 1) * HG * hd, tok]
                                 .rearrange("(h d) t -> d h t", d=hd)).then_inc(row_staged[par], 16)
                    k0 = q_rows + j * hd
                    sp.dma_start(k_row[n * hd:(n + 1) * hd, par, :],
                                 scr[K_PARTS[n], k0:k0 + hd, tok]).then_inc(row_staged[par], 16)

            if plain:
                stage_rows(0)
                stage_rows(1)
            for g in range(B * GB):
                if g >= 2:
                    sp.wait_ge(weighed, (g - 1) * NS)
                stage(g)
                if plain:
                    sp.wait_ge(max_step, SPLIT * (g + 1))
                    for s in range(3):
                        sp.dma_start(q_st[rows + s:rows + s + 1, g % 2, :, 0, :], nmp[:, s, :]).then_inc(max_staged, 16)
                    if g + 2 < B * GB:
                        stage_rows(g + 2)

        @block.tensor
        def _(pe):
            pe.wait_ge(ones_set, 3 if plain else 1)
            pe.wait_ge(wo_loaded, 16)

            def row_piece(k):
                def run(i, u):
                    g, par, s, *_ = place(u)
                    n = 4 * s + k
                    h, t, key, keys, c = piece(n)
                    if n == 0:
                        pe.wait_ge(row_staged[par], i * (12 * 16) + (g // 2 + 1) * 12 * 16)
                    wait(pe, row_max, i, 4 * PER, 4 * u + k - 1)
                    last = pe.matmul(m.ps[:, 5 + k % 2, 0:keys], q_row[:, par, h, t * P:(t + 1) * P],
                                     k_row[:, par, key:key + keys], start=True, stop=True)
                    if c != 0:
                        last = pe.matmul(m.ps[:, 5 + k % 2, keys - P:keys], m.ident_b[:], m.later_k[:],
                                         start=False, stop=True, skip_group_check=True)
                    last.then_inc(row_scores, 1)
                return run

            def turn_maxima(i, u):
                g, par, s, *_ = place(u)
                if s == NS - 1:
                    wait(pe, max_step, i, 2 * SPLIT, g * SPLIT + 1)
                    wait(pe, o_added, i, 4 * NQ, 2 * (g - 1) * NQ + 2)
                    pe.transpose(m.ps[0:HG * BT, 7, 0:P], nm[:].rearrange("p h t -> p (h t)"), m.ident[:]).then_inc(max_turned, 1)

            def scores(p):
                def run(i, u):
                    g, par, s, qb, kt, lo = place(u)
                    if s == 0 and p == 0:
                        pe.wait_ge(staged[par], i * (16 * N_DMA) + (g // 2 + 1) * 16 * N_DMA)
                        if plain:
                            pe.wait_ge(max_staged, i * 96 + (g + 1) * 48)
                    wait(pe, s_read[p], i, PER, u)
                    for h in (2 * p, 2 * p + 1):
                        for st in range(stacks):
                            last = pe.matmul(m.ps[:, h, lo:QB], k_st[:, par, h // share, st, kt * P:(kt + 1) * P],
                                             q_st[:, par, h, st, qb * QB + lo:(qb + 1) * QB],
                                             start=(st == 0), stop=(st == stacks - 1))
                        if plain and kt * P >= qb * QB:
                            last = pe.matmul(m.ps[:, h, lo:lo + P], m.ident_b[:], m.later_q[:],
                                             start=False, stop=True, skip_group_check=True)
                    last.then_inc(s_ready[p], 1)
                return run

            def weigh(i, u):
                g, par, s, qb, kt, lo = place(u)
                wait(pe, exped, i, PER, u + 1)
                if kt * P >= qb * QB and not plain:
                    wait(pe, masked, i, 2 * BT, g * BT + kt + 1)
                if kt == 0:
                    wait(pe, raw_copied if plain else y_scaled, i, 2 * NQ, g * NQ + qb)
                for h in range(HG):
                    last = pe.matmul(m.ps[32 * h:32 * h + 32, 4, lo:QB], v_st[:, par, kt, h // share, :],
                                     e[:, u % ER, h, lo:QB], start=(kt == 0), stop=(s in ends))
                if not plain:
                    for h in range(HG):
                        last = pe.matmul(m.ps[32 * h:32 * h + 32, 5, lo:QB], ones[:], e[:, u % ER, h, lo:QB],
                                         start=(kt == 0), stop=(s in ends))
                last.then_inc(weighed, 1)

            def spread_z(i, u):
                g, par, s, qb, *_ = place(u)
                if s in ends:
                    wait(pe, raw_copied, i, 2 * NQ, g * NQ + qb + 1)
                    wait(pe, o_added, i, 4 * NQ, 2 * (g * NQ + qb))
                    if qb == 0 or g == 0 or not isinstance(i, int):
                        wait(pe, max_step, i, 2 * SPLIT, (g + qb) * SPLIT + 2)
                    pe.matmul(m.ps[:, 7, :], spread[:], y_raw[:], start=True, stop=True).then_inc(z_spread, 1)

            def project(half):
                def run(i, u):
                    g, par, s, qb, *_ = place(u)
                    if s not in ends:
                        return
                    bank = 7 if plain else 6 + half
                    wait(pe, y_scaled, i, 2 * NQ, g * NQ + qb + 1)
                    wait(pe, o_added, i, 4 * NQ, 2 * (g * NQ + qb) + half - (0 if plain else 1))
                    j = (i % 2) * 2 + g if isinstance(i, int) else (i + g // 2) % 2 * 2 + par
                    w = wo[:, j % GB, :] if isinstance(i, int) else wo[:, ds(j, 1), :].rearrange("p o c -> p (o c)")
                    for t in range(2):
                        q = (2 * half + t) * P
                        last = pe.matmul(m.ps[:, bank, t * C:(t + 1) * C], y[:, q:q + P], w, start=True, stop=True)
                    last.then_inc(o_ready, 1)
                return run

            if plain:
                pipelined(pe, [(1, turn_maxima), (0, row_piece(0)), (15, scores(0)), (0, row_piece(1)), (15, scores(1)), (0, row_piece(2)),
                               (17, weigh), (0, row_piece(3)), (18, spread_z),
                               (19, project(0)), (20, project(1))], PER, ITERS, lead=23)
            else:
                pipelined(pe, [(0, scores(0)), (0, scores(1)), (2, weigh), (3, project(0)), (4, project(1))], PER, ITERS)

        @block.scalar
        def _(act):
            def from_scores(i, u):
                g, par, s, qb, kt, lo = place(u)
                wait(act, weighed, i, PER, u - ER + 1)
                for p in range(2):
                    wait(act, s_ready[p], i, PER, u + 1)
                    src, dst = m.ps[:, 2 * p:2 * p + 2, lo:QB], e[:, u % ER, 2 * p:2 * p + 2, lo:QB]
                    if softcap:
                        act.activation(dst, src, ACT.Tanh, scale=scale / softcap).then_inc(s_read[p], 1)
                    else:
                        act.activation(dst, src, ACT.Exp, scale=scale).then_inc(s_read[p], 1)

            def exponential(i, u):
                g, par, s, qb, kt, lo = place(u)
                wait(act, s_read[1], i, PER, u + 1)
                tile = e[:, u % ER, :, lo:QB]
                act.activation(tile, tile, ACT.Exp, scale=softcap).then_inc(exped, 1)

            def signal(i, u):
                wait(act, s_read[1], i, PER, u + 1)
                act.sem_inc(exped, 1)

            def copy_raw(i, u):
                g, par, s, qb, *_ = place(u)
                if s in ends:
                    wait(act, weighed, i, PER, u + 1)
                    wait(act, y_scaled, i, 2 * NQ, g * NQ + qb)
                    act.copy(y_raw[:], m.ps[:, 4, :]).then_inc(raw_copied, 1)

            if plain:
                pipelined(act, [(15, from_scores), (15, signal), (17, copy_raw)], PER, ITERS, lead=23)
            else:
                pipelined(act, [(0, from_scores), (1, exponential)], PER, ITERS)

        @block.gpsimd
        def _(pool):
            if plain:
                pool.memset(k_st[rows:rows + aug, :, :, :, :], 1.0).then_inc(ones_set, 1)
                pool.wait_ge(ones_set, 1)
                pool.memset(spread[:], 0.0).then_inc(ones_set, 1)
                pool.wait_ge(ones_set, 2)
                sel = spread[:].rearrange("p (h r) -> p h r", r=32)
                pool.affine_select(out=sel, in_=sel, compare_op=ALU.not_equal, fill=1.0, base=-16,
                                   pattern=[[-32, HG], [0, 32]], channel_multiplier=1).then_inc(ones_set, 1)
            else:
                pool.memset(ones[:], 1.0).then_inc(ones_set, 1)

                def mask(i, u):
                    g, par, s, qb, kt, lo = place(u)
                    if kt * P >= qb * QB:
                        wait(pool, exped, i, PER, u + 1)
                        tile = e[:, u % ER, :, lo:lo + P]
                        pool.tensor_tensor(tile, tile, m.keep[:, None, :].to_broadcast([P, HG, P]),
                                           ALU.mult).then_inc(masked, 1)

                pipelined(pool, [(1, mask)], PER, ITERS)

        @block.vector
        def _(dve):
            def maxima(i, u):
                g, par, s, *_ = place(u)
                for k in range(4):
                    h, t, key, keys, c = piece(4 * s + k)
                    if 4 * s + k == 0:
                        wait(dve, max_turned, i, 2, g)
                    wait(dve, row_scores, i, 4 * PER, 4 * u + k + 1)
                    dst = nm[:, h, t:t + 1] if c is None else nm_two[:, h, c, t - 4:t - 3]
                    dve.tensor_reduce(dst, m.ps[:, 5 + k % 2, 0:keys], AX.X, ALU.max, negate=True).then_inc(row_max, 1)

            def split_maxima(i, u):
                g, par, s, *_ = place(u)
                if s != NS - 1:
                    return
                step = lambda k: wait(dve, max_step, i, 2 * SPLIT, g * SPLIT + k)
                wait(dve, row_max, i, 4 * PER, 4 * u + 4)
                dve.tensor_tensor(nm[:, :, 4:8], nm_two[:, :, 0, :], nm_two[:, :, 1, :], ALU.min).then_inc(max_step, 1)
                wait(dve, max_staged, i, 96, g * 48)
                wait(dve, max_turned, i, 2, g + 1)
                dve.tensor_copy(nmT[:], m.ps[0:HG * BT, 7, 0:P]).then_inc(max_step, 1)
                step(2)
                dve.tensor_copy(nmp[:, 0, :], nmT[:]).then_inc(max_step, 1)
                step(3)
                dve.tensor_tensor(nmT[:], nmT[:], nmp[:, 0, :], ALU.subtract).then_inc(max_step, 1)
                step(4)
                dve.tensor_copy(nmp[:, 1, :], nmT[:]).then_inc(max_step, 1)
                step(5)
                dve.tensor_tensor(nmp[:, 2, :], nmT[:], nmp[:, 1, :], ALU.subtract).then_inc(max_step, 1)

            def normalise(i, u):
                g, par, s, qb, *_ = place(u)
                if s not in ends:
                    return
                n = g * NQ + qb
                if plain:
                    wait(dve, z_spread, i, 2 * NQ, n + 1)
                else:
                    wait(dve, weighed, i, PER, u + 1)
                dve.reciprocal(rz[:], m.ps[:, 7 if plain else 5, :]).then_inc(inverse, 1)
                wait(dve, inverse, i, 2 * NQ, n + 1)
                wait(dve, o_ready, i, 4 * NQ, 2 * n)
                dve.tensor_tensor(y[:], y_raw[:] if plain else m.ps[:, 4, :], rz[:], ALU.mult).then_inc(y_scaled, 1)

            def add(half):
                def run(i, u):
                    g, par, s, qb, *_ = place(u)
                    if s not in ends:
                        return
                    wait(dve, o_ready, i, 4 * NQ, 2 * (g * NQ + qb) + half + 1)
                    b = (i * 2 + g) // GB if isinstance(i, int) else (i + g // 2) // 2
                    rows_x = m.x[:, ds(b * BT + (qb * 4 + 2 * half), 2), :]
                    dve.tensor_tensor(rows_x, rows_x, m.ps[:, 7 if plain else 6 + half, :]
                                      .rearrange("p (t c) -> p t c", c=C), ALU.add).then_inc(o_added, 1)
                return run

            if plain:
                pipelined(dve, [(0, maxima), (18, normalise), (19, add(0)), (20, add(1)), (0, split_maxima)],
                          PER, ITERS, lead=23)
            else:
                pipelined(dve, [(2, normalise), (3, add(0)), (4, add(1))], PER, ITERS)
    ph.close()


def in_blocks(e, n, body):
    body(0)
    with e.Fori(1, n) as i:
        body(i)


def wait_from(e, sem, i, each, k=0):
    assert k >= 0
    if not isinstance(i, int) or i * each + k > 0:
        e.wait_ge(sem, i * each + k)


def relu_ffn(nc, m, tag, w1_d, b1_d, w2_d, b2_d, w3_d, b3_d):
    ph = Phase(nc, tag)
    H = 512
    HT = H // P
    w1 = ph.sb("w1", [P, KC, H])
    w2 = ph.sb("w2", [P, HT, H])
    w3 = ph.sb("w3", [P, HT, C])
    b1 = ph.sb("b1", [P, HT])
    b2 = ph.sb("b2", [P, HT])
    b3 = ph.sb("b3", [P, C])
    h1 = ph.sb("h1", [P, HT, QB])
    h2 = ph.sb("h2", [P, HT, QB])
    loaded, b3_added = ph.sem("loaded"), ph.sem("b3_added")
    p1, p2, p3 = ph.sem("p1"), ph.sem("p2"), ph.sem("p3")
    r1, r2, added = ph.sem("r1"), ph.sem("r2"), ph.sem("added")
    NB = TOK // QB
    with nc.Block() as block:
        @block.sync
        def _(sp):
            sp.dma_start(w1[:], w1_d.rearrange("(k p) n -> p k n", p=P)).then_inc(loaded, 16)
            sp.dma_start(w2[:], w2_d.rearrange("(k p) n -> p k n", p=P)).then_inc(loaded, 16)
            sp.dma_start(w3[:], w3_d.rearrange("(k p) n -> p k n", p=P)).then_inc(loaded, 16)
            sp.dma_start(b1[:], b1_d).then_inc(loaded, 16)
            sp.dma_start(b2[:], b2_d).then_inc(loaded, 16)
            sp.dma_start(b3[:], b3_d.partition_broadcast(P)).then_inc(loaded, 16)

        @block.gpsimd
        def _(pool):
            pool.wait_ge(loaded, 96)
            for t in range(TILES):
                pool.tensor_tensor(m.x[:, t, :], m.x[:, t, :], b3[:], ALU.add).then_inc(b3_added, 1)

        @block.tensor
        def _(pe):
            pe.wait_ge(loaded, 96)
            def block_of(i):
                for o in range(HT):
                    wait_from(pe, r1, i, HT)
                    for k in range(KC):
                        last = pe.matmul(m.ps[:, o, :], w1[:, k, o * P:(o + 1) * P], m.xnT[:, k, ds(i * QB, QB)],
                                         start=(k == 0), stop=(k == KC - 1))
                    last.then_inc(p1, 1)
                for o in range(HT):
                    wait_from(pe, added, i, HT)
                    for k in range(HT):
                        if o == 0:
                            wait_from(pe, r1, i, HT, k + 1)
                        last = pe.matmul(m.ps[:, 4 + o, :], w2[:, k, o * P:(o + 1) * P], h1[:, k, :],
                                         start=(k == 0), stop=(k == HT - 1))
                    last.then_inc(p2, 1)
                wait_from(pe, r2, i, HT, HT)
                for t in range(HT):
                    for k in range(HT):
                        last = pe.matmul(m.ps[:, 4 + t, 0:C], h2[:, k, t * P:(t + 1) * P], w3[:, k, :],
                                         start=(k == 0), stop=(k == HT - 1))
                    last.then_inc(p3, 1)

            in_blocks(pe, NB, block_of)

        @block.scalar
        def _(act):
            act.wait_ge(loaded, 96)
            def block_of(i):
                for o in range(HT):
                    wait_from(act, p1, i, HT, o + 1)
                    if o == 0:
                        wait_from(act, p2, i, HT)
                    act.activation(h1[:, o, :], m.ps[:, o, :], ACT.Relu, bias=b1[:, o:o + 1]).then_inc(r1, 1)
                for o in range(HT):
                    wait_from(act, p2, i, HT, o + 1)
                    if o == 0:
                        wait_from(act, p3, i, HT)
                    act.activation(h2[:, o, :], m.ps[:, 4 + o, :], ACT.Relu, bias=b2[:, o:o + 1]).then_inc(r2, 1)

            in_blocks(act, NB, block_of)

        @block.vector
        def _(dve):
            dve.wait_ge(b3_added, TILES)
            def block_of(i):
                for t in range(HT):
                    wait_from(dve, p3, i, HT, t + 1)
                    row = m.x[:, ds(i * HT + t, 1), :]
                    dve.tensor_tensor(row, row, m.ps[:, 4 + t:5 + t, 0:C], ALU.add).then_inc(added, 1)

            in_blocks(dve, NB, block_of)
    ph.close()


MLP = 2048


def dequantise(nc, m, a):
    ph = Phase(nc, "dq")
    packed = ph.sb("packed", [P, 3, MLP], I32)
    scale = ph.sb("scale", [P, 3, MLP])
    code = ph.sb("code", [P, MLP], I32)
    sign = ph.sb("sign", [P, MLP], I32)
    val = ph.sb("val", [P, MLP])
    half = ph.sb("half", [P, MLP])
    loaded, step = ph.sem("loaded"), ph.sem("step")
    with nc.Block() as block:
        @block.sync
        def _(sp):
            sp.dma_start(packed[:, 0, :], a["gate_p"]).then_inc(loaded, 16)
            sp.dma_start(packed[:, 1, :], a["up_p"]).then_inc(loaded, 16)
            sp.dma_start(packed[:, 2, :].rearrange("p (m h) -> p m h", m=8),
                         a["down_p"].rearrange("(m p) h -> p m h", p=P)).then_inc(loaded, 16)
            for k in range(8):
                rows = slice(16 * k, 16 * k + 16)
                sp.dma_start(scale[rows, 0, :], a["gate_s"][k].partition_broadcast(16)).then_inc(loaded, 16)
                sp.dma_start(scale[rows, 1, :], a["up_s"][k].partition_broadcast(16)).then_inc(loaded, 16)
                sp.dma_start(scale[rows, 2, :], a["down_s"][k].partition_broadcast(16)).then_inc(loaded, 16)

        @block.vector
        def _(dve):
            dve.wait_ge(loaded, 16 * 27)
            n = 0
            for w in range(3):
                for odd in range(2):
                    dst = (m.wg, m.wu, m.wd)[w][:, odd, :]
                    sh = 4 * odd
                    dve.wait_ge(step, n) if n else None
                    dve.tensor_scalar(code[:], packed[:, w, :], sh, 7, ALU.logical_shift_right,
                                      ALU.bitwise_and).then_inc(step, 1)
                    dve.tensor_scalar(sign[:], packed[:, w, :], sh, 8, ALU.logical_shift_right,
                                      ALU.bitwise_and).then_inc(step, 1)
                    dve.wait_ge(step, n + 2)
                    dve.scalar_tensor_tensor(val[:], code[:], 4.0, code[:], ALU.max, ALU.add).then_inc(step, 1)
                    dve.tensor_scalar(half[:], sign[:], -0.125, 0.5, ALU.mult, ALU.add).then_inc(step, 1)
                    dve.wait_ge(step, n + 4)
                    dve.scalar_tensor_tensor(val[:], code[:], 6.0, val[:], ALU.max, ALU.add).then_inc(step, 1)
                    dve.wait_ge(step, n + 5)
                    dve.scalar_tensor_tensor(val[:], code[:], 6.0, val[:], ALU.max, ALU.add).then_inc(step, 1)
                    dve.wait_ge(step, n + 6)
                    dve.scalar_tensor_tensor(val[:], val[:], -16.0, half[:], ALU.add, ALU.mult).then_inc(step, 1)
                    dve.wait_ge(step, n + 7)
                    dve.tensor_tensor(dst, val[:], scale[:, w, :], ALU.mult).then_inc(step, 1)
                    n += 8
    ph.close()


def gated_ffn(nc, m, tag):
    ph = Phase(nc, tag)
    NT, NB = MLP // P, TOK // QB
    ge = ph.sb("ge", [P, 2, QB])
    it = ph.sb("it", [P, 2, QB])
    gate, up, gelued, gated, down, added = (ph.sem("gate"), ph.sem("up"), ph.sem("gelued"), ph.sem("gated"),
                                            ph.sem("down"), ph.sem("added"))
    with nc.Block() as block:
        @block.tensor
        def _(pe):
            def first(i, n):
                cols = slice(n * P, (n + 1) * P)
                wait_from(pe, gated, i, NT, max(n - 1, 0))
                for w, bank, done in ((m.wg, 0, gate), (m.wu, 2, up)):
                    for k in range(2):
                        last = pe.matmul(m.ps[:, bank + n % 2, :], w[:, k, cols], m.xnT[:, k, ds(i * QB, QB)],
                                         start=(k == 0), stop=(k == 1))
                    last.then_inc(done, 1)

            def second(i, n):
                wait_from(pe, gated, i, NT, n + 1)
                if n == 0:
                    wait_from(pe, added, i, 4)
                for t in range(4):
                    last = pe.matmul(m.ps[:, 4 + t, 0:C], it[:, n % 2, t * P:(t + 1) * P],
                                     m.wd[:, n % 2, (n // 2) * C:(n // 2 + 1) * C],
                                     start=(n == 0), stop=(n == NT - 1))
                last.then_inc(down, 1)

            def block_of(i):
                first(i, 0)
                for n in range(NT):
                    if n + 1 < NT:
                        first(i, n + 1)
                    second(i, n)

            in_blocks(pe, NB, block_of)

        @block.scalar
        def _(act):
            def block_of(i):
                for n in range(NT):
                    wait_from(act, gate, i, NT, n + 1)
                    if n >= 2:
                        wait_from(act, gated, i, NT, n - 1)
                    act.activation(ge[:, n % 2, :], m.ps[:, n % 2, :], ACT.Gelu_apprx_tanh).then_inc(gelued, 1)

            in_blocks(act, NB, block_of)

        @block.vector
        def _(dve):
            def block_of(i):
                for n in range(NT):
                    wait_from(dve, gelued, i, NT, n + 1)
                    wait_from(dve, up, i, NT, n + 1)
                    if n >= 2:
                        wait_from(dve, down, i, NT, n - 1)
                    dve.tensor_tensor(it[:, n % 2, :], ge[:, n % 2, :], m.ps[:, 2 + n % 2, :],
                                      ALU.mult).then_inc(gated, 1)
                wait_from(dve, down, i, NT, NT)
                x_block = m.x[:, ds(i * 4, 4), :]
                dve.tensor_tensor(x_block, x_block, m.ps[:, 4:8, 0:C], ALU.add).then_inc(added, 4)

            in_blocks(dve, NB, block_of)
    ph.close()


def diff_attention(nc, m, a, tag, scr, v_sb):
    ph = Phase(nc, tag)
    HD, U = 16, HG * BT
    QUADS = 2 * U // HG
    EB = 4
    PER, ITERS = 2 * U, GB
    q_st = ph.sb("q_st", [96, 2, 2 * HG, T], BF16)
    k_st = ph.sb("k_st", [96, 2, 2, T], BF16)
    v_st = ph.sb("v_st", [P, 2, BT, 32])
    lv = ph.sb("lv", [P, 4, 256])
    dots = ph.sb("dots", [P, 2, 16])
    nlam = ph.sb("nlam", [P, 16])
    nm = ph.sb("nm", [P, EB, 2])
    e = ph.sb("e", [P, EB, 2, T])
    z = ph.sb("z", [P, EB, 2])
    rz = ph.sb("rz", [P, EB, 2])
    c = ph.sb("c", [P, EB])
    t2 = ph.sb("t2", [P, 2, T])
    low = ph.sb("low", [P, EB])
    rz2 = ph.sb("rz2", [P, HG])
    pr = ph.sb("pr", [P, 2, T])
    prT = ph.sb("prT", [P, 2 * HG, T])
    outT = ph.sb("outT", [P, P])
    lam_loaded, lam_step = ph.sem("lam_loaded"), ph.sem("lam_step")
    staged = [ph.sem("staged0"), ph.sem("staged1")]
    two = lambda name: [ph.sem(name + "0"), ph.sem(name + "1")]
    scored, maxed, exped, copied = two("scored"), two("maxed"), two("exped"), two("copied")
    masked = ph.sem("masked")
    inv, coef, mixed, lowered = ph.sem("inv"), ph.sem("coef"), ph.sem("mixed"), ph.sem("lowered")
    p_done, turned, valued = ph.sem("p_done"), ph.sem("turned"), ph.sem("valued")
    out_copied, returned = ph.sem("out_copied"), ph.sem("returned")
    inv2, scaled, mixable = ph.sem("inv2"), ph.sem("scaled"), ph.sem("mixable")

    def place(u):
        b, t, h = (u // U) % 2, (u // HG) % BT, u % HG
        return b, h, t, (t + 1) * P

    def copier(u):
        return 0 if (u // HG) % BT < 4 and u % 2 == 0 else 1

    def copies(u, x):
        return sum(copier(v) == x for v in range(u))

    COPIES = (copies(2 * U, 0), copies(2 * U, 1))

    def short_second(u):
        return 1 if 1 <= u % U < U // 2 else 0

    with nc.Block() as block:
        @block.sync
        def _(sp):
            for n, name in enumerate(("lq1", "lk1", "lq2", "lk2")):
                sp.dma_start(lv[:, n, :], a[name].partition_broadcast(P)).then_inc(lam_loaded, 16)
            for g in range(2 * GB):
                if g >= 2:
                    sp.wait_ge(valued, BT * (g - 1))
                j, b = g // 2, g % 2
                tok = slice(b * T, (b + 1) * T)
                for n in range(6):
                    sp.dma_start(q_st[n * HD:(n + 1) * HD, b, :, :],
                                 scr[Q_PARTS[n], j * 128:(j + 1) * 128, tok]
                                 .rearrange("(h d) t -> d h t", d=HD)).then_inc(staged[b], 16)
                    sp.dma_start(k_st[n * HD:(n + 1) * HD, b, :, :],
                                 scr[K_PARTS[n], 512 + j * 32:512 + (j + 1) * 32, tok]
                                 .rearrange("(h d) t -> d h t", d=HD)).then_inc(staged[b], 16)
                sp.dma_start(v_st[:, b, :, :], v_sb[:, b * BT:(b + 1) * BT, j, :]).then_inc(staged[b], 16)

        @block.tensor
        def _(pe):
            def score(s):
                def run(i, u):
                    b, h, t, L = place(u)
                    if u % U == 0 and s == 0:
                        pe.wait_ge(staged[b], (i + u // PER) * (16 * 13) + 16 * 13)
                    wait(pe, exped[s], i, PER, u - short_second(u))
                    for cc in range(t // 4 + 1):
                        bank = 2 * s + (u % 2 if t < 4 else cc)
                        n = min(QB, L - cc * QB)
                        last = pe.matmul(m.ps[:, bank, 0:n], q_st[:, b, 2 * h + s, t * P:(t + 1) * P],
                                         k_st[:, b, s, cc * QB:cc * QB + n], start=True, stop=True)
                    last = pe.matmul(m.ps[:, bank, n - P:n], m.ident_b[:], m.later_k[:],
                                     start=False, stop=True, skip_group_check=True)
                    last.then_inc(scored[s], 1)
                return run

            def turn(i, u):
                b, h, t, L = place(u)
                wait(pe, p_done, i, PER, u + 1)
                for x in range(2):
                    wait(pe, copied[x], i, COPIES[x], copies(u - short_second(u), x))
                for kb in range(t + 1):
                    bank = 4 + (u % 2 if t < 4 else kb // 4)
                    last = pe.transpose(m.ps[:, bank, (kb % 4) * P:(kb % 4 + 1) * P],
                                        pr[:, u % 2, kb * P:(kb + 1) * P], m.ident[:])
                last.then_inc(turned, 1)

            def value(part):
                def run(i, u):
                    b, h, t, L = place(u)
                    if h != HG - 1:
                        return
                    if part == 0:
                        for x in range(2):
                            wait(pe, copied[x], i, COPIES[x], copies(u + 1, x))
                        wait(pe, out_copied, i, QUADS, u // HG)
                    for kb in range((t + 1) * part // 3, (t + 1) * (part + 1) // 3):
                        for hq in range(HG):
                            last = pe.matmul(m.ps[32 * hq:32 * hq + 32, 6, 0:P], v_st[:, b, kb, :],
                                             prT[:, (u - h + hq) % (2 * HG), kb * P:(kb + 1) * P],
                                             start=(kb == 0), stop=(kb == t))
                    if part == 2:
                        last.then_inc(valued, 1)
                return run

            def turn_back(i, u):
                if u % HG == HG - 1:
                    wait(pe, out_copied, i, QUADS, u // HG + 1)
                    wait(pe, scaled, i, QUADS, u // HG)
                    pe.transpose(m.ps[:, 7, 0:P], outT[:], m.ident[:]).then_inc(returned, 1)

            pipelined(pe, [(0, score(0)), (5, turn), (0, score(1)), (6, value(0)), (7, value(1)), (8, value(2)),
                           (10, turn_back)], PER, ITERS, lead=14)

        def copy_turned(e, x):
            def run(i, u):
                b, h, t, L = place(u)
                if copier(u) != x:
                    return
                wait(e, turned, i, PER, u + 1)
                wait(e, valued, i, QUADS, u // HG - 1)
                src = m.ps[:, 4 + u % 2, 0:L] if t < 4 else m.ps[:, 4:6, :].rearrange("p a n -> p (a n)")[:, 0:L]
                (e.copy if x else e.tensor_copy)(prT[:, u % (2 * HG), 0:L], src).then_inc(copied[x], 1)
            return run

        @block.scalar
        def _(act):
            act.wait_ge(lam_step, 2)
            act.activation(dots[:], dots[:], ACT.Exp).then_inc(lam_step, 1)

            def exps(s):
                def run(i, u):
                    b, h, t, L = place(u)
                    wait(act, maxed[s], i, PER, u + 1)
                    wait(act, lowered, i, PER, u - (EB - 1))
                    src = m.ps[:, 2 * s + u % 2, 0:L] if t < 4 else \
                        m.ps[:, 2 * s:2 * s + 2, :].rearrange("p a n -> p (a n)")[:, 0:L]
                    act.activation(e[:, u % EB, s, 0:L], src, ACT.Exp, bias=nm[:, u % EB, s:s + 1],
                                   accum_out=z[:, u % EB, s:s + 1]).then_inc(exped[s], 1)
                return run

            def softmax(i, u):
                b, h, t, L = place(u)
                wait(act, lowered, i, PER, u + 1)
                wait(act, turned, i, PER, u - 1)
                act.activation(pr[:, u % 2, 0:L], t2[:, u % 2, 0:L], ACT.Exp, bias=low[:, u % EB:u % EB + 1],
                               scale=-1.0).then_inc(p_done, 1)

            def copy_out(i, u):
                if u % HG == HG - 1:
                    wait(act, valued, i, QUADS, u // HG + 1)
                    wait(act, returned, i, QUADS, u // HG)
                    act.copy(outT[:], m.ps[:, 6, 0:P]).then_inc(out_copied, 1)

            pipelined(act, [(0, exps(0)), (4, softmax), (5, copy_turned(act, 1)), (0, exps(1)), (9, copy_out)],
                      PER, ITERS, lead=14)

        @block.gpsimd
        def _(pool):
            def mask(i, u):
                b, h, t, L = place(u)
                wait(pool, exped[0], i, PER, u + 1)
                tile = e[:, u % EB, 0, t * P:L]
                pool.tensor_tensor(tile, tile, m.later_k[:], ALU.add).then_inc(masked, 1)

            def scale_second(i, u):
                b, h, t, L = place(u)
                k = u % EB
                wait(pool, coef, i, 2 * PER, 2 * u + 1)
                pool.tensor_tensor(e[:, k, 1, 0:L], e[:, k, 1, 0:L], c[:, k:k + 1].to_broadcast([P, L]),
                                   ALU.mult).then_inc(mixed, 1)

            pipelined(pool, [(0, mask), (1, scale_second)], PER, ITERS, lead=14)

        @block.vector
        def _(dve):
            dve.wait_ge(lam_loaded, 64)
            dve.tensor_tensor(lv[:, 0, :], lv[:, 0, :], lv[:, 1, :], ALU.mult).then_inc(lam_step, 1)
            dve.tensor_tensor(lv[:, 2, :], lv[:, 2, :], lv[:, 3, :], ALU.mult).then_inc(inv, 1)
            dve.wait_ge(lam_step, 1)
            dve.wait_ge(inv, 1)
            dve.tensor_reduce(dots[:], lv[:, 0:4:2, :].rearrange("p n (h d) -> p n h d", d=HD), AX.X,
                              ALU.add).then_inc(lam_step, 1)
            dve.wait_ge(lam_step, 3)
            dve.tensor_tensor(nlam[:], dots[:, 1, :], dots[:, 0, :], ALU.subtract).then_inc(lam_step, 1)
            dve.wait_ge(lam_step, 4)
            dve.tensor_scalar(nlam[:], nlam[:], float(0.8 - 0.6 * float(np.exp(-0.3 * 0))), None,
                              ALU.subtract).then_inc(lam_step, 1)
            dve.wait_ge(lam_step, 5)

            def maxima(s):
                def run(i, u):
                    b, h, t, L = place(u)
                    wait(dve, scored[s], i, PER, u + 1)
                    src = m.ps[:, 2 * s + u % 2, 0:L] if t < 4 else \
                        m.ps[:, 2 * s:2 * s + 2, :].rearrange("p a n -> p (a n)")[:, 0:L]
                    dve.tensor_reduce(nm[:, u % EB, s:s + 1], src, AX.X, ALU.max, negate=True).then_inc(maxed[s], 1)
                return run

            def coefficients(i, u):
                hh = i * HG + (u % HG + HG * (u // PER))
                k = u % EB
                wait(dve, exped[0], i, PER, u + 1)
                wait(dve, exped[1], i, PER, u + 1)
                dve.reciprocal(rz[:, k, :], z[:, k, :]).then_inc(inv, 1)
                wait(dve, inv, i, PER, u + 2)
                dve.scalar_tensor_tensor(c[:, k:k + 1], rz[:, k, 1:2], nlam[:, ds(hh, 1)], z[:, k, 0:1],
                                         ALU.mult, ALU.mult).then_inc(coef, 1)
                dve.tensor_scalar(rz[:, k, 0:1], rz[:, k, 0:1], -1.0, None, ALU.mult).then_inc(coef, 1)

            def mix(i, u):
                b, h, t, L = place(u)
                k = u % EB
                wait(dve, coef, i, 2 * PER, 2 * u + 2)
                wait(dve, mixed, i, PER, u + 1)
                wait(dve, masked, i, PER, u + 1)
                wait(dve, p_done, i, PER, u - 1)
                dve.sem_inc(mixable, 1)
                dve.tensor_tensor_reduce(t2[:, u % 2, 0:L], e[:, k, 0, 0:L], e[:, k, 1, 0:L], rz[:, k, 0:1], 3.0e38,
                                         ALU.add, ALU.min, low[:, k:k + 1]).then_inc(lowered, 1)

            def result(i, u):
                b, h, t, L = place(u)
                if h != HG - 1:
                    return
                wait(dve, returned, i, QUADS, u // HG + 1)
                out = m.ps[:, 7, 0:P].rearrange("p (h d) -> p h d", h=HG)
                dve.reciprocal(rz2[:], out[:, :, HD]).then_inc(inv2, 1)
                wait(dve, inv2, i, QUADS, u // HG + 1)
                cols = ds((i + u // PER) * (HG * HD), HG * HD)
                dve.tensor_tensor(m.y_tok[:, b * BT + t, cols].rearrange("p (h d) -> p h d", h=HG), out[:, :, 0:HD],
                                  rz2[:, :, None].to_broadcast([P, HG, HD]), ALU.mult).then_inc(scaled, 1)

            pipelined(dve, [(0, maxima(0)), (3, mix), (5, copy_turned(dve, 0)), (1, coefficients), (0, maxima(1)),
                            (11, result)], PER, ITERS, lead=14)
    ph.close()


def norm_project(nc, m, tag, w_d, g_d, eps, factor):
    ph = Phase(nc, tag)
    w = ph.sb("w", [P, KC, C])
    g = ph.sb("g", [P, C])
    sq = ph.sb("sq", [P, TILES, C])
    ms = ph.sb("ms", [P, TILES, 16])
    yT = ph.sb("yT", [P, 2, C])
    loaded, step, root = ph.sem("loaded"), ph.sem("step"), ph.sem("root")
    turned, copied, product, added = ph.sem("turned"), ph.sem("copied"), ph.sem("product"), ph.sem("added")
    with nc.Block() as block:
        @block.sync
        def _(sp):
            sp.dma_start(w[:], w_d.rearrange("(k p) n -> p k n", p=P)).then_inc(loaded, 16)
            sp.dma_start(g[:], g_d.partition_broadcast(P)).then_inc(loaded, 16)

        @block.vector
        def _(dve):
            y = m.y_tok
            dve.tensor_tensor(sq[:], y[:], y[:], ALU.mult).then_inc(step, 1)
            dve.wait_ge(step, 1)
            dve.tensor_reduce(ms[:], sq[:].rearrange("p t (h d) -> p t h d", d=16), AX.X, ALU.add).then_inc(step, 1)
            dve.wait_ge(step, 2)
            dve.tensor_scalar(ms[:], ms[:], 1.0 / 16, eps, ALU.mult, ALU.add).then_inc(step, 1)
            dve.wait_ge(root, 1)
            dve.reciprocal(ms[:], ms[:]).then_inc(step, 1)
            dve.wait_ge(step, 4)
            dve.wait_ge(loaded, 32)
            for t in range(TILES):
                dve.scalar_tensor_tensor(sq[:, t, :], y[:, t, :], factor, g[:], ALU.mult, ALU.mult).then_inc(step, 1)
                dve.wait_ge(step, 5 + 2 * t)
                yt = sq[:, t, :].rearrange("p (h d) -> p h d", d=16)
                dve.tensor_tensor(yt, yt, ms[:, t, :, None].to_broadcast([P, 16, 16]), ALU.mult).then_inc(step, 1)
                if t >= 1:
                    dve.wait_ge(product, t)
                    dve.tensor_tensor(m.x[:, t - 1, :], m.x[:, t - 1, :], m.ps[:, 2 + (t - 1) % 2, 0:C],
                                      ALU.add).then_inc(added, 1)
            dve.wait_ge(product, TILES)
            dve.tensor_tensor(m.x[:, TILES - 1, :], m.x[:, TILES - 1, :], m.ps[:, 2 + (TILES - 1) % 2, 0:C], ALU.add)

        @block.scalar
        def _(act):
            act.wait_ge(step, 3)
            act.activation(ms[:], ms[:], ACT.Sqrt).then_inc(root, 1)
            for t in range(TILES):
                act.wait_ge(turned, t + 1)
                if t >= 2:
                    act.wait_ge(product, t - 1)
                act.copy(yT[:, t % 2, :], m.ps[:, t % 2, 0:C]).then_inc(copied, 1)

        @block.tensor
        def _(pe):
            pe.wait_ge(loaded, 32)

            def turn(t):
                pe.wait_ge(step, 6 + 2 * t)
                if t >= 2:
                    pe.wait_ge(copied, t - 1)
                for k in range(KC):
                    last = pe.transpose(m.ps[:, t % 2, k * P:(k + 1) * P], sq[:, t, k * P:(k + 1) * P], m.ident[:])
                last.then_inc(turned, 1)

            turn(0)
            for t in range(TILES):
                if t + 1 < TILES:
                    turn(t + 1)
                pe.wait_ge(copied, t + 1)
                if t >= 2:
                    pe.wait_ge(added, t - 1)
                for k in range(KC):
                    last = pe.matmul(m.ps[:, 2 + t % 2, 0:C], yT[:, t % 2, k * P:(k + 1) * P], w[:, k, :],
                                     start=(k == 0), stop=(k == KC - 1))
                last.then_inc(product, 1)
    ph.close()


CH = 16
NCH = T // CH
NG = 4
HL = 8


def ttt_project(nc, m, a, tag):
    ph = Phase(nc, tag)
    w = ph.sb("w", [P, KC, 3 * C + 16])
    wg1 = ph.sb("wg1", [P, KC, 16])
    wg2 = ph.sb("wg2", [16, C])
    g1T = ph.sb("g1T", [16, TOK])
    k = ph.sb("k", [P, TILES, 16, CH + 1])
    k_flat = ph.sb("k_flat", [P, TILES, C])
    v = ph.sb("v", [P, TILES, C])
    sq = ph.sb("sq", [P, C])
    kn = ph.sb("kn", [P, TILES, 16])
    lw = ph.sb("lw", [P, 2, C])
    loaded, g1, g1_copied = ph.sem("loaded"), ph.sem("g1"), ph.sem("g1_copied")
    product, read_a, read_d = ph.sem("product"), ph.sem("read_a"), ph.sem("read_d")
    norm, root, keyed, acts = ph.sem("norm"), ph.sem("root"), ph.sem("keyed"), ph.sem("acts")
    target, turned, copied, stored = ph.sem("target"), ph.sem("turned"), ph.sem("copied"), ph.sem("stored")
    qT, kT = m.xnT, m.kT
    with nc.Block() as block:
        @block.sync
        def _(sp):
            sp.dma_start(w[:], a["w_t"].rearrange("(k p) n -> p k n", p=P)).then_inc(loaded, 16)
            sp.dma_start(wg1[:], a["wg1"].rearrange("(k p) n -> p k n", p=P)).then_inc(loaded, 16)
            sp.dma_start(wg2[:], a["wg2"]).then_inc(loaded, 16)
            sp.dma_start(lw[:, 0, :], a["ln_w"].partition_broadcast(P)).then_inc(loaded, 16)
            sp.dma_start(lw[:, 1, :], a["ln_b"].partition_broadcast(P)).then_inc(loaded, 16)
            sp.wait_ge(acts, 3)
            sp.wait_ge(keyed, 1)
            sp.dma_start(a["scr_k"].rearrange("(t p) n -> p t n", p=P), k[:].rearrange("p t h d -> p t (h d)")).then_inc(stored, 16)
            sp.wait_ge(target, 2 * TILES)
            sp.dma_start(a["scr_t"].rearrange("(t p) n -> p t n", p=P), v[:]).then_inc(stored, 16)
            sp.wait_ge(stored, 32)

        @block.tensor
        def _(pe):
            pe.wait_ge(loaded, 80)
            for n in range(4):
                for c in range(KC):
                    last = pe.matmul(m.ps[0:16, n, :], wg1[:, c, :], m.xnT[:, c, n * QB:(n + 1) * QB],
                                     start=(c == 0), stop=(c == KC - 1))
            last.then_inc(g1, 1)
            pe.wait_ge(g1_copied, 1)
            for t in range(TILES):
                s = 4 * (t % 2)
                if t >= 2:
                    pe.wait_ge(read_a, 2 * (t - 1))
                    pe.wait_ge(read_d, t - 1)
                for bank, col, n in ((0, 0, C), (1, C, 2 * C), (2, 3 * C, 16)):
                    for c in range(KC):
                        pe.matmul(m.ps[:, s + bank, 0:n], m.xnT[:, c, t * P:(t + 1) * P], w[:, c, col:col + n],
                                  start=(c == 0), stop=(c == KC - 1))
                pe.matmul(m.ps[:, s, C:2 * C], g1T[:, t * P:(t + 1) * P], wg2[:], start=True, stop=True).then_inc(product, 1)
            pe.wait_ge(acts, 1)
            pe.wait_ge(keyed, 1)
            n = 0
            for src in (m.q_tok, k_flat):
                for c in range(KC):
                    for q in range(4):
                        if n >= 8:
                            pe.wait_ge(copied, n - 7)
                        else:
                            pe.wait_ge(read_a, 2 * TILES)
                            pe.wait_ge(read_d, TILES)
                        for t in range(4):
                            last = pe.transpose(m.ps[:, n % 8, t * P:(t + 1) * P],
                                                src[:, 4 * q + t, c * P:(c + 1) * P], m.ident[:])
                        last.then_inc(turned, 1)
                        n += 1

        @block.scalar
        def _(act):
            act.wait_ge(g1, 1)
            act.copy(g1T[:].rearrange("p (n t) -> p n t", n=4), m.ps[0:16, 0:4, :]).then_inc(g1_copied, 1)
            for t in range(TILES):
                s = 4 * (t % 2)
                act.wait_ge(product, t + 1)
                act.copy(m.q_tok[:, t, :], m.ps[:, s, 0:C]).then_inc(read_a, 1)
                act.copy(m.gate[:, t, :], m.ps[:, s, C:2 * C]).then_inc(read_a, 1)
            act.wait_ge(read_a, 2 * TILES)
            act.activation(m.q_tok[:], m.q_tok[:], ACT.Silu).then_inc(acts, 1)
            act.activation(m.gate[:], m.gate[:], ACT.Sigmoid).then_inc(acts, 1)
            act.wait_ge(read_d, TILES)
            act.activation(k[:, :, :, CH], k[:, :, :, CH], ACT.Sigmoid).then_inc(acts, 1)
            act.wait_ge(norm, TILES + 1)
            act.activation(kn[:], kn[:], ACT.Sqrt).then_inc(root, 1)
            for n in range(16):
                act.wait_ge(turned, n + 1)
                c, q = (n // 4) % 2, n % 4
                dst = (qT if n < 8 else kT)[:, c, q * QB:(q + 1) * QB]
                act.copy(dst, m.ps[:, n % 8, :]).then_inc(copied, 1)

        @block.vector
        def _(dve):
            for t in range(TILES):
                s = 4 * (t % 2)
                dve.wait_ge(product, t + 1)
                dve.tensor_copy(k_flat[:, t, :], m.ps[:, s + 1, 0:C])
                dve.tensor_copy(v[:, t, :], m.ps[:, s + 1, C:2 * C])
                dve.tensor_copy(k[:, t, :, CH], m.ps[:, s + 2, 0:16]).then_inc(read_d, 1)
                dve.wait_ge(read_d, t + 1)
                dve.tensor_tensor(sq[:], k_flat[:, t, :], k_flat[:, t, :], ALU.mult).then_inc(target, 1)
                dve.wait_ge(target, t + 1)
                dve.tensor_reduce(kn[:, t, :], sq[:].rearrange("p (h d) -> p h d", d=CH), AX.X, ALU.add).then_inc(norm, 1)
            dve.wait_ge(norm, TILES)
            dve.tensor_scalar(kn[:], kn[:], 1e-6, None, ALU.add).then_inc(norm, 1)
            dve.wait_ge(root, 1)
            dve.reciprocal(kn[:], kn[:]).then_inc(norm, 1)
            dve.wait_ge(norm, TILES + 2)
            kf = k_flat[:].rearrange("p t (h d) -> p t h d", d=CH)
            bc = kn[:, :, :, None].to_broadcast([P, TILES, 16, CH])
            dve.tensor_tensor(kf, kf, bc, ALU.mult).then_inc(norm, 1)
            dve.wait_ge(norm, TILES + 3)
            dve.tensor_copy(k[:, :, :, 0:CH], kf).then_inc(keyed, 1)
            dve.wait_ge(acts, 3)
            dve.wait_ge(loaded, 80)
            for t in range(TILES):
                dve.tensor_tensor(v[:, t, :], k_flat[:, t, :], v[:, t, :], ALU.subtract).then_inc(read_d, 1)
                dve.wait_ge(read_d, TILES + 2 * t + 1)
                dve.tensor_tensor(v[:, t, :], v[:, t, :], lw[:, 1, :], ALU.add).then_inc(read_d, 1)
                dve.wait_ge(read_d, TILES + 2 * t + 2)
                dve.tensor_tensor(v[:, t, :], v[:, t, :], lw[:, 0, :], ALU.mult).then_inc(target, 1)
    ph.close()


def ttt_scan(nc, m, a, tag):
    ph = Phase(nc, tag)
    tb = ph.sb("tb", [P, NCH, NG, CH])
    kc = ph.sb("kc", [P, NCH, NG, CH + 1])
    qh = ph.sb("qh", [P, NCH, NG, CH])
    block_mask = ph.sb("block_mask", [P, P])
    tri = ph.sb("tri", [P, P])
    w2 = ph.sb("w2", [P, 2, CH])
    S = ph.sb("S", [P, NG, 2 * CH])
    qhT = ph.sb("qhT", [P, 2, P])
    kT_bd = ph.sb("kT_bd", [P, 2, NG, P])
    qT_bd = ph.sb("qT_bd", [P, 2, NG, P])
    k_bd = ph.sb("k_bd", [P, 2, NG, P])
    at = ph.sb("at", [P, 2, NG, P])
    s4 = lambda name: ph.sb(name, [P, NG])
    s64 = lambda name: ph.sb(name, [P, NG, CH])
    mu, var, root, rstd, rate, m1, m2 = (s4(x) for x in ("mu", "var", "root", "rstd", "rate", "m1", "m2"))
    cen, sq, hat, gw, pg, hm, vv = (s64(x) for x in ("cen", "sq", "hat", "gw", "pg", "hm", "vv"))
    eps = ph.sb("eps", [P, 1])
    u = ph.sb("u", [P, NG, 2 * CH])
    loaded, made = ph.sem("loaded"), ph.sem("made")
    bd_p, k_spread = ph.sem("bd_p"), ph.sem("k_spread")
    kh_ready, at_ready, at_done, qh_ready, qh_copied = (ph.sem("kh_ready"), ph.sem("at_ready"), ph.sem("at_done"),
                                                        ph.sem("qh_ready"), ph.sem("qh_copied"))
    chain, u_ready, ds_ready, s_ready = ph.sem("chain"), ph.sem("u_ready"), ph.sem("ds_ready"), ph.sem("s_ready")
    rooted, eps_set = ph.sem("rooted"), ph.sem("eps_set")
    q_used, back_copied, turned_back = ph.sem("q_used"), ph.sem("back_copied"), ph.sem("turned_back")
    stored = ph.sem("stored")
    qT, kT = m.xnT, m.kT
    LINKS, PER = 15, 8
    FIRST = 2
    bc = lambda x: x[:, :, None].to_broadcast([P, NG, CH])

    with nc.Block() as block:
        @block.sync
        def _(sp):
            n = 0
            for b in range(B):
                for half in range(2):
                    g = 2 * b + half
                    for h in range(HL):
                        rows, hd = slice(h * CH, (h + 1) * CH), half * HL + h
                        tok = slice(b * T, (b + 1) * T)
                        sp.dma_start(tb[rows, :, g, :], a["scr_t"][tok, hd * CH:(hd + 1) * CH]
                                     .rearrange("(n c) e -> c n e", c=CH)).then_inc(loaded, 16)
                        sp.dma_start(kc[rows, :, g, :], a["scr_k"][tok, hd * (CH + 1):(hd + 1) * (CH + 1)]
                                     .rearrange("(n c) e -> c n e", c=CH)).then_inc(loaded, 16)
            sp.dma_start(w2[:], a["ln_w_rows"]).then_inc(loaded, 16)
            sp.wait_ge(back_copied, NCH)
            for b in range(B):
                for half in range(2):
                    for h in range(HL):
                        rows, hd = slice(h * CH, (h + 1) * CH), half * HL + h
                        sp.dma_start(a["scr_q"][b * T:(b + 1) * T, hd * CH:(hd + 1) * CH]
                                     .rearrange("(n c) e -> c n e", c=CH), qh[rows, :, 2 * b + half, :]).then_inc(stored, 16)
            sp.wait_ge(stored, 16 * 32)

        @block.gpsimd
        def _(pool):
            pool.memset(block_mask[:], 1.0).then_inc(made, 1)
            pool.memset(tri[:], 1.0).then_inc(made, 1)
            pool.wait_ge(made, 2)
            bm = block_mask[:].rearrange("p (h c) -> p h c", c=CH)
            pool.affine_select(out=bm, in_=bm, compare_op=ALU.is_ge, fill=0.0, base=0,
                               pattern=[[-CH, HL], [0, CH]], channel_multiplier=1).then_inc(made, 1)
            pool.affine_select(out=tri[:], in_=tri[:], compare_op=ALU.is_ge, fill=0.0, base=0,
                               pattern=[[1, P]], channel_multiplier=-1).then_inc(made, 1)
            pool.wait_ge(made, 4)
            pool.affine_select(out=bm, in_=bm, compare_op=ALU.is_ge, fill=0.0, base=CH - 1,
                               pattern=[[CH, HL], [0, CH]], channel_multiplier=-1).then_inc(made, 1)
            pool.wait_ge(made, 5)

            def spread(i, n):
                wait(pool, q_used, i, PER, n - 1)
                for src, dst in ((kT, kT_bd), (qT, qT_bd)):
                    for b in range(B):
                        cols = src[:, :, ds(i * (PER * CH) + (b * T + n * CH), CH)][:, :, None, :].to_broadcast([P, 2, HL, CH])
                        pool.tensor_tensor(dst[:, n % 2, 2 * b:2 * b + 2, :].rearrange("p g (h c) -> p g h c", c=CH), cols,
                                           block_mask[:].rearrange("p (h c) -> p h c", c=CH)[:, None, :, :]
                                           .to_broadcast([P, 2, HL, CH]), ALU.mult).then_inc(bd_p, 1)

            def spread_k(i, n):
                wait(pool, ds_ready, i, PER, n - 1)
                keys = kc[:, ds(i * PER + n, 1), :, 0:CH].rearrange("p o g d -> p (o g) d")[:, :, None, :]
                pool.tensor_tensor(k_bd[:, n % 2, :, :].rearrange("p g (h d) -> p g h d", d=CH),
                                   keys.to_broadcast([P, NG, HL, CH]),
                                   block_mask[:].rearrange("p (h d) -> p h d", d=CH)[:, None, :, :]
                                   .to_broadcast([P, NG, HL, CH]), ALU.mult).then_inc(k_spread, 1)

            pool.wait_ge(loaded, 16 * 65)
            pipelined(pool, [(0, spread), (0, spread_k)], PER, NCH // PER, lead=6)

        @block.tensor
        def _(pe):
            def early(i, n):
                wait(pe, bd_p, i, 4 * PER, 4 * n + 4)
                wait(pe, at_done, i, PER, n - 1)
                for g in range(NG):
                    last = pe.matmul(m.ps[:, 4 + n % 2, g * P:(g + 1) * P], kT_bd[:, n % 2, g, :],
                                     qT_bd[:, n % 2, g, :], start=True, stop=True)
                last.then_inc(at_ready, 1)

            def state_keys(i, n):
                wait(pe, s_ready, i, PER, n + 1)
                for g in range(NG):
                    last = pe.matmul(m.ps[:, 0, g * CH:(g + 1) * CH], kT_bd[:, n % 2, g, :], S[:, g, 0:CH],
                                     start=True, stop=True)
                last.then_inc(kh_ready, 1)

            def state_queries(i, n):
                wait(pe, qh_copied, i, PER, n - 1)
                for g in range(NG):
                    last = pe.matmul(m.ps[32 * g:32 * g + 32, 2 + n % 2, 0:P], S[:, g, :], qT_bd[:, n % 2, g, :],
                                     start=True, stop=True)
                last.then_inc(q_used, 1)

            def update(i, n):
                wait(pe, k_spread, i, PER, n + 1)
                wait(pe, u_ready, i, PER, n + 1)
                for g in range(NG):
                    last = pe.matmul(m.ps[:, 1, g * CH:(g + 1) * CH], k_bd[:, n % 2, g, :], u[:, g, 0:CH],
                                     start=True, stop=True)
                last.then_inc(ds_ready, 1)

            def within_chunk(i, n):
                wait(pe, at_done, i, PER, n + 1)
                for g in range(NG):
                    last = pe.matmul(m.ps[32 * g:32 * g + 32, 2 + n % 2, 0:P], u[:, g, :], at[:, n % 2, g, :],
                                     start=False, stop=True, skip_group_check=True)
                last.then_inc(qh_ready, 1)

            def turn_back(i, n):
                wait(pe, qh_copied, i, PER, n + 1)
                wait(pe, back_copied, i, PER, n - 1)
                pe.transpose(m.ps[:, 6 + n % 2, 0:P], qhT[:, n % 2, :], m.ident[:]).then_inc(turned_back, 1)

            pipelined(pe, [(2, update), (1, state_keys), (2, within_chunk), (1, state_queries), (0, early),
                           (3, turn_back)], PER, NCH // PER, lead=6)

        @block.scalar
        def _(act):
            def square_root(i, n):
                wait(act, chain, i, PER * LINKS, n * LINKS + 4 + FIRST)
                act.activation(root[:], var[:], ACT.Sqrt, scale=1.0 / CH, bias=eps[:]).then_inc(rooted, 1)

            def copy(i, n):
                wait(act, qh_ready, i, PER, n + 1)
                wait(act, turned_back, i, PER, n - 1)
                act.copy(qhT[:, n % 2, :], m.ps[:, 2 + n % 2, 0:P]).then_inc(qh_copied, 1)

            def copy_back(i, n):
                wait(act, turned_back, i, PER, n + 1)
                act.copy(qh[:, ds(i * PER + n, 1), :, :].rearrange("p o g e -> p (o g) e"),
                         m.ps[:, 6 + n % 2, 0:P].rearrange("p (g e) -> p g e", g=NG)[:, :, 0:CH]).then_inc(back_copied, 1)

            act.wait_ge(eps_set, 1)
            pipelined(act, [(0, square_root), (1, copy), (2, copy_back)], PER, NCH // PER, lead=6)

        @block.vector
        def _(dve):
            dve.memset(eps[:], 1e-6).then_inc(eps_set, 1)
            dve.memset(u[:], 0.0)
            dve.memset(S[:], 0.0).then_inc(s_ready, 1)
            dve.wait_ge(made, 5)
            dve.wait_ge(loaded, 16 * 65)
            dve.tensor_scalar(kc[:, :, :, CH], kc[:, :, :, CH], -2.0, None, ALU.mult).then_inc(chain, 1)
            dve.tensor_tensor(w2[:], w2[:], w2[:], ALU.mult).then_inc(chain, 1)
            dve.wait_ge(chain, 2)

            def done(i, n, k):
                wait(dve, chain, i, PER * LINKS, n * LINKS + k + FIRST)

            def variance(i, n):
                kh = m.ps[:, 0, 0:NG * CH].rearrange("p (g e) -> p g e", e=CH)
                wait(dve, kh_ready, i, PER, n + 1)
                dve.tensor_reduce(mu[:], kh, AX.X, ALU.add).then_inc(chain, 1)
                done(i, n, 1)
                dve.scalar_tensor_tensor(cen[:], bc(mu), -1.0 / CH, kh, ALU.mult, ALU.add).then_inc(chain, 1)
                done(i, n, 2)
                dve.tensor_tensor(sq[:], cen[:], cen[:], ALU.mult).then_inc(chain, 1)
                done(i, n, 3)
                dve.tensor_reduce(var[:], sq[:], AX.X, ALU.add).then_inc(chain, 1)
                done(i, n, 4)

            def gradient(i, n):
                wait(dve, rooted, i, PER, n + 1)
                dve.reciprocal(rstd[:], root[:]).then_inc(chain, 1)
                done(i, n, 5)
                dve.tensor_tensor(hat[:], cen[:], bc(rstd), ALU.mult).then_inc(chain, 1)
                now = kc[:, ds(i * PER + n, 1), :, CH].rearrange("p o g -> p (o g)")
                dve.tensor_tensor(rate[:], rstd[:], now, ALU.mult).then_inc(chain, 1)
                done(i, n, 6)
                dve.tensor_tensor(gw[:].rearrange("p (b h) e -> p b h e", h=2),
                                  hat[:].rearrange("p (b h) e -> p b h e", h=2),
                                  w2[:, None, :, :].to_broadcast([P, B, 2, CH]), ALU.mult).then_inc(chain, 1)
                done(i, n, 8)
                dve.tensor_tensor(gw[:], gw[:], tb[:, ds(i * PER + n, 1), :, :].rearrange("p o g e -> p (o g) e"),
                                  ALU.add).then_inc(chain, 1)
                done(i, n, 9)
                dve.tensor_tensor(pg[:], gw[:], hat[:], ALU.mult).then_inc(chain, 1)
                dve.tensor_reduce(m1[:], gw[:], AX.X, ALU.add).then_inc(chain, 1)
                done(i, n, 10)
                dve.tensor_reduce(m2[:], pg[:], AX.X, ALU.add).then_inc(chain, 1)
                done(i, n, 11)
                dve.scalar_tensor_tensor(vv[:], bc(m1), -1.0 / CH, gw[:], ALU.mult, ALU.add).then_inc(chain, 1)
                done(i, n, 12)
                dve.scalar_tensor_tensor(hm[:], hat[:], -1.0 / CH, bc(m2), ALU.mult, ALU.mult).then_inc(chain, 1)
                done(i, n, 14)
                dve.tensor_tensor(vv[:], vv[:], hm[:], ALU.add).then_inc(chain, 1)
                done(i, n, 15)
                wait(dve, qh_ready, i, PER, n)
                dve.tensor_tensor(u[:, :, 0:CH], vv[:], bc(rate), ALU.mult).then_inc(u_ready, 1)

            def mask(i, n):
                wait(dve, at_ready, i, PER, n + 1)
                wait(dve, qh_ready, i, PER, n - 1)
                dve.tensor_tensor(at[:, n % 2, :, :], m.ps[:, 4 + n % 2, :].rearrange("p (g c) -> p g c", c=P),
                                  tri[:, None, :].to_broadcast([P, NG, P]), ALU.mult).then_inc(at_done, 1)

            def advance(i, n):
                wait(dve, ds_ready, i, PER, n + 1)
                dve.tensor_tensor(S[:, :, 0:CH], S[:, :, 0:CH], m.ps[:, 1, 0:NG * CH].rearrange("p (g e) -> p g e", e=CH),
                                  ALU.add).then_inc(s_ready, 1)

            pipelined(dve, [(0, variance), (0, gradient), (0, mask), (0, advance)], PER, NCH // PER, lead=6)
    ph.close()


def ttt_output(nc, m, a, tag):
    ph = Phase(nc, tag)
    z = m.y_tok
    sq = ph.sb("sq", [P, TILES, C])
    lw = ph.sb("lw", [P, 2, C])
    mu = ph.sb("mu", [P, TILES, 16])
    var = ph.sb("var", [P, TILES, 16])
    loaded, step, root = ph.sem("loaded"), ph.sem("step"), ph.sem("root")
    heads = lambda t: t[:].rearrange("p t (h e) -> p t h e", e=CH)
    wide = lambda t: t[:, :, :, None].to_broadcast([P, TILES, 16, CH])
    with nc.Block() as block:
        @block.sync
        def _(sp):
            sp.dma_start(z[:], a["scr_q"].rearrange("(t p) n -> p t n", p=P)).then_inc(loaded, 16)
            sp.dma_start(lw[:, 0, :], a["ln_w"].partition_broadcast(P)).then_inc(loaded, 16)
            sp.dma_start(lw[:, 1, :], a["ln_b"].partition_broadcast(P)).then_inc(loaded, 16)

        @block.scalar
        def _(act):
            act.wait_ge(step, 6)
            act.activation(var[:], var[:], ACT.Sqrt).then_inc(root, 1)

        @block.vector
        def _(dve):
            n = [0]

            def then(ins):
                n[0] += 1
                ins.then_inc(step, 1)
                dve.wait_ge(step, n[0])

            dve.wait_ge(loaded, 48)
            then(dve.tensor_reduce(mu[:], heads(z), AX.X, ALU.add))
            then(dve.tensor_scalar(mu[:], mu[:], 1.0 / CH, None, ALU.mult))
            then(dve.tensor_tensor(heads(z), heads(z), wide(mu), ALU.subtract))
            then(dve.tensor_tensor(sq[:], z[:], z[:], ALU.mult))
            then(dve.tensor_reduce(var[:], heads(sq), AX.X, ALU.add))
            then(dve.tensor_scalar(var[:], var[:], 1.0 / CH, 1e-6, ALU.mult, ALU.add))
            dve.wait_ge(root, 1)
            then(dve.reciprocal(var[:], var[:]))
            then(dve.tensor_tensor(heads(z), heads(z), wide(var), ALU.mult))
            then(dve.tensor_tensor(z[:], z[:], lw[:, 0:1, :].to_broadcast([P, TILES, C]), ALU.mult))
            then(dve.tensor_tensor(z[:], z[:], lw[:, 1:2, :].to_broadcast([P, TILES, C]), ALU.add))
            then(dve.tensor_tensor(z[:], z[:], m.q_tok[:], ALU.add))
            then(dve.tensor_tensor(z[:], z[:], m.gate[:], ALU.mult))
    ph.close()


def store_x(nc, m, out_d):
    ph = Phase(nc, "store")
    stored = ph.sem("stored")
    with nc.Block() as block:
        @block.sync
        def _(sp):
            sp.dma_start(out_d.rearrange("b (t p) c -> p (b t) c", p=P), m.x[:]).then_inc(stored, 16)
            sp.wait_ge(stored, 16)
    ph.close()


class Memory:
    pass


def build_program(nc, a, out_d, limit=99):
    m = Memory()
    m.weights = ExitStack()
    with ExitStack() as ctx:
        def sb(name, shape, dt=F32):
            return ctx.enter_context(nc.sbuf_tensor(name, shape, dt))

        m.x = sb("x", [P, TILES, C])
        m.xnT = sb("xnT", [P, KC, TOK])
        m.ident = sb("ident", [P, P])
        m.ident_b = sb("ident_b", [P, P], BF16)
        m.later_k = sb("later_k", [P, P], BF16)
        m.keep = sb("keep", [P, P])
        m.later_q = sb("later_q", [P, P], BF16)
        m.ps = ctx.enter_context(nc.psum_tensor("ps", [P, 8, 512], F32))

        load_and_constants(nc, m, a["x"])
        stages = STAGES(nc, m, a)
        for n, s in enumerate(stages[:limit]):
            s()
        m.weights.close()
        store_x(nc, m, out_d)


def STAGES(nc, m, a):
    def attn_softcap():
        norm_transpose(nc, m, "n1")
        with nc.sbuf_tensor("v_a", [P, TILES, 8, 32], F32) as v_sb:
            project_rope(nc, m, "pa", a["wqk_a"], 6, a["wv_a"], 8, 32, 32, a["cos_a"], a["sin_a"], a["scr_a"], v_sb)
            attention(nc, m, "aa", a["scr_a"], v_sb, a["wo_a"], 32, 2, 512, 256.0 ** -0.5, 50.0)

    def ffn(tag):
        norm_transpose(nc, m, tag + "n")
        relu_ffn(nc, m, tag, a["w1"], a["b1"], a["w2"], a["b2"], a["w3"], a["b3"])

    def attn_plain():
        norm_transpose(nc, m, "n3")
        with nc.sbuf_tensor("v_b", [P, TILES, 4, 32], F32) as v_sb:
            project_rope(nc, m, "pb", a["wqk_b"], 3, a["wv_b"], 4, 16, 32, a["cos_b"], a["sin_b"], a["scr_b"], v_sb)
            attention(nc, m, "ab", a["scr_b"], v_sb, a["wo_b"], 16, 1, 256, 0.25, None)

    def weights():
        sb = lambda name: m.weights.enter_context(nc.sbuf_tensor(name, [P, 2, MLP], F32))
        m.wg, m.wu = sb("wg"), sb("wu")
        m.wd = sb("wd")
        dequantise(nc, m, a)

    def gated(tag):
        norm_transpose(nc, m, tag + "n", interleave=True)
        gated_ffn(nc, m, tag)

    def attn_diff():
        norm_transpose(nc, m, "n5")
        with nc.sbuf_tensor("y_tok", [P, TILES, C], F32) as m.y_tok:
            with nc.sbuf_tensor("v_d", [P, TILES, 4, 32], F32) as v_sb:
                project_rope(nc, m, "pd", a["wqk_d"], 5, a["wv_d"], 4, 16, 32, a["cos_d"], a["sin_d"], a["scr_d"], v_sb)
                diff_attention(nc, m, a, "ad", a["scr_d"], v_sb)
            norm_project(nc, m, "od", a["wo_d"], a["rms_d"], 1e-8, 1.0 - (0.8 - 0.6 * float(np.exp(-0.3 * 0))))

    def attn_ttt():
        norm_transpose(nc, m, "n7")
        with ExitStack() as st:
            sb = lambda name, shape: st.enter_context(nc.sbuf_tensor(name, shape, F32))
            m.q_tok, m.gate = sb("q_tok", [P, TILES, C]), sb("gate_t", [P, TILES, C])
            with nc.sbuf_tensor("kT_t", [P, KC, TOK], F32) as m.kT:
                ttt_project(nc, m, a, "pt")
                ttt_scan(nc, m, a, "st")
            m.y_tok = sb("y_tok2", [P, TILES, C])
            ttt_output(nc, m, a, "ot")
            norm_project(nc, m, "ow", a["wo_t"], a["norm_w"], 1e-6, 1.0)

    return [attn_softcap, lambda: ffn("f2"), attn_plain, lambda: ffn("f4"),
            attn_diff, lambda: (weights(), gated("g6")), attn_ttt, lambda: gated("g8")]


def rope_tables(hd, interleaved, factor=1.0):
    inv = (1.0 / np.float32(10000.0) ** (np.arange(0, hd, 2, dtype=np.float32) / np.float32(hd))).astype(np.float32)
    ang = np.arange(T, dtype=np.float32)[:, None] * inv[None, :]
    cos, sin = np.cos(ang).T, np.sin(ang).T
    if interleaved:
        cos, sin = np.repeat(cos, 2, 0), np.stack([-sin, sin], 1).reshape(hd, T)
    else:
        cos, sin = np.concatenate([cos, cos]), np.concatenate([-sin, sin])
    cos, sin = cos * np.float32(factor), sin * np.float32(factor)
    return (np.ascontiguousarray(np.tile(cos, (P // hd, 1)), np.float32),
            np.ascontiguousarray(np.tile(sin, (P // hd, 1)), np.float32))


def swap_halves(w, hd):
    n = w.shape[1]
    return w.reshape(-1, n // hd, 2, hd // 2)[:, :, ::-1].reshape(-1, n)


def lay_out(i):
    f = {k: np.asarray(v) for k, v in i.items()}
    cat = lambda *p: np.ascontiguousarray(np.concatenate(p, 1))
    d = {"x": f["L0_attn_a_X"]}
    q, k = f["L0_attn_a_Wq"], f["L0_attn_a_Wk"]
    d["wqk_a"] = cat(q, k, swap_halves(q, 32), swap_halves(k, 32))
    d["wv_a"], d["wo_a"] = f["L0_attn_a_Wv"], f["L0_attn_a_Wo"]
    d["cos_a"], d["sin_a"] = rope_tables(32, False)
    q, k = f["L0_attn_b_Wq"], f["L0_attn_b_Wk"]
    ks = swap_halves(k, 16)
    d["wqk_b"] = cat(q, k, k, swap_halves(q, 16), ks, ks)
    d["wv_b"] = f["L0_attn_b_Wv"]
    wo = np.zeros((16, 32, C), np.float32)
    wo[:, :16] = f["L0_attn_b_Wproj"].reshape(16, 16, C)
    d["wo_b"] = wo.reshape(512, C)
    d["cos_b"], d["sin_b"] = rope_tables(16, False)
    d["w1"], d["w2"], d["w3"] = (np.ascontiguousarray(f[f"L0_ffn_W{n}"].T) for n in (1, 2, 3))
    d["b1"], d["b2"] = (np.ascontiguousarray(f[f"L0_ffn_b{n}"].reshape(4, P).T) for n in (1, 2))
    d["b3"] = f["L0_ffn_b3"]
    q, k = f["L1_attn_a_Wq"], f["L1_attn_a_Wk"]
    d["wqk_d"] = cat(q, k, swap_halves(q, 2), swap_halves(k, 2))
    d["wv_d"], d["wo_d"] = f["L1_attn_a_Wv"], f["L1_attn_a_Wo"]
    d["cos_d"], d["sin_d"] = rope_tables(32, True, 0.5)
    d["lq1"], d["lk1"], d["lq2"], d["lk2"] = (f[f"L1_attn_a_{n}"].reshape(-1) for n in ("lq1", "lk1", "lq2", "lk2"))
    d["rms_d"] = np.tile(f["L1_attn_a_rms_w"], 16)

    w = [f[f"L1_attn_b_W{n}"] for n in ("q", "k", "v", "beta")]
    d["w_t"], d["wg1"], d["wg2"], d["wo_t"] = cat(*w), f["L1_attn_b_Wg1"], f["L1_attn_b_Wg2"], f["L1_attn_b_Wo"]
    ln_w = f["L1_attn_b_ln_w"]
    d["ln_w"], d["ln_b"], d["norm_w"] = ln_w.reshape(-1), f["L1_attn_b_ln_b"].reshape(-1), f["L1_attn_b_norm_w"]
    d["ln_w_rows"] = np.ascontiguousarray(np.repeat(ln_w.reshape(2, 8, 1, 16), 16, 2).reshape(2, P, 16).transpose(1, 0, 2))

    def hidden(p):
        return np.ascontiguousarray(p.T.reshape(-1, MLP // 256, P, 2).transpose(0, 1, 3, 2).reshape(-1, MLP))
    d["gate_p"], d["up_p"] = hidden(f["L1_ffn_gate_W_packed"]), hidden(f["L1_ffn_up_W_packed"])
    d["gate_s"], d["up_s"] = hidden(f["L1_ffn_gate_scales"]), hidden(f["L1_ffn_up_scales"])
    d["down_p"] = np.ascontiguousarray(f["L1_ffn_down_W_packed"].T)
    d["down_s"] = np.ascontiguousarray(f["L1_ffn_down_scales"].T.reshape(8, 8, C).transpose(1, 0, 2).reshape(8, MLP))
    return d


SCRATCH = {"scr_a": (3, 768, TOK), "scr_b": (3, 384, TOK), "scr_d": (3, 640, TOK)}
SCRATCH_F32 = {"scr_k": (TOK, 16 * 17), "scr_t": (TOK, C), "scr_q": (TOK, C)}


def kernel(**inputs):
    import concourse.bacc as bacc
    from concourse.bass_utils import run_bass_kernel_spmd

    nc = bacc.Bacc("TRN2", target_bir_lowering=False, num_devices=1)
    arrays = {f"in_{k}": v for k, v in lay_out(inputs).items()}
    a = {k[3:]: nc.dram_tensor(k, v.shape, mybir.dt.from_np(v.dtype), kind="ExternalInput").ap()
         for k, v in arrays.items()}
    for k, shape in SCRATCH.items():
        a[k] = nc.dram_tensor(k, shape, BF16, kind="Internal").ap()
    for k, shape in SCRATCH_F32.items():
        a[k] = nc.dram_tensor(k, shape, F32, kind="Internal").ap()
    out = nc.dram_tensor("out", (B, T, C), F32, kind="ExternalOutput").ap()
    build_program(nc, a, out)
    return run_bass_kernel_spmd(nc, [arrays], core_ids=[0]).results[0]["out"]
```

```python
from contextlib import ExitStack

import concourse.bass as bass
import numpy as np
from concourse import mybir

F32 = mybir.dt.float32
BF16 = mybir.dt.bfloat16
I32 = mybir.dt.int32
ALU = mybir.AluOpType
ACT = mybir.ActivationFunctionType
AX = mybir.AxisListType
ds = bass.ds

P = 128
B, T, C = 2, 1024, 256
TOK = B * T
TILES = TOK // P
BT = T // P
KC = C // P
QB = 512
NEG = -1.0e30


class Phase:

    def __init__(self, nc, tag):
        self.nc, self.tag, self.sems, self.stack = nc, tag, [], ExitStack()

    def sem(self, name):
        s = self.nc.alloc_semaphore(name=f"{self.tag}_{name}")
        self.sems.append(s)
        return s

    def sb(self, name, shape, dt=F32):
        return self.stack.enter_context(self.nc.sbuf_tensor(f"{self.tag}_{name}", shape, dt))

    def close(self):
        self.nc.clear_and_free_semaphores(self.sems)
        self.nc.all_engine_barrier()
        self.stack.close()


def load_and_constants(nc, m, x_d):
    ph = Phase(nc, "init")
    x_loaded, filled, made = ph.sem("x_loaded"), ph.sem("filled"), ph.sem("made")
    with nc.Block() as block:
        @block.sync
        def _(sp):
            sp.dma_start(m.x[:], x_d.rearrange("b (t p) c -> p (b t) c", p=P)).then_inc(x_loaded, 16)
            sp.wait_ge(x_loaded, 16)

        @block.gpsimd
        def _(pool):
            pool.memset(m.ident[:], 0.0).then_inc(filled, 1)
            pool.memset(m.later_k[:], 0.0).then_inc(filled, 1)
            pool.memset(m.later_q[:], 0.0).then_inc(filled, 1)
            pool.memset(m.warm[:], 0.0).then_inc(filled, 1)
            pool.memset(m.keep[:], 1.0).then_inc(filled, 1)
            pool.wait_ge(filled, 5)
            pool.affine_select(out=m.ident[:], in_=m.ident[:], compare_op=ALU.not_equal, fill=1.0, base=0,
                               pattern=[[-1, P]], channel_multiplier=1).then_inc(made, 1)
            pool.affine_select(out=m.later_k[:], in_=m.later_k[:], compare_op=ALU.is_ge, fill=NEG, base=0,
                               pattern=[[-1, P]], channel_multiplier=1).then_inc(made, 1)
            pool.affine_select(out=m.later_q[:], in_=m.later_q[:], compare_op=ALU.is_ge, fill=NEG, base=0,
                               pattern=[[1, P]], channel_multiplier=-1).then_inc(made, 1)
            pool.affine_select(out=m.keep[:], in_=m.keep[:], compare_op=ALU.is_ge, fill=0.0, base=0,
                               pattern=[[1, P]], channel_multiplier=-1).then_inc(made, 1)

        @block.vector
        def _(dve):
            dve.wait_ge(made, 1)
            dve.tensor_copy(m.ident_b[:], m.ident[:]).then_inc(made, 1)
    ph.close()


def norm_transpose(nc, m, tag, interleave=False, loads=None):
    ph = Phase(nc, tag)
    st = ph.sb("st", [P, TILES, 6])
    mv = ph.sb("mv", [P, TILES, 2])
    rstd = ph.sb("rstd", [P, TILES])
    shift = ph.sb("shift", [P, TILES])
    eps = ph.sb("eps", [P, 1])
    xn = ph.sb("xn", [P, TILES, C])
    eps_set, stats, variance, root = ph.sem("eps_set"), ph.sem("stats"), ph.sem("variance"), ph.sem("root")
    inverse, shifted = ph.sem("inverse"), ph.sem("shifted")
    scaled_d, scaled_a, turned = ph.sem("scaled_d"), ph.sem("scaled_a"), ph.sem("turned")
    NQ = TILES // 4
    quarter = lambda q: slice(4 * q, 4 * q + 4)
    with nc.Block() as block:
        if loads:
            @block.sync
            def _(sp):
                loads(sp)

        @block.vector
        def _(dve):
            def statistics(q):
                for t in range(4 * q, 4 * q + 4):
                    dve.bn_stats(st[:, t, :], m.x[:, t, :]).then_inc(stats, 1)
                for t in range(4 * q, 4 * q + 4):
                    dve.wait_ge(stats, t + 1)
                    dve.bn_aggr(mv[:, t, :], st[:, t, :]).then_inc(variance, 1)

            def scale(q):
                dve.wait_ge(root, q + 1)
                dve.reciprocal(rstd[:, quarter(q)], rstd[:, quarter(q)]).then_inc(inverse, 1)
                dve.wait_ge(inverse, q + 1)
                dve.scalar_tensor_tensor(shift[:, quarter(q)], mv[:, quarter(q), 0], -1.0, rstd[:, quarter(q)],
                                         ALU.mult, ALU.mult).then_inc(shifted, 1)
                for t in (4 * q, 4 * q + 1):
                    dve.tensor_scalar(xn[:, t, :], m.x[:, t, :], mv[:, t, 0:1], rstd[:, t:t + 1],
                                      ALU.subtract, ALU.mult).then_inc(scaled_d, 1)

            dve.memset(eps[:], 1e-5).then_inc(eps_set, 1)
            for q in range(NQ):
                statistics(q)
                if q >= 1:
                    scale(q - 1)
            scale(NQ - 1)
            for q in range(NQ):
                dve.wait_ge(turned, 2 * q + 2)
                dve.tensor_copy(m.xnT[:, 1, q * 512:(q + 1) * 512], m.ps[:, 2 * q + 1, :])

        @block.scalar
        def _(act):
            act.wait_ge(eps_set, 1)

            def square_root(q):
                act.wait_ge(variance, 4 * q + 4)
                act.activation(rstd[:, quarter(q)], mv[:, quarter(q), 1], ACT.Sqrt, bias=eps[:]).then_inc(root, 1)

            square_root(0)
            for q in range(NQ):
                if q + 1 < NQ:
                    square_root(q + 1)
                act.wait_ge(shifted, q + 1)
                for t in (4 * q + 2, 4 * q + 3):
                    act.activation(xn[:, t, :], m.x[:, t, :], ACT.Identity, bias=shift[:, t:t + 1],
                                   scale=rstd[:, t:t + 1]).then_inc(scaled_a, 1)
            for q in range(NQ):
                act.wait_ge(turned, 2 * q + 1)
                act.copy(m.xnT[:, 0, q * 512:(q + 1) * 512], m.ps[:, 2 * q, :])

        @block.tensor
        def _(pe):
            for q in range(NQ):
                for c in range(KC):
                    for t in range(4):
                        if c == 0 and t == 0:
                            pe.wait_ge(scaled_d, 2 * q + 2)
                        if c == 0 and t == 2:
                            pe.wait_ge(scaled_a, 2 * q + 2)
                        src = xn[:, 4 * q + t, c::2] if interleave else xn[:, 4 * q + t, c * P:(c + 1) * P]
                        last = pe.transpose(m.ps[:, 2 * q + c, t * P:(t + 1) * P], src, m.ident[:])
                    last.then_inc(turned, 1)
    ph.close()


def project_rope(nc, m, tag, w_d, tiles, wv_d, kv, hd, vpad, cos_d, sin_d, scr, v_sb):
    ph = Phase(nc, tag)
    PB = 4
    w = ph.sb("w", [P, KC, 2 * tiles * P])
    wv = ph.sb("wv", [P, KC, kv * hd])
    cos = ph.sb("cos", [P, T])
    sin = ph.sb("sin", [P, T])
    loaded = ph.sem("loaded")

    def loads(sp):
        sp.dma_start(w[:], w_d.rearrange("(k p) n -> p k n", p=P)).then_inc(loaded, 16)
        sp.dma_start(wv[:], wv_d.rearrange("(k p) n -> p k n", p=P)).then_inc(loaded, 16)
        sp.dma_start(cos[:], cos_d).then_inc(loaded, 16)
        sp.dma_start(sin[:], sin_d).then_inc(loaded, 16)

    norm_transpose(nc, m, tag + "n", loads=loads)
    tc = ph.sb("tc", [P, 2, QB])
    ts = ph.sb("ts", [P, 2, QB])
    r = ph.sb("r", [P, 2, QB])
    rest = ph.sb("rest", [P, 2, QB])
    parts = ph.sb("parts", [P, PB, 3, QB], BF16)
    product, turned, summed = ph.sem("product"), ph.sem("turned"), ph.sem("summed")
    high, low1, mid, low2 = ph.sem("high"), ph.sem("low1"), ph.sem("mid"), ph.sem("low2")
    stored = [ph.sem(f"stored{p}") for p in range(PB)]
    v_product, v_copied, padded = ph.sem("v_product"), ph.sem("v_copied"), ph.sem("padded")
    items = [(mt, tb) for tb in range(TOK // QB) for mt in range(tiles)]
    with nc.Block() as block:
        @block.sync
        def _(sp):
            for n, (mt, tb) in enumerate(items):
                sp.wait_ge(low2, n + 1)
                sp.dma_start(scr[:, mt * P:(mt + 1) * P, tb * QB:(tb + 1) * QB].rearrange("s p n -> p s n"),
                             parts[:, n % PB, :, :]).then_inc(stored[n % PB], 16)
            for par in range(PB):
                sp.wait_ge(stored[par], 16 * (len(items) // PB))

        @block.tensor
        def _(pe):
            pe.wait_ge(loaded, 64)
            for n, (mt, tb) in enumerate(items):
                if n >= 2:
                    pe.wait_ge(turned, 2 * (n - 1))
                for s in range(2):
                    for k in range(KC):
                        col = (s * tiles + mt) * P
                        last = pe.matmul(m.ps[:, 2 * (n % 2) + s, :], w[:, k, col:col + P],
                                         m.xnT[:, k, tb * QB:(tb + 1) * QB], start=(k == 0), stop=(k == KC - 1))
                last.then_inc(product, 1)
            for t in range(TILES):
                if t >= 4:
                    pe.wait_ge(v_copied, t - 3)
                for k in range(KC):
                    last = pe.matmul(m.ps[:, 4 + t % 4, 0:kv * hd], m.xnT[:, k, t * P:(t + 1) * P], wv[:, k, :],
                                     start=(k == 0), stop=(k == KC - 1))
                last.then_inc(v_product, 1)

        @block.vector
        def _(dve):
            def rotate(n):
                mt, tb = items[n]
                at, a = (tb * QB) % T, n % 2
                dve.wait_ge(product, n + 1)
                dve.tensor_tensor(tc[:, a, :], m.ps[:, 2 * a, :], cos[:, at:at + QB], ALU.mult).then_inc(turned, 1)
                dve.tensor_tensor(ts[:, a, :], m.ps[:, 2 * a + 1, :], sin[:, at:at + QB], ALU.mult).then_inc(turned, 1)

            def add(n):
                a = n % 2
                dve.wait_ge(turned, 2 * n + 2)
                if n >= 2:
                    dve.wait_ge(high, n - 1)
                dve.tensor_tensor(r[:, a, :], tc[:, a, :], ts[:, a, :], ALU.add).then_inc(summed, 1)

            def remainder(n):
                a = n % 2
                dve.wait_ge(high, n + 1)
                dve.wait_ge(summed, n + 1)
                if n >= 2:
                    dve.wait_ge(low2, n - 1)
                dve.tensor_tensor(rest[:, a, :], r[:, a, :], parts[:, n % PB, 0, :], ALU.subtract).then_inc(low1, 1)

            if vpad > hd:
                dve.memset(v_sb[:], 1.0).then_inc(padded, 1)
            dve.wait_ge(loaded, 64)
            for n in range(len(items)):
                rotate(n)
                if n >= 1:
                    remainder(n - 1)
                add(n)
            remainder(len(items) - 1)

        @block.gpsimd
        def _(pool):
            for n in range(len(items)):
                a = n % 2
                pool.wait_ge(mid, n + 1)
                pool.tensor_tensor(parts[:, n % PB, 2, :], rest[:, a, :], parts[:, n % PB, 1, :],
                                   ALU.subtract).then_inc(low2, 1)

        @block.scalar
        def _(act):
            def first_part(n):
                a = n % 2
                act.wait_ge(summed, n + 1)
                if n >= PB:
                    act.wait_ge(stored[n % PB], 16 * (n // PB))
                act.copy(parts[:, n % PB, 0, :], r[:, a, :]).then_inc(high, 1)

            def second_part(n):
                act.wait_ge(low1, n + 1)
                act.copy(parts[:, n % PB, 1, :], rest[:, n % 2, :]).then_inc(mid, 1)

            for n in range(len(items)):
                first_part(n)
                if n >= 1:
                    second_part(n - 1)
            second_part(len(items) - 1)
            if vpad > hd:
                act.wait_ge(padded, 1)
            for t in range(TILES):
                act.wait_ge(v_product, t + 1)
                act.copy(v_sb[:, t, :, 0:hd],
                         m.ps[:, 4 + t % 4, 0:kv * hd].rearrange("p (h d) -> p h d", h=kv)).then_inc(v_copied, 1)
    ph.close()


Q_PARTS = (0, 0, 0, 1, 1, 2)
K_PARTS = (0, 1, 2, 0, 1, 0)
HG = 4
GB = 16 // HG


def pipelined(e, ops, per, iters, lead=8):
    def slot(i, s, end):
        for lag, fn in ops:
            if 0 <= s - lag < end:
                fn(i, s - lag)

    assert max(lag for lag, _ in ops) < lead <= per
    for s in range(lead):
        slot(0, s, per)
    with e.Fori(0, iters - 1) as i:
        for s in range(lead, per + lead):
            slot(i, s, per + lead)
    for s in range(lead, per + max(lag for lag, _ in ops)):
        slot(iters - 1, s, per)


def wait(e, sem, i, each, k):
    if isinstance(i, int):
        if i * each + k > 0:
            e.wait_ge(sem, i * each + k)
    else:
        assert k > 0
        e.wait_ge(sem, i * each + k)


def keep_warm(pe, m, bank, count):
    for _ in range(count):
        pe.matmul(m.ps[:, bank, :], m.ident_b[:], m.warm[:], start=True, stop=True)


def attention(nc, m, tag, scr, v_sb, wo_d, hd, kv_in_group, q_rows, scale, softcap):
    ph = Phase(nc, tag)
    plain = not softcap
    stacks = 1 if 6 * hd <= 96 else 2
    per = 6 // stacks
    rows = per * hd
    aug = 3 if plain else 0
    ER = 4
    wo = ph.sb("wo", [P, GB, C])
    q_st = ph.sb("q_st", [rows + aug, 2, HG, stacks, T], BF16)
    k_st = ph.sb("k_st", [rows + aug, 2, kv_in_group, stacks, T], BF16)
    v_st = ph.sb("v_st", [P, 2, BT, kv_in_group, 32])
    e = ph.sb("e", [P, ER, HG, QB])
    y = ph.sb("y", [P, QB])
    rz = ph.sb("rz", [P, QB])
    y_raw = ph.sb("y_raw", [P, QB])
    if plain:
        q_row = ph.sb("q_row", [rows, 2, HG, T], BF16)
        k_row = ph.sb("k_row", [rows, 2, T], BF16)
        nm = ph.sb("nm", [P, 2, HG, BT])
        nm_two = ph.sb("nm_two", [P, HG, 2, 4])
        nmT = ph.sb("nmT", [HG * BT, P])
        nmp = ph.sb("nmp", [HG * BT, 3, P], BF16)
        spread = ph.sb("spread", [P, P])
    else:
        ones = ph.sb("ones", [P, 32])
        z_raw = ph.sb("z_raw", [P, QB])
        e_sum = ph.sb("e_sum", [P, 2, HG, QB])
    wo_loaded, ones_set = ph.sem("wo_loaded"), ph.sem("ones_set")
    staged, row_staged = [ph.sem("staged0"), ph.sem("staged1")], [ph.sem("row_staged0"), ph.sem("row_staged1")]
    s_ready = [ph.sem("s_ready0"), ph.sem("s_ready1")]
    s_read = [ph.sem("s_read0"), ph.sem("s_read1")]
    exped, masked, weighed = ph.sem("exped"), ph.sem("masked"), ph.sem("weighed")
    z_copied, raw_copied, z_spread, accrued = ph.sem("z_copied"), ph.sem("raw_copied"), ph.sem("z_spread"), ph.sem("accrued")
    inverse, y_scaled, o_ready, o_added = ph.sem("inverse"), ph.sem("y_scaled"), ph.sem("o_ready"), ph.sem("o_added")
    row_scores, row_max, max_turned = ph.sem("row_scores"), ph.sem("row_max"), ph.sem("max_turned")
    max_step, max_staged = ph.sem("max_step"), ph.sem("max_staged")
    steps = [(qb, kt) for qb in range(T // QB) for kt in range((qb + 1) * QB // P)]
    NS, NQ = len(steps), T // QB
    PER, ITERS = 2 * NS, B * GB // 2
    ends = {s: qb for s, (qb, kt) in enumerate(steps) if kt == (qb + 1) * QB // P - 1}
    share = HG // kv_in_group
    N_DMA, SPLIT = 13, 6
    PIECES = 12
    ROW_BANKS = (3, 5, 6)
    n4 = lambda u, k: 4 * u + k
    lo_of = lambda qb, kt: max(kt * P - qb * QB, 0)

    def place(u):
        g, s = u // NS, u % NS
        return g, g % 2, s, *steps[s], lo_of(*steps[s])

    def piece(n):
        h, r = n // PIECES, n % PIECES
        if r < 4:
            return h, r, 0, (r + 1) * P, None
        t, c = 4 + (r - 4) // 2, (r - 4) % 2
        return h, t, c * QB, QB if c == 0 else (t - 3) * P, c

    with nc.Block() as block:
        @block.sync
        def _(sp):
            sp.dma_start(wo[:], wo_d.rearrange("(j p) n -> p j n", p=P)).then_inc(wo_loaded, 16)

            def stage(g):
                b, j, par = g // GB, g % GB, g % 2
                tok = slice(b * T, (b + 1) * T)
                for n in range(6):
                    row, st = (n % per) * hd, n // per
                    sp.dma_start(q_st[row:row + hd, par, :, st, :],
                                 scr[Q_PARTS[n], j * HG * hd:(j + 1) * HG * hd, tok]
                                 .rearrange("(h d) t -> d h t", d=hd)).then_inc(staged[par], 16)
                    k0 = q_rows + j * kv_in_group * hd
                    sp.dma_start(k_st[row:row + hd, par, :, st, :],
                                 scr[K_PARTS[n], k0:k0 + kv_in_group * hd, tok]
                                 .rearrange("(h d) t -> d h t", d=hd)).then_inc(staged[par], 16)
                sp.dma_start(v_st[:, par, :, :, :], v_sb[:, b * BT:(b + 1) * BT,
                                                         j * kv_in_group:(j + 1) * kv_in_group, :]).then_inc(staged[par], 16)

            def stage_rows(g):
                b, j, par = g // GB, g % GB, g % 2
                tok = slice(b * T, (b + 1) * T)
                for n in range(6):
                    sp.dma_start(q_row[n * hd:(n + 1) * hd, par, :, :],
                                 scr[Q_PARTS[n], j * HG * hd:(j + 1) * HG * hd, tok]
                                 .rearrange("(h d) t -> d h t", d=hd)).then_inc(row_staged[par], 16)
                    k0 = q_rows + j * hd
                    sp.dma_start(k_row[n * hd:(n + 1) * hd, par, :],
                                 scr[K_PARTS[n], k0:k0 + hd, tok]).then_inc(row_staged[par], 16)

            if plain:
                stage_rows(0)
                stage_rows(1)
            for g in range(B * GB):
                if g >= 2:
                    sp.wait_ge(weighed, (g - 1) * NS)
                stage(g)
                if plain:
                    sp.wait_ge(max_step, SPLIT * (g + 1))
                    for s in range(3):
                        sp.dma_start(q_st[rows + s:rows + s + 1, g % 2, :, 0, :], nmp[:, s, :]).then_inc(max_staged, 16)
                    if g + 2 < B * GB:
                        stage_rows(g + 2)

        @block.tensor
        def _(pe):
            pe.wait_ge(ones_set, 3 if plain else 1)
            pe.wait_ge(wo_loaded, 16)

            def row_piece(k):
                def run(i, u):
                    g, par, s, *_ = place(u)
                    n = 4 * s + k
                    h, t, key, keys, c = piece(n)
                    if n == 0:
                        pe.wait_ge(row_staged[par], i * (12 * 16) + (g // 2 + 1) * 12 * 16)
                    bank = ROW_BANKS[n4(u, k) % 3]
                    wait(pe, row_max, i, 4 * PER, n4(u, k) - 2)
                    last = pe.matmul(m.ps[:, bank, 0:keys], q_row[:, par, h, t * P:(t + 1) * P],
                                     k_row[:, par, key:key + keys], start=True, stop=True)
                    if c != 0:
                        last = pe.matmul(m.ps[:, bank, keys - P:keys], m.ident_b[:], m.later_k[:],
                                         start=False, stop=True, skip_group_check=True)
                    last.then_inc(row_scores, 1)
                return run

            def turn_maxima(i, u):
                g, par, s, *_ = place(u)
                if s == NS - 1:
                    wait(pe, max_step, i, 2 * SPLIT, g * SPLIT + 1)
                    wait(pe, o_added, i, 4 * NQ, 2 * (g - 1) * NQ + 2)
                    pe.transpose(m.ps[0:HG * BT, 7, 0:P], nm[:, par].rearrange("p h t -> p (h t)"), m.ident[:]).then_inc(max_turned, 1)

            def scores(p):
                def run(i, u):
                    g, par, s, qb, kt, lo = place(u)
                    if s == 0 and p == 0:
                        pe.wait_ge(staged[par], i * (16 * N_DMA) + (g // 2 + 1) * 16 * N_DMA)
                        if plain:
                            pe.wait_ge(max_staged, i * 96 + (g + 1) * 48)
                    if not plain:
                        wait(pe, s_read[p], i, PER, u)
                    for h in (2 * p, 2 * p + 1):
                        bank = n4(u, h) % 3 if plain else h
                        if plain:
                            wait(pe, s_read[0], i, 4 * PER, n4(u, h) - 2)
                        for st in range(stacks):
                            last = pe.matmul(m.ps[:, bank, lo:QB], k_st[:, par, h // share, st, kt * P:(kt + 1) * P],
                                             q_st[:, par, h, st, qb * QB + lo:(qb + 1) * QB],
                                             start=(st == 0), stop=(st == stacks - 1))
                        if plain and kt * P >= qb * QB:
                            last = pe.matmul(m.ps[:, bank, lo:lo + P], m.ident_b[:], m.later_q[:],
                                             start=False, stop=True, skip_group_check=True)
                        if plain:
                            last.then_inc(s_ready[0], 1)
                    if not plain:
                        last.then_inc(s_ready[p], 1)
                return run

            def weigh(i, u):
                g, par, s, qb, kt, lo = place(u)
                if plain:
                    wait(pe, s_read[0], i, 4 * PER, 4 * u + 4)
                else:
                    wait(pe, exped, i, PER, u + 1)
                if kt * P >= qb * QB and not plain:
                    wait(pe, masked, i, 2 * BT, g * BT + kt + 1)
                if kt == 0:
                    wait(pe, raw_copied, i, 2 * NQ, g * NQ + qb)
                for h in range(HG):
                    last = pe.matmul(m.ps[32 * h:32 * h + 32, 4, lo:QB], v_st[:, par, kt, h // share, :],
                                     e[:, u % ER, h, lo:QB], start=(kt == 0), stop=(s in ends))
                last.then_inc(weighed, 1)

            def denominators(i, u):
                g, par, s, qb, *_ = place(u)
                if s in ends:
                    wait(pe, accrued, i, PER, u + 1)
                    wait(pe, z_copied, i, 2 * NQ, g * NQ + qb)
                    for h in range(HG):
                        last = pe.matmul(m.ps[32 * h:32 * h + 32, 5, :], ones[:], e_sum[:, qb % 2, h, :],
                                         start=True, stop=True)
                    last.then_inc(z_spread, 1)

            def spread_z(i, u):
                g, par, s, qb, *_ = place(u)
                if s in ends:
                    wait(pe, raw_copied, i, 2 * NQ, g * NQ + qb + 1)
                    wait(pe, o_added, i, 4 * NQ, 2 * (g * NQ + qb))
                    if qb == 0 or g == 0 or not isinstance(i, int):
                        wait(pe, max_step, i, 2 * SPLIT, (g + qb) * SPLIT + 2)
                    pe.matmul(m.ps[:, 7, :], spread[:], y_raw[:], start=True, stop=True).then_inc(z_spread, 1)

            def project(half):
                def run(i, u):
                    g, par, s, qb, *_ = place(u)
                    if s not in ends:
                        return
                    bank = 7 if plain else 6 + half
                    wait(pe, y_scaled, i, 2 * NQ, g * NQ + qb + 1)
                    wait(pe, o_added, i, 4 * NQ, 2 * (g * NQ + qb) + half - (0 if plain else 1))
                    j = (i % 2) * 2 + g if isinstance(i, int) else (i + g // 2) % 2 * 2 + par
                    w = wo[:, j % GB, :] if isinstance(i, int) else wo[:, ds(j, 1), :].rearrange("p o c -> p (o c)")
                    for t in range(2):
                        q = (2 * half + t) * P
                        last = pe.matmul(m.ps[:, bank, t * C:(t + 1) * C], y[:, q:q + P], w, start=True, stop=True)
                    last.then_inc(o_ready, 1)
                return run

            if plain:
                pipelined(pe, [(2, turn_maxima), (0, row_piece(0)), (0, row_piece(1)), (15, scores(0)),
                               (0, row_piece(2)), (17, weigh), (15, scores(1)), (0, row_piece(3)), (18, spread_z),
                               (20, project(0)), (21, project(1))], PER, ITERS, lead=24)
            else:
                pipelined(pe, [(4, denominators), (0, scores(0)), (3, weigh), (0, scores(1)),
                               (7, project(0)), (8, project(1))], PER, ITERS, lead=12)


        @block.scalar
        def _(act):
            def from_scores(i, u):
                g, par, s, qb, kt, lo = place(u)
                wait(act, weighed, i, PER, u - ER + 1)
                if not plain:
                    wait(act, accrued, i, PER, u - ER + 1)
                if plain:
                    for h in range(HG):
                        wait(act, s_ready[0], i, 4 * PER, n4(u, h) + 1)
                        act.activation(e[:, u % ER, h, lo:QB], m.ps[:, n4(u, h) % 3, lo:QB], ACT.Exp,
                                       scale=scale).then_inc(s_read[0], 1)
                    return
                for p in range(2):
                    wait(act, s_ready[p], i, PER, u + 1)
                    act.activation(e[:, u % ER, 2 * p:2 * p + 2, lo:QB], m.ps[:, 2 * p:2 * p + 2, lo:QB], ACT.Tanh,
                                   scale=scale / softcap).then_inc(s_read[p], 1)

            def exponential(i, u):
                g, par, s, qb, kt, lo = place(u)
                wait(act, s_read[1], i, PER, u + 1)
                tile = e[:, u % ER, :, lo:QB]
                act.activation(tile, tile, ACT.Exp, scale=softcap).then_inc(exped, 1)

            def copy_raw(i, u):
                g, par, s, qb, *_ = place(u)
                if s in ends:
                    wait(act, weighed, i, PER, u + 1)
                    wait(act, y_scaled, i, 2 * NQ, g * NQ + qb)
                    act.copy(y_raw[:], m.ps[:, 4, :]).then_inc(raw_copied, 1)

            if plain:
                pipelined(act, [(15, from_scores), (17, copy_raw)], PER, ITERS, lead=24)
            else:
                pipelined(act, [(0, from_scores), (1, exponential)], PER, ITERS)

        @block.gpsimd
        def _(pool):
            if plain:
                pool.memset(k_st[rows:rows + aug, :, :, :, :], 1.0).then_inc(ones_set, 1)
                pool.wait_ge(ones_set, 1)
                pool.memset(spread[:], 0.0).then_inc(ones_set, 1)
                pool.wait_ge(ones_set, 2)
                sel = spread[:].rearrange("p (h r) -> p h r", r=32)
                pool.affine_select(out=sel, in_=sel, compare_op=ALU.not_equal, fill=1.0, base=-16,
                                   pattern=[[-32, HG], [0, 32]], channel_multiplier=1).then_inc(ones_set, 1)
            else:
                pool.memset(ones[:], 1.0).then_inc(ones_set, 1)

                def mask(i, u):
                    g, par, s, qb, kt, lo = place(u)
                    if kt * P >= qb * QB:
                        wait(pool, exped, i, PER, u + 1)
                        tile = e[:, u % ER, :, lo:lo + P]
                        pool.tensor_tensor(tile, tile, m.keep[:, None, :].to_broadcast([P, HG, P]),
                                           ALU.mult).then_inc(masked, 1)

                pipelined(pool, [(1, mask)], PER, ITERS)

        @block.vector
        def _(dve):
            def maxima(i, u):
                g, par, s, *_ = place(u)
                for k in range(4):
                    h, t, key, keys, c = piece(4 * s + k)
                    if 4 * s + k == 0:
                        wait(dve, max_turned, i, 2, g - 1)
                    wait(dve, row_scores, i, 4 * PER, 4 * u + k + 1)
                    dst = nm[:, par, h, t:t + 1] if c is None else nm_two[:, h, c, t - 4:t - 3]
                    dve.tensor_reduce(dst, m.ps[:, ROW_BANKS[n4(u, k) % 3], 0:keys], AX.X, ALU.max, negate=True).then_inc(row_max, 1)

            def join_maxima(i, u):
                g, par, s, *_ = place(u)
                if s == NS - 1:
                    wait(dve, row_max, i, 4 * PER, 4 * u + 4)
                    dve.tensor_tensor(nm[:, par, :, 4:8], nm_two[:, :, 0, :], nm_two[:, :, 1, :],
                                      ALU.min).then_inc(max_step, 1)

            def split_maxima(i, u):
                g, par, s, *_ = place(u)
                if s != NS - 1:
                    return
                step = lambda k: wait(dve, max_step, i, 2 * SPLIT, g * SPLIT + k)
                wait(dve, max_staged, i, 96, g * 48)
                wait(dve, max_turned, i, 2, g + 1)
                dve.tensor_copy(nmT[:], m.ps[0:HG * BT, 7, 0:P]).then_inc(max_step, 1)
                step(2)
                dve.tensor_copy(nmp[:, 0, :], nmT[:]).then_inc(max_step, 1)
                step(3)
                dve.tensor_tensor(nmT[:], nmT[:], nmp[:, 0, :], ALU.subtract).then_inc(max_step, 1)
                step(4)
                dve.tensor_copy(nmp[:, 1, :], nmT[:]).then_inc(max_step, 1)
                step(5)
                dve.tensor_tensor(nmp[:, 2, :], nmT[:], nmp[:, 1, :], ALU.subtract).then_inc(max_step, 1)

            def accrue(i, u):
                g, par, s, qb, kt, lo = place(u)
                wait(dve, exped, i, PER, u + 1)
                if kt * P >= qb * QB:
                    wait(dve, masked, i, 2 * BT, g * BT + kt + 1)
                total, tile = e_sum[:, qb % 2, :, lo:QB], e[:, u % ER, :, lo:QB]
                if kt == 0:
                    wait(dve, z_spread, i, 2 * NQ, g * NQ + qb - 1)
                    dve.tensor_copy(total, tile).then_inc(accrued, 1)
                else:
                    wait(dve, accrued, i, PER, u)
                    dve.tensor_tensor(total, total, tile, ALU.add).then_inc(accrued, 1)

            def read_y(i, u):
                g, par, s, qb, *_ = place(u)
                if s in ends:
                    wait(dve, weighed, i, PER, u + 1)
                    wait(dve, y_scaled, i, 2 * NQ, g * NQ + qb)
                    dve.tensor_copy(y_raw[:], m.ps[:, 4, :]).then_inc(raw_copied, 1)

            def read_z(i, u):
                g, par, s, qb, *_ = place(u)
                if s in ends:
                    wait(dve, z_spread, i, 2 * NQ, g * NQ + qb + 1)
                    dve.tensor_copy(z_raw[:], m.ps[:, 5, :]).then_inc(z_copied, 1)

            def invert(part, parts):
                def run(i, u):
                    g, par, s, qb, *_ = place(u)
                    if s in ends:
                        n = g * NQ + qb
                        if plain:
                            wait(dve, z_spread, i, 2 * NQ, n + 1)
                        else:
                            wait(dve, z_copied, i, 2 * NQ, n + 1)
                        wait(dve, y_scaled, i, 2 * NQ, n)
                        cols = slice(part * QB // parts, (part + 1) * QB // parts)
                        dve.reciprocal(rz[:, cols], m.ps[:, 7, cols] if plain else z_raw[:, cols]).then_inc(inverse, 1)
                return run

            def normalise(parts):
                def run(i, u):
                    g, par, s, qb, *_ = place(u)
                    if s in ends:
                        n = g * NQ + qb
                        wait(dve, inverse, i, 2 * NQ * parts, (n + 1) * parts)
                        wait(dve, o_ready, i, 4 * NQ, 2 * n)
                        dve.tensor_tensor(y[:], y_raw[:], rz[:], ALU.mult).then_inc(y_scaled, 1)
                return run

            def add(half):
                def run(i, u):
                    g, par, s, qb, *_ = place(u)
                    if s not in ends:
                        return
                    wait(dve, o_ready, i, 4 * NQ, 2 * (g * NQ + qb) + half + 1)
                    b = (i * 2 + g) // GB if isinstance(i, int) else (i + g // 2) // 2
                    rows_x = m.x[:, ds(b * BT + (qb * 4 + 2 * half), 2), :]
                    dve.tensor_tensor(rows_x, rows_x, m.ps[:, 7 if plain else 6 + half, :]
                                      .rearrange("p (t c) -> p t c", c=C), ALU.add).then_inc(o_added, 1)
                return run

            if plain:
                pipelined(dve, [(0, maxima), (18, invert(0, 4)), (18, invert(1, 4)), (19, invert(2, 4)), (19, invert(3, 4)),
                                (19, normalise(4)), (20, add(0)), (21, add(1)), (0, join_maxima), (2, split_maxima)],
                          PER, ITERS, lead=24)
            else:
                pipelined(dve, [(3, accrue), (3, read_y), (4, read_z), (4, invert(0, 4)), (5, invert(1, 4)), (6, invert(2, 4)),
                                (6, invert(3, 4)), (6, normalise(4)), (7, add(0)), (8, add(1))], PER, ITERS, lead=12)
    ph.close()


def in_blocks(e, n, body):
    body(0)
    with e.Fori(1, n) as i:
        body(i)


def wait_from(e, sem, i, each, k=0):
    assert k >= 0
    if not isinstance(i, int) or i * each + k > 0:
        e.wait_ge(sem, i * each + k)


def relu_ffn(nc, m, tag, w1_d, b1_d, w2_d, b2_d, w3_d, b3_d):
    ph = Phase(nc, tag)
    H = 512
    HT = H // P
    w1 = ph.sb("w1", [P, KC, H])
    w2 = ph.sb("w2", [P, HT, H])
    w3 = ph.sb("w3", [P, HT, C])
    b1 = ph.sb("b1", [P, HT])
    b2 = ph.sb("b2", [P, HT])
    b3 = ph.sb("b3", [P, C])
    loaded = ph.sem("loaded")

    def loads(sp):
        sp.dma_start(w1[:], w1_d.rearrange("(k p) n -> p k n", p=P)).then_inc(loaded, 16)
        sp.dma_start(w2[:], w2_d.rearrange("(k p) n -> p k n", p=P)).then_inc(loaded, 16)
        sp.dma_start(w3[:], w3_d.rearrange("(k p) n -> p k n", p=P)).then_inc(loaded, 16)
        sp.dma_start(b1[:], b1_d).then_inc(loaded, 16)
        sp.dma_start(b2[:], b2_d).then_inc(loaded, 16)
        sp.dma_start(b3[:], b3_d.partition_broadcast(P)).then_inc(loaded, 16)

    norm_transpose(nc, m, tag + "n", loads=loads)
    h1 = ph.sb("h1", [P, HT, QB])
    h2 = ph.sb("h2", [P, HT, QB])
    b3_added = ph.sem("b3_added")
    p1, p2, p3 = ph.sem("p1"), ph.sem("p2"), ph.sem("p3")
    r1, r2, added = ph.sem("r1"), ph.sem("r2"), ph.sem("added")
    NB = TOK // QB
    with nc.Block() as block:
        @block.gpsimd
        def _(pool):
            pool.wait_ge(loaded, 96)
            for t in range(TILES):
                pool.tensor_tensor(m.x[:, t, :], m.x[:, t, :], b3[:], ALU.add).then_inc(b3_added, 1)

        @block.tensor
        def _(pe):
            pe.wait_ge(loaded, 96)
            def block_of(i):
                for o in range(HT):
                    wait_from(pe, r1, i, HT)
                    for k in range(KC):
                        last = pe.matmul(m.ps[:, o, :], w1[:, k, o * P:(o + 1) * P], m.xnT[:, k, ds(i * QB, QB)],
                                         start=(k == 0), stop=(k == KC - 1))
                    last.then_inc(p1, 1)
                for o in range(HT):
                    wait_from(pe, added, i, HT)
                    for k in range(HT):
                        if o == 0:
                            wait_from(pe, r1, i, HT, k + 1)
                        last = pe.matmul(m.ps[:, 4 + o, :], w2[:, k, o * P:(o + 1) * P], h1[:, k, :],
                                         start=(k == 0), stop=(k == HT - 1))
                    last.then_inc(p2, 1)
                wait_from(pe, r2, i, HT, HT)
                for t in range(HT):
                    for k in range(HT):
                        last = pe.matmul(m.ps[:, 4 + t, 0:C], h2[:, k, t * P:(t + 1) * P], w3[:, k, :],
                                         start=(k == 0), stop=(k == HT - 1))
                    last.then_inc(p3, 1)

            in_blocks(pe, NB, block_of)

        @block.scalar
        def _(act):
            act.wait_ge(loaded, 96)
            def block_of(i):
                for o in range(HT):
                    wait_from(act, p1, i, HT, o + 1)
                    if o == 0:
                        wait_from(act, p2, i, HT)
                    act.activation(h1[:, o, :], m.ps[:, o, :], ACT.Relu, bias=b1[:, o:o + 1]).then_inc(r1, 1)
                for o in range(HT):
                    wait_from(act, p2, i, HT, o + 1)
                    if o == 0:
                        wait_from(act, p3, i, HT)
                    act.activation(h2[:, o, :], m.ps[:, 4 + o, :], ACT.Relu, bias=b2[:, o:o + 1]).then_inc(r2, 1)

            in_blocks(act, NB, block_of)

        @block.vector
        def _(dve):
            dve.wait_ge(b3_added, TILES)
            def block_of(i):
                for t in range(HT):
                    wait_from(dve, p3, i, HT, t + 1)
                    row = m.x[:, ds(i * HT + t, 1), :]
                    dve.tensor_tensor(row, row, m.ps[:, 4 + t:5 + t, 0:C], ALU.add).then_inc(added, 1)

            in_blocks(dve, NB, block_of)
    ph.close()


MLP = 2048


def gated_ffn(nc, m, a, tag, unpack):
    ph = Phase(nc, tag)
    NT, NB, NCHUNK = MLP // P, TOK // QB, MLP // C
    loaded, converted = ph.sem("loaded"), ph.sem("converted")
    if unpack:
        packed = ph.sb("packed", [P, 3, MLP], I32)
        scale = ph.sb("scale", [P, 3, MLP])

    def loads(sp):
        sp.dma_start(packed[:, 0, :], a["gate_p"]).then_inc(loaded, 16)
        sp.dma_start(packed[:, 1, :], a["up_p"]).then_inc(loaded, 16)
        sp.dma_start(packed[:, 2, :].rearrange("p (m h) -> p m h", m=8),
                     a["down_p"].rearrange("(m p) h -> p m h", p=P)).then_inc(loaded, 16)
        for k in range(8):
            rows = slice(16 * k, 16 * k + 16)
            for w, name in enumerate(("gate_s", "up_s", "down_s")):
                sp.dma_start(scale[rows, w, :], a[name][k].partition_broadcast(16)).then_inc(loaded, 16)

    norm_transpose(nc, m, tag + "n", interleave=True, loads=loads if unpack else None)
    ge = ph.sb("ge", [P, 2, QB])
    it = ph.sb("it", [P, 2, QB])
    if unpack:
        code = ph.sb("code", [P, 2, 3, C], I32)
        sign = ph.sb("sign", [P, 2, 3, C], I32)
        val = ph.sb("val", [P, 2, 3, C])
        factor = ph.sb("factor", [P, 2, 3, C])
    gate, up, gelued, gated, down, added = (ph.sem("gate"), ph.sem("up"), ph.sem("gelued"), ph.sem("gated"),
                                            ph.sem("down"), ph.sem("added"))
    step, signed, halved, factored = ph.sem("step"), ph.sem("signed"), ph.sem("halved"), ph.sem("factored")
    parts = [(c, odd) for c in range(NCHUNK) for odd in range(2)] if unpack else []
    columns = lambda t, c: t[:, :, c * C:(c + 1) * C]
    with nc.Block() as block:
        @block.tensor
        def _(pe):
            def first(i, n):
                cols = slice(n * P, (n + 1) * P)
                wait_from(pe, gated, i, NT, max(n - 1, 0))
                if unpack and isinstance(i, int) and n % 2 == 0:
                    pe.wait_ge(converted, n + 2)
                for w, bank, done in ((0, 0, gate), (1, 2, up)):
                    for k in range(2):
                        last = pe.matmul(m.ps[:, bank + n % 2, :], m.w[:, w, k, cols], m.xnT[:, k, ds(i * QB, QB)],
                                         start=(k == 0), stop=(k == 1))
                    last.then_inc(done, 1)

            def second(i, n):
                wait_from(pe, gated, i, NT, n + 1)
                if n == 0:
                    wait_from(pe, added, i, 4)
                for t in range(4):
                    last = pe.matmul(m.ps[:, 4 + t, 0:C], it[:, n % 2, t * P:(t + 1) * P],
                                     m.w[:, 2, n % 2, (n // 2) * C:(n // 2 + 1) * C],
                                     start=(n == 0), stop=(n == NT - 1))
                last.then_inc(down, 1)

            def block_of(i):
                first(i, 0)
                for n in range(NT):
                    if n + 1 < NT:
                        first(i, n + 1)
                    second(i, n)

            in_blocks(pe, NB, block_of)

        @block.scalar
        def _(act):
            def halve(p):
                act.wait_ge(signed, p + 1)
                if p >= 2:
                    act.wait_ge(converted, p - 1)
                act.activation(factor[:, p % 2], sign[:, p % 2], ACT.Copy, scale=-0.125, bias=0.5).then_inc(halved, 1)

            def block_of(i):
                for n in range(NT):
                    if unpack and isinstance(i, int) and n + 4 < len(parts):
                        halve(n + 4)
                    wait_from(act, gate, i, NT, n + 1)
                    if n >= 2:
                        wait_from(act, gated, i, NT, n - 1)
                    act.activation(ge[:, n % 2, :], m.ps[:, n % 2, :], ACT.Gelu_apprx_tanh).then_inc(gelued, 1)

            for p in range(min(4, len(parts))):
                halve(p)
            in_blocks(act, NB, block_of)

        @block.gpsimd
        def _(pool):
            for p, (c, odd) in enumerate(parts):
                if p == 0:
                    pool.wait_ge(loaded, 16 * 27)
                pool.wait_ge(halved, p + 1)
                pool.tensor_tensor(factor[:, p % 2], factor[:, p % 2], columns(scale, c), ALU.mult).then_inc(factored, 1)

        @block.vector
        def _(dve):
            def split_codes(p):
                c, odd = parts[p]
                if p >= 2:
                    dve.wait_ge(halved, p - 1)
                dve.tensor_scalar(sign[:, p % 2], columns(packed, c), 4 * odd, 8, ALU.logical_shift_right,
                                  ALU.bitwise_and).then_inc(signed, 1)
                dve.tensor_scalar(code[:, p % 2], columns(packed, c), 4 * odd, 7, ALU.logical_shift_right,
                                  ALU.bitwise_and).then_inc(step, 1)

            def convert(p):
                c, odd = parts[p]
                x, v = code[:, p % 2], val[:, p % 2]
                dve.wait_ge(step, 4 * p + 1)
                dve.scalar_tensor_tensor(v, x, 4.0, x, ALU.max, ALU.add).then_inc(step, 1)
                if p + 1 < len(parts):
                    split_codes(p + 1)
                else:
                    dve.sem_inc(step, 1)
                dve.wait_ge(step, 4 * p + 3)
                dve.scalar_tensor_tensor(v, x, 6.0, v, ALU.max, ALU.add).then_inc(step, 1)
                dve.wait_ge(step, 4 * p + 4)
                dve.scalar_tensor_tensor(v, x, 6.0, v, ALU.max, ALU.add).then_inc(step, 1)
                dve.wait_ge(step, 4 * p + 5)
                dve.wait_ge(factored, p + 1)
                dve.scalar_tensor_tensor(columns(m.w[:, :, odd, :], c), v, -16.0, factor[:, p % 2],
                                         ALU.add, ALU.mult).then_inc(converted, 1)

            def block_of(i):
                for n in range(NT):
                    if unpack and isinstance(i, int) and n + 4 < len(parts):
                        convert(n + 4)
                    wait_from(dve, gelued, i, NT, n + 1)
                    wait_from(dve, up, i, NT, n + 1)
                    if n >= 2:
                        wait_from(dve, down, i, NT, n - 1)
                    dve.tensor_tensor(it[:, n % 2, :], ge[:, n % 2, :], m.ps[:, 2 + n % 2, :],
                                      ALU.mult).then_inc(gated, 1)
                wait_from(dve, down, i, NT, NT)
                x_block = m.x[:, ds(i * 4, 4), :]
                dve.tensor_tensor(x_block, x_block, m.ps[:, 4:8, 0:C], ALU.add).then_inc(added, 4)

            if unpack:
                dve.wait_ge(loaded, 16 * 27)
                split_codes(0)
                for p in range(4):
                    convert(p)
            in_blocks(dve, NB, block_of)
    ph.close()


def diff_attention(nc, m, a, tag, scr, v_sb):
    ph = Phase(nc, tag)
    HD, U = 16, HG * BT
    QUADS = 2 * U // HG
    EB = 4
    PER, ITERS = 2 * U, GB
    q_st = ph.sb("q_st", [96, 2, 2 * HG, T], BF16)
    k_st = ph.sb("k_st", [96, 2, 2, T], BF16)
    v_st = ph.sb("v_st", [P, 2, BT, 32])
    lv = ph.sb("lv", [P, 4, 256])
    dots = ph.sb("dots", [P, 2, 16])
    nlam = ph.sb("nlam", [P, 16])
    nm = ph.sb("nm", [P, EB, 2])
    e = ph.sb("e", [P, EB, 2, T])
    z = ph.sb("z", [P, EB, 2])
    rz = ph.sb("rz", [P, EB, 2])
    c = ph.sb("c", [P, EB])
    t2 = ph.sb("t2", [P, 2, T])
    low = ph.sb("low", [P, EB])
    rz2 = ph.sb("rz2", [P, HG])
    pr = ph.sb("pr", [P, 2, T])
    prT = ph.sb("prT", [P, 2 * HG, T])
    outT = ph.sb("outT", [P, P])
    lam_loaded, lam_step = ph.sem("lam_loaded"), ph.sem("lam_step")
    staged = [ph.sem("staged0"), ph.sem("staged1")]
    two = lambda name: [ph.sem(name + "0"), ph.sem(name + "1")]
    scored, maxed, exped, copied = two("scored"), two("maxed"), two("exped"), two("copied")
    masked = ph.sem("masked")
    inv, coef, mixed, lowered = ph.sem("inv"), ph.sem("coef"), ph.sem("mixed"), ph.sem("lowered")
    p_done, turned, valued = ph.sem("p_done"), ph.sem("turned"), ph.sem("valued")
    out_copied, returned = ph.sem("out_copied"), ph.sem("returned")
    inv2, scaled, mixable = ph.sem("inv2"), ph.sem("scaled"), ph.sem("mixable")

    def place(u):
        b, t, h = (u // U) % 2, (u // HG) % BT, u % HG
        return b, h, t, (t + 1) * P

    def copier(u):
        return 0 if (u // HG) % BT < 4 and u % 2 == 0 else 1

    def copies(u, x):
        return sum(copier(v) == x for v in range(u))

    COPIES = (copies(2 * U, 0), copies(2 * U, 1))

    def short_second(u):
        return 1 if 1 <= u % U < U // 2 else 0

    with nc.Block() as block:
        @block.sync
        def _(sp):
            for n, name in enumerate(("lq1", "lk1", "lq2", "lk2")):
                sp.dma_start(lv[:, n, :], a[name].partition_broadcast(P)).then_inc(lam_loaded, 16)
            for g in range(2 * GB):
                if g >= 2:
                    sp.wait_ge(valued, BT * (g - 1))
                j, b = g // 2, g % 2
                tok = slice(b * T, (b + 1) * T)
                for n in range(6):
                    sp.dma_start(q_st[n * HD:(n + 1) * HD, b, :, :],
                                 scr[Q_PARTS[n], j * 128:(j + 1) * 128, tok]
                                 .rearrange("(h d) t -> d h t", d=HD)).then_inc(staged[b], 16)
                    sp.dma_start(k_st[n * HD:(n + 1) * HD, b, :, :],
                                 scr[K_PARTS[n], 512 + j * 32:512 + (j + 1) * 32, tok]
                                 .rearrange("(h d) t -> d h t", d=HD)).then_inc(staged[b], 16)
                sp.dma_start(v_st[:, b, :, :], v_sb[:, b * BT:(b + 1) * BT, j, :]).then_inc(staged[b], 16)

        @block.tensor
        def _(pe):
            def score(s):
                def run(i, u):
                    b, h, t, L = place(u)
                    if u % U == 0 and s == 0:
                        pe.wait_ge(staged[b], (i + u // PER) * (16 * 13) + 16 * 13)
                    wait(pe, exped[s], i, PER, u - short_second(u))
                    for cc in range(t // 4 + 1):
                        bank = 2 * s + (u % 2 if t < 4 else cc)
                        n = min(QB, L - cc * QB)
                        last = pe.matmul(m.ps[:, bank, 0:n], q_st[:, b, 2 * h + s, t * P:(t + 1) * P],
                                         k_st[:, b, s, cc * QB:cc * QB + n], start=True, stop=True)
                    last = pe.matmul(m.ps[:, bank, n - P:n], m.ident_b[:], m.later_k[:],
                                     start=False, stop=True, skip_group_check=True)
                    last.then_inc(scored[s], 1)
                return run

            def turn(i, u):
                b, h, t, L = place(u)
                for x in range(2):
                    wait(pe, copied[x], i, COPIES[x], copies(u - short_second(u), x))
                keep_warm(pe, m, 4 + (u % 2 if t < 4 else 0), 2)
                wait(pe, p_done, i, PER, u + 1)
                for kb in range(t + 1):
                    bank = 4 + (u % 2 if t < 4 else kb // 4)
                    last = pe.transpose(m.ps[:, bank, (kb % 4) * P:(kb % 4 + 1) * P],
                                        pr[:, u % 2, kb * P:(kb + 1) * P], m.ident[:])
                last.then_inc(turned, 1)

            def value(part):
                def run(i, u):
                    b, h, t, L = place(u)
                    if h != HG - 1:
                        return
                    if part == 0:
                        for x in range(2):
                            wait(pe, copied[x], i, COPIES[x], copies(u + 1, x))
                        wait(pe, out_copied, i, QUADS, u // HG)
                    for kb in range((t + 1) * part // 3, (t + 1) * (part + 1) // 3):
                        for hq in range(HG):
                            last = pe.matmul(m.ps[32 * hq:32 * hq + 32, 6, 0:P], v_st[:, b, kb, :],
                                             prT[:, (u - h + hq) % (2 * HG), kb * P:(kb + 1) * P],
                                             start=(kb == 0), stop=(kb == t))
                    if part == 2:
                        last.then_inc(valued, 1)
                return run

            def turn_back(i, u):
                if u % HG == HG - 1:
                    wait(pe, out_copied, i, QUADS, u // HG + 1)
                    wait(pe, scaled, i, QUADS, u // HG)
                    pe.transpose(m.ps[:, 7, 0:P], outT[:], m.ident[:]).then_inc(returned, 1)

            pipelined(pe, [(0, score(0)), (5, turn), (0, score(1)), (6, value(0)), (7, value(1)), (8, value(2)),
                           (10, turn_back)], PER, ITERS, lead=14)

        def copy_turned(e, x):
            def run(i, u):
                b, h, t, L = place(u)
                if copier(u) != x:
                    return
                wait(e, turned, i, PER, u + 1)
                wait(e, valued, i, QUADS, u // HG - 1)
                src = m.ps[:, 4 + u % 2, 0:L] if t < 4 else m.ps[:, 4:6, :].rearrange("p a n -> p (a n)")[:, 0:L]
                (e.copy if x else e.tensor_copy)(prT[:, u % (2 * HG), 0:L], src).then_inc(copied[x], 1)
            return run

        @block.scalar
        def _(act):
            act.wait_ge(lam_step, 2)
            act.activation(dots[:], dots[:], ACT.Exp).then_inc(lam_step, 1)

            def exps(s):
                def run(i, u):
                    b, h, t, L = place(u)
                    wait(act, maxed[s], i, PER, u + 1)
                    wait(act, lowered, i, PER, u - (EB - 1))
                    src = m.ps[:, 2 * s + u % 2, 0:L] if t < 4 else \
                        m.ps[:, 2 * s:2 * s + 2, :].rearrange("p a n -> p (a n)")[:, 0:L]
                    act.activation(e[:, u % EB, s, 0:L], src, ACT.Exp, bias=nm[:, u % EB, s:s + 1],
                                   accum_out=z[:, u % EB, s:s + 1]).then_inc(exped[s], 1)
                return run

            def softmax(i, u):
                b, h, t, L = place(u)
                wait(act, lowered, i, PER, u + 1)
                wait(act, turned, i, PER, u - 1)
                act.activation(pr[:, u % 2, 0:L], t2[:, u % 2, 0:L], ACT.Exp, bias=low[:, u % EB:u % EB + 1],
                               scale=-1.0).then_inc(p_done, 1)

            def copy_out(i, u):
                if u % HG == HG - 1:
                    wait(act, valued, i, QUADS, u // HG + 1)
                    wait(act, returned, i, QUADS, u // HG)
                    act.copy(outT[:], m.ps[:, 6, 0:P]).then_inc(out_copied, 1)

            pipelined(act, [(0, exps(0)), (4, softmax), (5, copy_turned(act, 1)), (0, exps(1)), (9, copy_out)],
                      PER, ITERS, lead=14)

        @block.gpsimd
        def _(pool):
            def mask(i, u):
                b, h, t, L = place(u)
                wait(pool, exped[0], i, PER, u + 1)
                tile = e[:, u % EB, 0, t * P:L]
                pool.tensor_tensor(tile, tile, m.later_k[:], ALU.add).then_inc(masked, 1)

            def scale_second(i, u):
                b, h, t, L = place(u)
                k = u % EB
                wait(pool, coef, i, 2 * PER, 2 * u + 1)
                pool.tensor_tensor(e[:, k, 1, 0:L], e[:, k, 1, 0:L], c[:, k:k + 1].to_broadcast([P, L]),
                                   ALU.mult).then_inc(mixed, 1)

            pipelined(pool, [(0, mask), (1, scale_second)], PER, ITERS, lead=14)

        @block.vector
        def _(dve):
            dve.wait_ge(lam_loaded, 64)
            dve.tensor_tensor(lv[:, 0, :], lv[:, 0, :], lv[:, 1, :], ALU.mult).then_inc(lam_step, 1)
            dve.tensor_tensor(lv[:, 2, :], lv[:, 2, :], lv[:, 3, :], ALU.mult).then_inc(inv, 1)
            dve.wait_ge(lam_step, 1)
            dve.wait_ge(inv, 1)
            dve.tensor_reduce(dots[:], lv[:, 0:4:2, :].rearrange("p n (h d) -> p n h d", d=HD), AX.X,
                              ALU.add).then_inc(lam_step, 1)
            dve.wait_ge(lam_step, 3)
            dve.tensor_tensor(nlam[:], dots[:, 1, :], dots[:, 0, :], ALU.subtract).then_inc(lam_step, 1)
            dve.wait_ge(lam_step, 4)
            dve.tensor_scalar(nlam[:], nlam[:], float(0.8 - 0.6 * float(np.exp(-0.3 * 0))), None,
                              ALU.subtract).then_inc(lam_step, 1)
            dve.wait_ge(lam_step, 5)

            def maxima(s):
                def run(i, u):
                    b, h, t, L = place(u)
                    wait(dve, scored[s], i, PER, u + 1)
                    src = m.ps[:, 2 * s + u % 2, 0:L] if t < 4 else \
                        m.ps[:, 2 * s:2 * s + 2, :].rearrange("p a n -> p (a n)")[:, 0:L]
                    dve.tensor_reduce(nm[:, u % EB, s:s + 1], src, AX.X, ALU.max, negate=True).then_inc(maxed[s], 1)
                return run

            def coefficients(i, u):
                hh = i * HG + (u % HG + HG * (u // PER))
                k = u % EB
                wait(dve, exped[0], i, PER, u + 1)
                wait(dve, exped[1], i, PER, u + 1)
                dve.reciprocal(rz[:, k, :], z[:, k, :]).then_inc(inv, 1)
                wait(dve, inv, i, PER, u + 2)
                dve.scalar_tensor_tensor(c[:, k:k + 1], rz[:, k, 1:2], nlam[:, ds(hh, 1)], z[:, k, 0:1],
                                         ALU.mult, ALU.mult).then_inc(coef, 1)
                dve.tensor_scalar(rz[:, k, 0:1], rz[:, k, 0:1], -1.0, None, ALU.mult).then_inc(coef, 1)

            def mix(i, u):
                b, h, t, L = place(u)
                k = u % EB
                wait(dve, coef, i, 2 * PER, 2 * u + 2)
                wait(dve, mixed, i, PER, u + 1)
                wait(dve, masked, i, PER, u + 1)
                wait(dve, p_done, i, PER, u - 1)
                dve.sem_inc(mixable, 1)
                dve.tensor_tensor_reduce(t2[:, u % 2, 0:L], e[:, k, 0, 0:L], e[:, k, 1, 0:L], rz[:, k, 0:1], 3.0e38,
                                         ALU.add, ALU.min, low[:, k:k + 1]).then_inc(lowered, 1)

            def result(i, u):
                b, h, t, L = place(u)
                if h != HG - 1:
                    return
                wait(dve, returned, i, QUADS, u // HG + 1)
                out = m.ps[:, 7, 0:P].rearrange("p (h d) -> p h d", h=HG)
                dve.reciprocal(rz2[:], out[:, :, HD]).then_inc(inv2, 1)
                wait(dve, inv2, i, QUADS, u // HG + 1)
                cols = ds((i + u // PER) * (HG * HD), HG * HD)
                dve.tensor_tensor(m.y_tok[:, b * BT + t, cols].rearrange("p (h d) -> p h d", h=HG), out[:, :, 0:HD],
                                  rz2[:, :, None].to_broadcast([P, HG, HD]), ALU.mult).then_inc(scaled, 1)

            pipelined(dve, [(0, maxima(0)), (3, mix), (5, copy_turned(dve, 0)), (1, coefficients), (0, maxima(1)),
                            (11, result)], PER, ITERS, lead=14)
    ph.close()


def norm_project(nc, m, tag, w_d, g_d, eps, factor, ttt=None):
    ph = Phase(nc, tag)
    w = ph.sb("w", [P, KC, C])
    g = ph.sb("g", [P, C])
    sq = ph.sb("sq", [P, TILES, C])
    mu = ph.sb("mu", [P, TILES, 16])
    ms = ph.sb("ms", [P, TILES, 16])
    yT = ph.sb("yT", [P, 2, KC, QB])
    eps_t = ph.sb("eps", [P, 2])
    loaded, step, eps_set = ph.sem("loaded"), ph.sem("step"), ph.sem("eps_set")
    y_loaded = [ph.sem(f"y_loaded{q}") for q in range(4)]
    centred, squared, summed, root = ph.sem("centred"), ph.sem("squared"), ph.sem("summed"), ph.sem("root")
    gained, based, squared2, summed2 = ph.sem("gained"), ph.sem("based"), ph.sem("squared2"), ph.sem("summed2")
    root2, ready = ph.sem("root2"), ph.sem("ready")
    turned, copied, product, added = ph.sem("turned"), ph.sem("copied"), ph.sem("product"), ph.sem("added")
    NQ = TILES // 4
    y = m.y_tok
    of = lambda t, q: t[:, 4 * q:4 * q + 4]
    heads = lambda t, q: of(t, q).rearrange("p t (h d) -> p t h d", d=16)
    wide = lambda t, q: of(t, q)[:, :, :, None].to_broadcast([P, 4, 16, 16])

    def slots(ops):
        for s in range(NQ + max(lag for lag, _ in ops)):
            for lag, fn in ops:
                if 0 <= s - lag < NQ:
                    fn(s - lag)

    with nc.Block() as block:
        @block.sync
        def _(sp):
            for q in range(NQ if ttt is not None else 0):
                sp.dma_start(of(y, q), ttt[q * QB:(q + 1) * QB, :].rearrange("(t p) n -> p t n", p=P)).then_inc(y_loaded[q], 16)
            sp.dma_start(w[:], w_d.rearrange("(k p) n -> p k n", p=P)).then_inc(loaded, 16)
            sp.dma_start(g[:], g_d.partition_broadcast(P)).then_inc(loaded, 16)

        @block.vector
        def _(dve):
            n = [0]

            def then(ins):
                n[0] += 1
                ins.then_inc(step, 1)
                dve.wait_ge(step, n[0])

            def centre(q):
                dve.wait_ge(y_loaded[q], 16)
                then(dve.tensor_reduce(of(mu, q), heads(y, q), AX.X, ALU.add))
                dve.scalar_tensor_tensor(heads(y, q), wide(mu, q), -1.0 / 16, heads(y, q),
                                         ALU.mult, ALU.add).then_inc(centred, 1)

            def variance(q):
                dve.wait_ge(squared, q + 1)
                dve.tensor_reduce(of(mu, q), heads(sq, q), AX.X, ALU.add).then_inc(summed, 1)

            def gain(q):
                dve.wait_ge(root, q + 1)
                then(dve.reciprocal(of(mu, q), of(mu, q)))
                then(dve.tensor_tensor(heads(y, q), heads(y, q), wide(mu, q), ALU.mult))
                dve.tensor_tensor(of(y, q), of(y, q), of(m.gain, q), ALU.mult).then_inc(gained, 1)

            def mean_square(q):
                dve.wait_ge(squared2, q + 1)
                dve.tensor_reduce(of(ms, q), heads(sq, q), AX.X, ALU.add).then_inc(summed2, 1)

            def scale(q):
                dve.wait_ge(root2, q + 1)
                then(dve.reciprocal(of(ms, q), of(ms, q)))
                if q == 0:
                    dve.wait_ge(loaded, 32)
                then(dve.scalar_tensor_tensor(of(sq, q), of(y, q), factor, g[:, None, :].to_broadcast([P, 4, C]),
                                              ALU.mult, ALU.mult))
                dve.tensor_tensor(heads(sq, q), heads(sq, q), wide(ms, q), ALU.mult).then_inc(ready, 1)

            def add(q):
                dve.wait_ge(product, q + 1)
                b = 4 + 2 * (q % 2)
                dve.tensor_tensor(of(m.x, q), of(m.x, q), m.ps[:, b:b + 2, :].rearrange("p a (t c) -> p (a t) c", c=C),
                                  ALU.add).then_inc(added, 1)

            dve.memset(eps_t[:, 0:1], eps).then_inc(eps_set, 1)
            if ttt is None:
                slots([(1, mean_square), (2, scale), (4, add)])
            else:
                slots([(0, centre), (1, variance), (2, gain), (4, mean_square), (5, scale), (7, add)])

        @block.gpsimd
        def _(pool):
            for q in range(NQ if ttt is not None else 0):
                pool.wait_ge(gained, q + 1)
                pool.tensor_tensor(of(y, q), of(y, q), of(m.base, q), ALU.add).then_inc(based, 1)

        @block.scalar
        def _(act):
            def square(q):
                act.wait_ge(centred, q + 1)
                act.activation(of(sq, q), of(y, q), ACT.Square).then_inc(squared, 1)

            def square_root(q):
                act.wait_ge(summed, q + 1)
                act.activation(of(mu, q), of(mu, q), ACT.Sqrt, scale=1.0 / 16, bias=eps_t[:, 0:1]).then_inc(root, 1)

            def square2(q):
                if ttt is not None:
                    act.wait_ge(based, q + 1)
                act.activation(of(sq, q), of(y, q), ACT.Square).then_inc(squared2, 1)

            def square_root2(q):
                act.wait_ge(summed2, q + 1)
                act.activation(of(ms, q), of(ms, q), ACT.Sqrt, scale=1.0 / 16, bias=eps_t[:, 0:1]).then_inc(root2, 1)

            def copy(q):
                act.wait_ge(turned, q + 1)
                if q >= 2:
                    act.wait_ge(product, q - 1)
                b = 2 * (q % 2)
                act.copy(yT[:, q % 2], m.ps[:, b:b + 2, :]).then_inc(copied, 1)

            act.wait_ge(eps_set, 1)
            if ttt is None:
                slots([(0, square2), (1, square_root2), (2, copy)])
            else:
                slots([(0, square), (1, square_root), (3, square2), (4, square_root2), (6, copy)])

        @block.tensor
        def _(pe):
            def turn(q):
                pe.wait_ge(ready, q + 1)
                if q >= 2:
                    pe.wait_ge(copied, q - 1)
                for k in range(KC):
                    for t in range(4):
                        last = pe.transpose(m.ps[:, 2 * (q % 2) + k, t * P:(t + 1) * P],
                                            sq[:, 4 * q + t, k * P:(k + 1) * P], m.ident[:])
                last.then_inc(turned, 1)

            def project(q):
                pe.wait_ge(copied, q + 1)
                if q >= 2:
                    pe.wait_ge(added, q - 1)
                for t in range(4):
                    for k in range(KC):
                        last = pe.matmul(m.ps[:, 4 + 2 * (q % 2) + t // 2, (t % 2) * C:(t % 2 + 1) * C],
                                         yT[:, q % 2, k, t * P:(t + 1) * P], w[:, k, :],
                                         start=(k == 0), stop=(k == KC - 1))
                last.then_inc(product, 1)

            pe.wait_ge(loaded, 32)
            slots([(0, turn), (1, project)])
    ph.close()


CH = 16
NCH = T // CH
NG = 4
HL = 8


def ttt_project(nc, m, a, tag):
    ph = Phase(nc, tag)
    w = ph.sb("w", [P, KC, 3 * C + 16])
    wg1 = ph.sb("wg1", [P, KC, 16])
    wg2 = ph.sb("wg2", [16, C])
    lw = ph.sb("lw", [P, 2, C])
    loaded = ph.sem("loaded")

    def loads(sp):
        sp.dma_start(w[:], a["w_t"].rearrange("(k p) n -> p k n", p=P)).then_inc(loaded, 16)
        sp.dma_start(wg1[:], a["wg1"].rearrange("(k p) n -> p k n", p=P)).then_inc(loaded, 16)
        sp.dma_start(wg2[:], a["wg2"]).then_inc(loaded, 16)
        sp.dma_start(lw[:, 0, :], a["ln_w"].partition_broadcast(P)).then_inc(loaded, 16)
        sp.dma_start(lw[:, 1, :], a["ln_b"].partition_broadcast(P)).then_inc(loaded, 16)

    norm_transpose(nc, m, tag + "n", loads=loads)
    g1T = ph.sb("g1T", [16, TOK])
    k = ph.sb("k", [P, TILES, 16, CH + 1])
    k_flat = ph.sb("k_flat", [P, TILES, C])
    v = ph.sb("v", [P, TILES, C])
    sq = ph.sb("sq", [P, C])
    kn = ph.sb("kn", [P, TILES, 16])
    g1, g1_copied = ph.sem("g1"), ph.sem("g1_copied")
    product, read_a, read_d = ph.sem("product"), ph.sem("read_a"), ph.sem("read_d")
    norm, root, keyed, acts = ph.sem("norm"), ph.sem("root"), ph.sem("keyed"), ph.sem("acts")
    target, turned, copied, stored = ph.sem("target"), ph.sem("turned"), ph.sem("copied"), ph.sem("stored")
    based = ph.sem("based")
    qT, kT = m.xnT, m.kT
    with nc.Block() as block:
        @block.gpsimd
        def _(pool):
            pool.wait_ge(acts, 2)
            pool.wait_ge(turned, 8)
            bc = lambda n: lw[:, n:n + 1, :].to_broadcast([P, TILES, C])
            pool.tensor_tensor(m.base[:], m.base[:], bc(1), ALU.add).then_inc(based, 1)
            pool.wait_ge(based, 1)
            pool.tensor_tensor(m.base[:], m.base[:], m.gain[:], ALU.mult).then_inc(based, 1)
            pool.wait_ge(based, 2)
            pool.tensor_tensor(m.gain[:], m.gain[:], bc(0), ALU.mult)

        @block.sync
        def _(sp):
            sp.wait_ge(acts, 3)
            sp.wait_ge(keyed, 1)
            sp.dma_start(a["scr_k"].rearrange("(t p) n -> p t n", p=P), k[:].rearrange("p t h d -> p t (h d)")).then_inc(stored, 16)
            for q in range(4):
                sp.wait_ge(target, TILES + q + 1)
                sp.dma_start(a["scr_t"][q * QB:(q + 1) * QB, :].rearrange("(t p) n -> p t n", p=P),
                             v[:, 4 * q:4 * q + 4, :]).then_inc(stored, 16)
            sp.wait_ge(stored, 16 * 5)

        @block.tensor
        def _(pe):
            pe.wait_ge(loaded, 80)
            for n in range(4):
                for c in range(KC):
                    last = pe.matmul(m.ps[0:16, n, :], wg1[:, c, :], m.xnT[:, c, n * QB:(n + 1) * QB],
                                     start=(c == 0), stop=(c == KC - 1))
            last.then_inc(g1, 1)
            pe.wait_ge(g1_copied, 1)
            for t in range(TILES):
                s = 4 * (t % 2)
                if t >= 2:
                    pe.wait_ge(read_a, 2 * (t - 1))
                    pe.wait_ge(read_d, t - 1)
                for bank, col, n in ((0, 0, C), (1, C, 2 * C), (2, 3 * C, 16)):
                    for c in range(KC):
                        pe.matmul(m.ps[:, s + bank, 0:n], m.xnT[:, c, t * P:(t + 1) * P], w[:, c, col:col + n],
                                  start=(c == 0), stop=(c == KC - 1))
                pe.matmul(m.ps[:, s, C:2 * C], g1T[:, t * P:(t + 1) * P], wg2[:], start=True, stop=True).then_inc(product, 1)
            pe.wait_ge(acts, 1)
            n = 0
            for src in (m.base, k_flat):
                if src is k_flat:
                    pe.wait_ge(keyed, 1)
                for c in range(KC):
                    for q in range(4):
                        if n >= 8:
                            pe.wait_ge(copied, n - 7)
                        else:
                            pe.wait_ge(read_a, 2 * TILES)
                            pe.wait_ge(read_d, TILES)
                        for t in range(4):
                            last = pe.transpose(m.ps[:, n % 8, t * P:(t + 1) * P],
                                                src[:, 4 * q + t, c * P:(c + 1) * P], m.ident[:])
                        last.then_inc(turned, 1)
                        n += 1

        @block.scalar
        def _(act):
            act.wait_ge(g1, 1)
            act.copy(g1T[:].rearrange("p (n t) -> p n t", n=4), m.ps[0:16, 0:4, :]).then_inc(g1_copied, 1)
            for t in range(TILES):
                s = 4 * (t % 2)
                act.wait_ge(product, t + 1)
                act.copy(m.base[:, t, :], m.ps[:, s, 0:C]).then_inc(read_a, 1)
                act.copy(m.gain[:, t, :], m.ps[:, s, C:2 * C]).then_inc(read_a, 1)
            act.wait_ge(read_a, 2 * TILES)
            act.activation(m.base[:], m.base[:], ACT.Silu).then_inc(acts, 1)
            act.activation(m.gain[:], m.gain[:], ACT.Sigmoid).then_inc(acts, 1)
            act.wait_ge(read_d, TILES)
            act.activation(k[:, :, :, CH], k[:, :, :, CH], ACT.Sigmoid).then_inc(acts, 1)
            act.wait_ge(norm, TILES + 1)
            act.activation(kn[:], kn[:], ACT.Sqrt).then_inc(root, 1)
            for n in range(16):
                act.wait_ge(turned, n + 1)
                c, q = (n // 4) % 2, n % 4
                dst = (qT if n < 8 else kT)[:, c, q * QB:(q + 1) * QB]
                act.copy(dst, m.ps[:, n % 8, :]).then_inc(copied, 1)

        @block.vector
        def _(dve):
            for t in range(TILES):
                s = 4 * (t % 2)
                dve.wait_ge(product, t + 1)
                dve.tensor_copy(k_flat[:, t, :], m.ps[:, s + 1, 0:C])
                dve.tensor_copy(v[:, t, :], m.ps[:, s + 1, C:2 * C])
                dve.tensor_copy(k[:, t, :, CH], m.ps[:, s + 2, 0:16]).then_inc(read_d, 1)
                dve.wait_ge(read_d, t + 1)
                dve.tensor_tensor(sq[:], k_flat[:, t, :], k_flat[:, t, :], ALU.mult).then_inc(target, 1)
                dve.wait_ge(target, t + 1)
                dve.tensor_reduce(kn[:, t, :], sq[:].rearrange("p (h d) -> p h d", d=CH), AX.X, ALU.add).then_inc(norm, 1)
            dve.wait_ge(norm, TILES)
            dve.tensor_scalar(kn[:], kn[:], 1e-6, None, ALU.add).then_inc(norm, 1)
            dve.wait_ge(root, 1)
            dve.reciprocal(kn[:], kn[:]).then_inc(norm, 1)
            dve.wait_ge(norm, TILES + 2)
            kf = k_flat[:].rearrange("p t (h d) -> p t h d", d=CH)
            bc = kn[:, :, :, None].to_broadcast([P, TILES, 16, CH])
            dve.tensor_tensor(kf, kf, bc, ALU.mult).then_inc(norm, 1)
            dve.wait_ge(norm, TILES + 3)
            dve.tensor_copy(k[:, :, :, 0:CH], kf).then_inc(keyed, 1)
            dve.wait_ge(acts, 3)
            dve.wait_ge(loaded, 80)
            for q in range(4):
                part = v[:, 4 * q:4 * q + 4, :]
                spread = lambda n: lw[:, n:n + 1, :].to_broadcast([P, 4, C])
                dve.tensor_tensor(part, k_flat[:, 4 * q:4 * q + 4, :], part, ALU.subtract).then_inc(read_d, 1)
                dve.wait_ge(read_d, TILES + 2 * q + 1)
                dve.tensor_tensor(part, part, spread(1), ALU.add).then_inc(read_d, 1)
                dve.wait_ge(read_d, TILES + 2 * q + 2)
                dve.tensor_tensor(part, part, spread(0), ALU.mult).then_inc(target, 1)
    ph.close()


def ttt_scan(nc, m, a, tag):
    ph = Phase(nc, tag)
    tb = ph.sb("tb", [P, NCH, NG, CH])
    kc = ph.sb("kc", [P, NCH, NG, CH + 1])
    qh = ph.sb("qh", [P, NCH, NG, CH])
    block_mask = ph.sb("block_mask", [P, P])
    tri = ph.sb("tri", [P, P])
    w2 = ph.sb("w2", [P, 2, CH])
    S = ph.sb("S", [P, NG, 2 * CH])
    qhT = ph.sb("qhT", [P, 2, P])
    kT_bd = ph.sb("kT_bd", [P, 2, NG, P])
    qT_bd = ph.sb("qT_bd", [P, 2, NG, P])
    k_bd = ph.sb("k_bd", [P, 2, NG, P])
    at = ph.sb("at", [P, 2, NG, P])
    s4 = lambda name: ph.sb(name, [P, NG])
    s64 = lambda name: ph.sb(name, [P, NG, CH])
    mu, var, root, rstd, rate, m1, m2 = (s4(x) for x in ("mu", "var", "root", "rstd", "rate", "m1", "m2"))
    cen, sq, hat, gw, pg, hm, vv = (s64(x) for x in ("cen", "sq", "hat", "gw", "pg", "hm", "vv"))
    FILL = 6
    eps = ph.sb("eps", [P, 1])
    u = ph.sb("u", [P, NG, 2 * CH])
    loaded, made = ph.sem("loaded"), ph.sem("made")
    bd_p, k_spread = ph.sem("bd_p"), ph.sem("k_spread")
    kh_ready, at_ready, at_done, qh_ready, qh_copied = (ph.sem("kh_ready"), ph.sem("at_ready"), ph.sem("at_done"),
                                                        ph.sem("qh_ready"), ph.sem("qh_copied"))
    chain, u_ready, ds_ready, s_ready = ph.sem("chain"), ph.sem("u_ready"), ph.sem("ds_ready"), ph.sem("s_ready")
    rooted, eps_set = ph.sem("rooted"), ph.sem("eps_set")
    q_used, back_copied, turned_back = ph.sem("q_used"), ph.sem("back_copied"), ph.sem("turned_back")
    stored = ph.sem("stored")
    qT, kT = m.xnT, m.kT
    LINKS, PER = 15, 8
    FIRST = 2
    bc = lambda x: x[:, :, None].to_broadcast([P, NG, CH])

    with nc.Block() as block:
        @block.sync
        def _(sp):
            n = 0
            for b in range(B):
                for half in range(2):
                    g = 2 * b + half
                    for h in range(HL):
                        rows, hd = slice(h * CH, (h + 1) * CH), half * HL + h
                        tok = slice(b * T, (b + 1) * T)
                        sp.dma_start(tb[rows, :, g, :], a["scr_t"][tok, hd * CH:(hd + 1) * CH]
                                     .rearrange("(n c) e -> c n e", c=CH)).then_inc(loaded, 16)
                        sp.dma_start(kc[rows, :, g, :], a["scr_k"][tok, hd * (CH + 1):(hd + 1) * (CH + 1)]
                                     .rearrange("(n c) e -> c n e", c=CH)).then_inc(loaded, 16)
            sp.dma_start(w2[:], a["ln_w_rows"]).then_inc(loaded, 16)
            sp.wait_ge(back_copied, NCH)
            for b in range(B):
                for half in range(2):
                    for h in range(HL):
                        rows, hd = slice(h * CH, (h + 1) * CH), half * HL + h
                        sp.dma_start(a["scr_q"][b * T:(b + 1) * T, hd * CH:(hd + 1) * CH]
                                     .rearrange("(n c) e -> c n e", c=CH), qh[rows, :, 2 * b + half, :]).then_inc(stored, 16)
            sp.wait_ge(stored, 16 * 32)

        @block.gpsimd
        def _(pool):
            pool.memset(block_mask[:], 1.0).then_inc(made, 1)
            pool.memset(tri[:], 1.0).then_inc(made, 1)
            pool.wait_ge(made, 2)
            bm = block_mask[:].rearrange("p (h c) -> p h c", c=CH)
            pool.affine_select(out=bm, in_=bm, compare_op=ALU.is_ge, fill=0.0, base=0,
                               pattern=[[-CH, HL], [0, CH]], channel_multiplier=1).then_inc(made, 1)
            pool.affine_select(out=tri[:], in_=tri[:], compare_op=ALU.is_ge, fill=0.0, base=0,
                               pattern=[[1, P]], channel_multiplier=-1).then_inc(made, 1)
            pool.wait_ge(made, 4)
            pool.affine_select(out=bm, in_=bm, compare_op=ALU.is_ge, fill=0.0, base=CH - 1,
                               pattern=[[CH, HL], [0, CH]], channel_multiplier=-1).then_inc(made, 1)
            pool.wait_ge(made, 5)

            def spread(i, n):
                wait(pool, q_used, i, PER, n - 1)
                for src, dst in ((kT, kT_bd), (qT, qT_bd)):
                    for b in range(B):
                        cols = src[:, :, ds(i * (PER * CH) + (b * T + n * CH), CH)][:, :, None, :].to_broadcast([P, 2, HL, CH])
                        pool.tensor_tensor(dst[:, n % 2, 2 * b:2 * b + 2, :].rearrange("p g (h c) -> p g h c", c=CH), cols,
                                           block_mask[:].rearrange("p (h c) -> p h c", c=CH)[:, None, :, :]
                                           .to_broadcast([P, 2, HL, CH]), ALU.mult).then_inc(bd_p, 1)

            def spread_k(i, n):
                wait(pool, ds_ready, i, PER, n - 1)
                keys = kc[:, ds(i * PER + n, 1), :, 0:CH].rearrange("p o g d -> p (o g) d")[:, :, None, :]
                pool.tensor_tensor(k_bd[:, n % 2, :, :].rearrange("p g (h d) -> p g h d", d=CH),
                                   keys.to_broadcast([P, NG, HL, CH]),
                                   block_mask[:].rearrange("p (h d) -> p h d", d=CH)[:, None, :, :]
                                   .to_broadcast([P, NG, HL, CH]), ALU.mult).then_inc(k_spread, 1)

            pool.wait_ge(loaded, 16 * 65)
            pipelined(pool, [(0, spread), (0, spread_k)], PER, NCH // PER, lead=6)

        @block.tensor
        def _(pe):
            def early(i, n):
                wait(pe, bd_p, i, 4 * PER, 4 * n + 4)
                wait(pe, at_done, i, PER, n - 1)
                for g in range(NG):
                    last = pe.matmul(m.ps[:, 4 + n % 2, g * P:(g + 1) * P], kT_bd[:, n % 2, g, :],
                                     qT_bd[:, n % 2, g, :], start=True, stop=True)
                last.then_inc(at_ready, 1)

            def state_keys(i, n):
                wait(pe, s_ready, i, PER, n + 1)
                for g in range(NG):
                    last = pe.matmul(m.ps[:, 0, g * CH:(g + 1) * CH], kT_bd[:, n % 2, g, :], S[:, g, 0:CH],
                                     start=True, stop=True)
                last.then_inc(kh_ready, 1)

            def state_queries(i, n):
                wait(pe, qh_copied, i, PER, n - 1)
                for g in range(NG):
                    last = pe.matmul(m.ps[32 * g:32 * g + 32, 2 + n % 2, 0:P], S[:, g, :], qT_bd[:, n % 2, g, :],
                                     start=True, stop=True)
                last.then_inc(q_used, 1)

            def update(i, n):
                wait(pe, k_spread, i, PER, n + 1)
                wait(pe, u_ready, i, PER, n + 1)
                for g in range(NG):
                    last = pe.matmul(m.ps[:, 1, g * CH:(g + 1) * CH], k_bd[:, n % 2, g, :], u[:, g, 0:CH],
                                     start=True, stop=True)
                last.then_inc(ds_ready, 1)

            def within_chunk(i, n):
                wait(pe, at_done, i, PER, n + 1)
                for g in range(NG):
                    last = pe.matmul(m.ps[32 * g:32 * g + 32, 2 + n % 2, 0:P], u[:, g, :], at[:, n % 2, g, :],
                                     start=False, stop=True, skip_group_check=True)
                last.then_inc(qh_ready, 1)

            def turn_back(i, n):
                wait(pe, qh_copied, i, PER, n + 1)
                wait(pe, back_copied, i, PER, n)
                pe.transpose(m.ps[:, 6, 0:P], qhT[:, n % 2, :], m.ident[:]).then_inc(turned_back, 1)

            def fill(i, n):
                keep_warm(pe, m, 7, FILL)

            pipelined(pe, [(2, update), (1, state_keys), (2, within_chunk), (1, state_queries), (1, fill), (0, early),
                           (3, turn_back)], PER, NCH // PER, lead=6)

        @block.scalar
        def _(act):
            def square_root(i, n):
                wait(act, chain, i, PER * LINKS, n * LINKS + 4 + FIRST)
                act.activation(root[:], var[:], ACT.Sqrt, scale=1.0 / CH, bias=eps[:]).then_inc(rooted, 1)

            def copy(i, n):
                wait(act, qh_ready, i, PER, n + 1)
                wait(act, turned_back, i, PER, n - 1)
                act.copy(qhT[:, n % 2, :], m.ps[:, 2 + n % 2, 0:P]).then_inc(qh_copied, 1)

            def copy_back(i, n):
                wait(act, turned_back, i, PER, n + 1)
                act.copy(qh[:, ds(i * PER + n, 1), :, :].rearrange("p o g e -> p (o g) e"),
                         m.ps[:, 6, 0:P].rearrange("p (g e) -> p g e", g=NG)[:, :, 0:CH]).then_inc(back_copied, 1)

            act.wait_ge(eps_set, 1)
            pipelined(act, [(0, square_root), (1, copy), (2, copy_back)], PER, NCH // PER, lead=6)

        @block.vector
        def _(dve):
            dve.memset(eps[:], 1e-6).then_inc(eps_set, 1)
            dve.memset(u[:], 0.0)
            dve.memset(S[:], 0.0).then_inc(s_ready, 1)
            dve.wait_ge(made, 5)
            dve.wait_ge(loaded, 16 * 65)
            dve.tensor_scalar(kc[:, :, :, CH], kc[:, :, :, CH], -2.0, None, ALU.mult).then_inc(chain, 1)
            dve.tensor_tensor(w2[:], w2[:], w2[:], ALU.mult).then_inc(chain, 1)
            dve.wait_ge(chain, 2)

            def done(i, n, k):
                wait(dve, chain, i, PER * LINKS, n * LINKS + k + FIRST)

            def variance(i, n):
                kh = m.ps[:, 0, 0:NG * CH].rearrange("p (g e) -> p g e", e=CH)
                wait(dve, kh_ready, i, PER, n + 1)
                dve.tensor_reduce(mu[:], kh, AX.X, ALU.add).then_inc(chain, 1)
                done(i, n, 1)
                dve.scalar_tensor_tensor(cen[:], bc(mu), -1.0 / CH, kh, ALU.mult, ALU.add).then_inc(chain, 1)
                done(i, n, 2)
                dve.tensor_tensor(sq[:], cen[:], cen[:], ALU.mult).then_inc(chain, 1)
                done(i, n, 3)
                dve.tensor_reduce(var[:], sq[:], AX.X, ALU.add).then_inc(chain, 1)
                done(i, n, 4)

            def gradient(i, n):
                wait(dve, rooted, i, PER, n + 1)
                dve.reciprocal(rstd[:], root[:]).then_inc(chain, 1)
                done(i, n, 5)
                dve.tensor_tensor(hat[:], cen[:], bc(rstd), ALU.mult).then_inc(chain, 1)
                now = kc[:, ds(i * PER + n, 1), :, CH].rearrange("p o g -> p (o g)")
                dve.tensor_tensor(rate[:], rstd[:], now, ALU.mult).then_inc(chain, 1)
                done(i, n, 6)
                dve.tensor_tensor(gw[:].rearrange("p (b h) e -> p b h e", h=2),
                                  hat[:].rearrange("p (b h) e -> p b h e", h=2),
                                  w2[:, None, :, :].to_broadcast([P, B, 2, CH]), ALU.mult).then_inc(chain, 1)
                done(i, n, 8)
                dve.tensor_tensor(gw[:], gw[:], tb[:, ds(i * PER + n, 1), :, :].rearrange("p o g e -> p (o g) e"),
                                  ALU.add).then_inc(chain, 1)
                done(i, n, 9)
                dve.tensor_tensor(pg[:], gw[:], hat[:], ALU.mult).then_inc(chain, 1)
                dve.tensor_reduce(m1[:], gw[:], AX.X, ALU.add).then_inc(chain, 1)
                done(i, n, 10)
                dve.tensor_reduce(m2[:], pg[:], AX.X, ALU.add).then_inc(chain, 1)
                done(i, n, 11)
                dve.scalar_tensor_tensor(vv[:], bc(m1), -1.0 / CH, gw[:], ALU.mult, ALU.add).then_inc(chain, 1)
                done(i, n, 12)
                dve.scalar_tensor_tensor(hm[:], hat[:], -1.0 / CH, bc(m2), ALU.mult, ALU.mult).then_inc(chain, 1)
                done(i, n, 14)
                dve.tensor_tensor(vv[:], vv[:], hm[:], ALU.add).then_inc(chain, 1)
                done(i, n, 15)
                wait(dve, qh_ready, i, PER, n)
                dve.tensor_tensor(u[:, :, 0:CH], vv[:], bc(rate), ALU.mult).then_inc(u_ready, 1)

            def mask(i, n):
                wait(dve, at_ready, i, PER, n + 1)
                wait(dve, qh_ready, i, PER, n - 1)
                dve.tensor_tensor(at[:, n % 2, :, :], m.ps[:, 4 + n % 2, :].rearrange("p (g c) -> p g c", c=P),
                                  tri[:, None, :].to_broadcast([P, NG, P]), ALU.mult).then_inc(at_done, 1)

            def advance(i, n):
                wait(dve, ds_ready, i, PER, n + 1)
                dve.tensor_tensor(S[:, :, 0:CH], S[:, :, 0:CH], m.ps[:, 1, 0:NG * CH].rearrange("p (g e) -> p g e", e=CH),
                                  ALU.add).then_inc(s_ready, 1)

            pipelined(dve, [(0, variance), (0, gradient), (0, mask), (0, advance)], PER, NCH // PER, lead=6)
    ph.close()


def store_x(nc, m, out_d):
    ph = Phase(nc, "store")
    stored = ph.sem("stored")
    with nc.Block() as block:
        @block.sync
        def _(sp):
            sp.dma_start(out_d.rearrange("b (t p) c -> p (b t) c", p=P), m.x[:]).then_inc(stored, 16)
            sp.wait_ge(stored, 16)
    ph.close()


class Memory:
    pass


def build_program(nc, a, out_d, limit=99):
    m = Memory()
    m.weights, m.w = ExitStack(), None
    with ExitStack() as ctx:
        def sb(name, shape, dt=F32):
            return ctx.enter_context(nc.sbuf_tensor(name, shape, dt))

        m.x = sb("x", [P, TILES, C])
        m.xnT = sb("xnT", [P, KC, TOK])
        m.ident = sb("ident", [P, P])
        m.ident_b = sb("ident_b", [P, P], BF16)
        m.later_k = sb("later_k", [P, P], BF16)
        m.keep = sb("keep", [P, P])
        m.warm = sb("warm", [P, QB], BF16)
        m.later_q = sb("later_q", [P, P], BF16)
        m.ps = ctx.enter_context(nc.psum_tensor("ps", [P, 8, 512], F32))

        load_and_constants(nc, m, a["x"])
        stages = STAGES(nc, m, a)
        for n, s in enumerate(stages[:limit]):
            s()
        m.weights.close()
        store_x(nc, m, out_d)


def STAGES(nc, m, a):
    def attn_softcap():
        with nc.sbuf_tensor("v_a", [P, TILES, 8, 32], F32) as v_sb:
            project_rope(nc, m, "pa", a["wqk_a"], 6, a["wv_a"], 8, 32, 32, a["cos_a"], a["sin_a"], a["scr_a"], v_sb)
            attention(nc, m, "aa", a["scr_a"], v_sb, a["wo_a"], 32, 2, 512, 256.0 ** -0.5, 50.0)

    def ffn(tag):
        relu_ffn(nc, m, tag, a["w1"], a["b1"], a["w2"], a["b2"], a["w3"], a["b3"])

    def attn_plain():
        with nc.sbuf_tensor("v_b", [P, TILES, 4, 32], F32) as v_sb:
            project_rope(nc, m, "pb", a["wqk_b"], 3, a["wv_b"], 4, 16, 32, a["cos_b"], a["sin_b"], a["scr_b"], v_sb)
            attention(nc, m, "ab", a["scr_b"], v_sb, a["wo_b"], 16, 1, 256, 0.25, None)

    def gated(tag, unpack):
        if m.w is None:
            m.w = m.weights.enter_context(nc.sbuf_tensor("w_gated", [P, 3, 2, MLP], F32))
        gated_ffn(nc, m, a, tag, unpack)

    def attn_diff():
        with nc.sbuf_tensor("y_tok", [P, TILES, C], F32) as m.y_tok:
            with nc.sbuf_tensor("v_d", [P, TILES, 4, 32], F32) as v_sb:
                project_rope(nc, m, "pd", a["wqk_d"], 5, a["wv_d"], 4, 16, 32, a["cos_d"], a["sin_d"], a["scr_d"], v_sb)
                diff_attention(nc, m, a, "ad", a["scr_d"], v_sb)
            norm_project(nc, m, "od", a["wo_d"], a["rms_d"], 1e-8, 1.0 - (0.8 - 0.6 * float(np.exp(-0.3 * 0))))

    def attn_ttt():
        with ExitStack() as st:
            sb = lambda name, shape: st.enter_context(nc.sbuf_tensor(name, shape, F32))
            m.base, m.gain = sb("base", [P, TILES, C]), sb("gain", [P, TILES, C])
            with nc.sbuf_tensor("kT_t", [P, KC, TOK], F32) as m.kT:
                ttt_project(nc, m, a, "pt")
                ttt_scan(nc, m, a, "st")
            m.y_tok = sb("y_tok2", [P, TILES, C])
            norm_project(nc, m, "ow", a["wo_t"], a["norm_w"], 1e-6, 1.0, ttt=a["scr_q"])

    return [attn_softcap, lambda: ffn("f2"), attn_plain, lambda: ffn("f4"),
            attn_diff, lambda: gated("g6", True), attn_ttt, lambda: gated("g8", False)]


def rope_tables(hd, interleaved, factor=1.0):
    inv = (1.0 / np.float32(10000.0) ** (np.arange(0, hd, 2, dtype=np.float32) / np.float32(hd))).astype(np.float32)
    ang = np.arange(T, dtype=np.float32)[:, None] * inv[None, :]
    cos, sin = np.cos(ang).T, np.sin(ang).T
    if interleaved:
        cos, sin = np.repeat(cos, 2, 0), np.stack([-sin, sin], 1).reshape(hd, T)
    else:
        cos, sin = np.concatenate([cos, cos]), np.concatenate([-sin, sin])
    cos, sin = cos * np.float32(factor), sin * np.float32(factor)
    return (np.ascontiguousarray(np.tile(cos, (P // hd, 1)), np.float32),
            np.ascontiguousarray(np.tile(sin, (P // hd, 1)), np.float32))


def swap_halves(w, hd):
    n = w.shape[1]
    return w.reshape(-1, n // hd, 2, hd // 2)[:, :, ::-1].reshape(-1, n)


def lay_out(i):
    f = {k: np.asarray(v) for k, v in i.items()}
    cat = lambda *p: np.ascontiguousarray(np.concatenate(p, 1))
    d = {"x": f["L0_attn_a_X"]}
    q, k = f["L0_attn_a_Wq"], f["L0_attn_a_Wk"]
    d["wqk_a"] = cat(q, k, swap_halves(q, 32), swap_halves(k, 32))
    d["wv_a"], d["wo_a"] = f["L0_attn_a_Wv"], f["L0_attn_a_Wo"]
    d["cos_a"], d["sin_a"] = rope_tables(32, False)
    q, k = f["L0_attn_b_Wq"], f["L0_attn_b_Wk"]
    ks = swap_halves(k, 16)
    d["wqk_b"] = cat(q, k, k, swap_halves(q, 16), ks, ks)
    d["wv_b"] = f["L0_attn_b_Wv"]
    wo = np.zeros((16, 32, C), np.float32)
    wo[:, :16] = f["L0_attn_b_Wproj"].reshape(16, 16, C)
    d["wo_b"] = wo.reshape(512, C)
    d["cos_b"], d["sin_b"] = rope_tables(16, False)
    d["w1"], d["w2"], d["w3"] = (np.ascontiguousarray(f[f"L0_ffn_W{n}"].T) for n in (1, 2, 3))
    d["b1"], d["b2"] = (np.ascontiguousarray(f[f"L0_ffn_b{n}"].reshape(4, P).T) for n in (1, 2))
    d["b3"] = f["L0_ffn_b3"]
    q, k = f["L1_attn_a_Wq"], f["L1_attn_a_Wk"]
    d["wqk_d"] = cat(q, k, swap_halves(q, 2), swap_halves(k, 2))
    d["wv_d"], d["wo_d"] = f["L1_attn_a_Wv"], f["L1_attn_a_Wo"]
    d["cos_d"], d["sin_d"] = rope_tables(32, True, 0.5)
    d["lq1"], d["lk1"], d["lq2"], d["lk2"] = (f[f"L1_attn_a_{n}"].reshape(-1) for n in ("lq1", "lk1", "lq2", "lk2"))
    d["rms_d"] = np.tile(f["L1_attn_a_rms_w"], 16)

    w = [f[f"L1_attn_b_W{n}"] for n in ("q", "k", "v", "beta")]
    d["w_t"], d["wg1"], d["wg2"], d["wo_t"] = cat(*w), f["L1_attn_b_Wg1"], f["L1_attn_b_Wg2"], f["L1_attn_b_Wo"]
    ln_w = f["L1_attn_b_ln_w"]
    d["ln_w"], d["ln_b"], d["norm_w"] = ln_w.reshape(-1), f["L1_attn_b_ln_b"].reshape(-1), f["L1_attn_b_norm_w"]
    d["ln_w_rows"] = np.ascontiguousarray(np.repeat(ln_w.reshape(2, 8, 1, 16), 16, 2).reshape(2, P, 16).transpose(1, 0, 2))

    def hidden(p):
        return np.ascontiguousarray(p.T.reshape(-1, MLP // 256, P, 2).transpose(0, 1, 3, 2).reshape(-1, MLP))
    d["gate_p"], d["up_p"] = hidden(f["L1_ffn_gate_W_packed"]), hidden(f["L1_ffn_up_W_packed"])
    d["gate_s"], d["up_s"] = hidden(f["L1_ffn_gate_scales"]), hidden(f["L1_ffn_up_scales"])
    d["down_p"] = np.ascontiguousarray(f["L1_ffn_down_W_packed"].T)
    d["down_s"] = np.ascontiguousarray(f["L1_ffn_down_scales"].T.reshape(8, 8, C).transpose(1, 0, 2).reshape(8, MLP))
    return d


SCRATCH = {"scr_a": (3, 768, TOK), "scr_b": (3, 384, TOK), "scr_d": (3, 640, TOK)}
SCRATCH_F32 = {"scr_k": (TOK, 16 * 17), "scr_t": (TOK, C), "scr_q": (TOK, C)}


def kernel(**inputs):
    import concourse.bacc as bacc
    from concourse.bass_utils import run_bass_kernel_spmd

    nc = bacc.Bacc("TRN2", target_bir_lowering=False, num_devices=1)
    arrays = {f"in_{k}": v for k, v in lay_out(inputs).items()}
    a = {k[3:]: nc.dram_tensor(k, v.shape, mybir.dt.from_np(v.dtype), kind="ExternalInput").ap()
         for k, v in arrays.items()}
    for k, shape in SCRATCH.items():
        a[k] = nc.dram_tensor(k, shape, BF16, kind="Internal").ap()
    for k, shape in SCRATCH_F32.items():
        a[k] = nc.dram_tensor(k, shape, F32, kind="Internal").ap()
    out = nc.dram_tensor("out", (B, T, C), F32, kind="ExternalOutput").ap()
    build_program(nc, a, out)
    return run_bass_kernel_spmd(nc, [arrays], core_ids=[0]).results[0]["out"]
```
